# Optimizing a Trainium2 kernel written in Bass

```python
import numpy as np
import jax
import jax.numpy as jnp

def _softmax(x, axis=-1):
    return jax.nn.softmax(x, axis=axis)

def _gelu(x):
    return jax.nn.gelu(x, approximate=True)

def _silu(x):
    return jax.nn.silu(x)

def _sigmoid(x):
    return jax.nn.sigmoid(x)

def _layernorm(x, axis=-1, eps=1e-05):
    m = jnp.mean(x, axis=axis, keepdims=True)
    v = jnp.var(x, axis=axis, keepdims=True)
    return (x - m) / jnp.sqrt(v + eps)

def _scatter_add(tgt, idx, src, axis=0):
    return tgt.at[idx].add(src)

def _segment_sum(src, seg, n):
    return jax.ops.segment_sum(src, seg, n)
kernel_name = 'mk_decoder_preln_d1_seqx_r4_38d478'

def setup_inputs(seed: int=0):
    np.random.seed(seed)
    _w = jnp.asarray

    def _rec_inputs():
        import jax
        import jax.numpy as jnp
        _rk = jax.random.key(seed)
        x = 7.22e-05 + 1 * jax.random.normal(jax.random.fold_in(_rk, 1), (4, 512, 512), jnp.float32)
        _lenS = 512 - jax.random.randint(jax.random.fold_in(_rk, 7), (4,), 0, max(1, 512 // 4) + 1, jnp.int32)
        _lenS2 = 512 - jax.random.randint(jax.random.fold_in(_rk, 8), (4,), 0, max(1, 512 // 4) + 1, jnp.int32)
        _ctx_1024P = jax.random.normal(jax.random.fold_in(_rk, 11), (4, 16, 256), jnp.float32)
        _ctx_1024c = jax.random.dirichlet(jax.random.fold_in(_rk, 511), 0.3 * jnp.ones((16,), jnp.float32), (4, 512))
        _ctx_1024t = jnp.einsum('bsk,bkd->bsd', _ctx_1024c, _ctx_1024P)
        _ctx_1024t = _ctx_1024t * jax.lax.rsqrt(jnp.mean(jnp.square(_ctx_1024t)) + 1e-12) * 0.953939
        ctx_1024 = 2.81802e-05 + 1.00001 * (_ctx_1024t + 0.3 * jax.random.normal(jax.random.fold_in(_rk, 611), (4, 512, 256), jnp.float32))
        return (x, ctx_1024)
    x, ctx_1024 = _rec_inputs()

    def _L0_attn_setup():
        import math
        import jax, jax.numpy as jnp
        import numpy as np
        B, S, HID = (2, 256, 512)
        H, D, R = (16, 128, 64)
        KVC, QC = (128, 384)
        MAX_POS = 1024

        def _lin(x, w, b):
            return x @ w.T + b

        def _rotate_half(x):
            x1, x2 = (x[..., :x.shape[-1] // 2], x[..., x.shape[-1] // 2:])
            return jnp.concatenate([-x2, x1], axis=-1)

        def _rope_tables(dim, end, theta=10000.0):
            freqs = 1.0 / theta ** (jnp.arange(0, dim, 2)[:dim // 2].astype(jnp.float32) / dim)
            f = jnp.outer(jnp.arange(end, dtype=jnp.float32), freqs)
            cos, sin = (jnp.cos(f), jnp.sin(f))
            return (jnp.concatenate([cos, cos], -1), jnp.concatenate([sin, sin], -1))

        def _reference_tuple_inner(hidden_states, W_DKV_w, W_DKV_b, W_UK_w, W_UK_b, W_UV_w, W_UV_b, W_KR_w, W_KR_b, W_DQ_w, W_DQ_b, W_UQ_w, W_UQ_b, W_QR_w, W_QR_b, W_O_w, W_O_b):
            b, s = hidden_states.shape[:2]
            c_kv = _lin(hidden_states, W_DKV_w, W_DKV_b)
            k = _lin(c_kv, W_UK_w, W_UK_b).reshape(b, s, H, D)
            v = _lin(c_kv, W_UV_w, W_UV_b).reshape(b, s, H, D)
            c_q = _lin(hidden_states, W_DQ_w, W_DQ_b)
            q = _lin(c_q, W_UQ_w, W_UQ_b).reshape(b, s, H, D)
            k_r = _lin(k, W_KR_w, W_KR_b)
            q_r = _lin(q, W_QR_w, W_QR_b)
            cos, sin = _rope_tables(R, MAX_POS)
            cos_p = cos[:s][:, None, :]
            sin_p = sin[:s][:, None, :]
            q_r = q_r * cos_p + _rotate_half(q_r) * sin_p
            k_r = k_r * cos_p + _rotate_half(k_r) * sin_p
            scale = 1.0 / math.sqrt(D)
            scores = jnp.einsum('bqhd,bkhd->bhqk', q, k) * scale
            probs = jax.nn.softmax(scores, axis=-1)
            attn = jnp.einsum('bhqk,bkhd->bqhd', probs, v).reshape(b, s, H * D)
            output = _lin(attn, W_O_w, W_O_b)
            return (output, c_kv, k_r)
        key = jax.random.key(seed)
        ks = jax.random.split(key, 17)
        w = lambda k, shape: jax.random.normal(k, shape, jnp.float32) * 0.02
        return {'hidden_states': jax.random.normal(ks[0], (B, S, HID), jnp.float32), 'W_DKV_w': w(ks[1], (KVC, HID)), 'W_DKV_b': w(ks[2], (KVC,)), 'W_UK_w': w(ks[3], (H * D, KVC)), 'W_UK_b': w(ks[4], (H * D,)), 'W_UV_w': w(ks[5], (H * D, KVC)), 'W_UV_b': w(ks[6], (H * D,)), 'W_KR_w': w(ks[7], (R, D)), 'W_KR_b': w(ks[8], (R,)), 'W_DQ_w': w(ks[9], (QC, HID)), 'W_DQ_b': w(ks[10], (QC,)), 'W_UQ_w': w(ks[11], (H * D, QC)), 'W_UQ_b': w(ks[12], (H * D,)), 'W_QR_w': w(ks[13], (R, D)), 'W_QR_b': w(ks[14], (R,)), 'W_O_w': w(ks[15], (HID, H * D)), 'W_O_b': w(ks[16], (HID,))}
    _L0_attn_all = _L0_attn_setup()
    _L0_attn_in = {k: v for k, v in _L0_attn_all.items() if k in ('W_DKV_w', 'W_DKV_b', 'W_UK_w', 'W_UK_b', 'W_UV_w', 'W_UV_b', 'W_KR_w', 'W_KR_b', 'W_DQ_w', 'W_DQ_b', 'W_UQ_w', 'W_UQ_b', 'W_QR_w', 'W_QR_b', 'W_O_w', 'W_O_b')}
    del _L0_attn_all

    def _L0_xattn_setup():
        import jax, jax.numpy as jnp
        import numpy as np
        key = jax.random.key(seed)
        ks = jax.random.split(key, 6)
        B, L, N, C, D = (8, 128, 512, 256, 128)
        return {'teacher_logits': jax.random.normal(ks[0], (B, L, N), dtype=jnp.float32), 'teacher_features': jax.random.normal(ks[1], (B, N, C), dtype=jnp.float32), 'Wq': jax.random.normal(ks[2], (D, C), dtype=jnp.float32) * (1.0 / np.sqrt(C)), 'bq': jnp.zeros((D,), dtype=jnp.float32), 'Wk': jax.random.normal(ks[3], (D, C), dtype=jnp.float32) * (1.0 / np.sqrt(C)), 'bk': jnp.zeros((D,), dtype=jnp.float32)}
    _L0_xattn_all = _L0_xattn_setup()
    _L0_xattn_in = {k: v for k, v in _L0_xattn_all.items() if k in ('Wq', 'bq', 'Wk', 'bk')}
    del _L0_xattn_all

    def _L0_ffn_setup():
        import jax, jax.numpy as jnp
        import numpy as np
        from jax import lax
        E = 8
        K = 2
        D = 512
        H = 352
        NS = 2
        B, T = (2, 512)
        EPS = 1e-20
        HS = H * NS

        def _silu(v):
            return v * jax.nn.sigmoid(v)
        key = jax.random.key(seed)
        ks = jax.random.split(key, 8)
        s = 0.02
        return {'x': jax.random.normal(ks[0], (B, T, D), jnp.float32), 'router_w': jax.random.normal(ks[1], (E, D), jnp.float32) * 0.006, 'wg': jax.random.normal(ks[2], (E, D, H), jnp.float32) * s, 'wu': jax.random.normal(ks[3], (E, D, H), jnp.float32) * s, 'wd': jax.random.normal(ks[4], (E, H, D), jnp.float32) * s, 'sg': jax.random.normal(ks[5], (D, HS), jnp.float32) * s, 'su': jax.random.normal(ks[6], (D, HS), jnp.float32) * s, 'sd': jax.random.normal(ks[7], (HS, D), jnp.float32) * s}
    _L0_ffn_all = _L0_ffn_setup()
    _L0_ffn_in = {k: v for k, v in _L0_ffn_all.items() if k in ('router_w', 'wg', 'wu', 'wd', 'sg', 'su', 'sd')}
    del _L0_ffn_all
    return {'x': x, 'ctx_1024': ctx_1024, 'L0_attn_W_DKV_w': _L0_attn_in['W_DKV_w'], 'L0_attn_W_DKV_b': _L0_attn_in['W_DKV_b'], 'L0_attn_W_UK_w': _L0_attn_in['W_UK_w'], 'L0_attn_W_UK_b': _L0_attn_in['W_UK_b'], 'L0_attn_W_UV_w': _L0_attn_in['W_UV_w'], 'L0_attn_W_UV_b': _L0_attn_in['W_UV_b'], 'L0_attn_W_KR_w': _L0_attn_in['W_KR_w'], 'L0_attn_W_KR_b': _L0_attn_in['W_KR_b'], 'L0_attn_W_DQ_w': _L0_attn_in['W_DQ_w'], 'L0_attn_W_DQ_b': _L0_attn_in['W_DQ_b'], 'L0_attn_W_UQ_w': _L0_attn_in['W_UQ_w'], 'L0_attn_W_UQ_b': _L0_attn_in['W_UQ_b'], 'L0_attn_W_QR_w': _L0_attn_in['W_QR_w'], 'L0_attn_W_QR_b': _L0_attn_in['W_QR_b'], 'L0_attn_W_O_w': _L0_attn_in['W_O_w'], 'L0_attn_W_O_b': _L0_attn_in['W_O_b'], 'L0_xattn_Wq': _L0_xattn_in['Wq'], 'L0_xattn_bq': _L0_xattn_in['bq'], 'L0_xattn_Wk': _L0_xattn_in['Wk'], 'L0_xattn_bk': _L0_xattn_in['bk'], 'L0_ffn_router_w': _L0_ffn_in['router_w'], 'L0_ffn_wg': _L0_ffn_in['wg'], 'L0_ffn_wu': _L0_ffn_in['wu'], 'L0_ffn_wd': _L0_ffn_in['wd'], 'L0_ffn_sg': _L0_ffn_in['sg'], 'L0_ffn_su': _L0_ffn_in['su'], 'L0_ffn_sd': _L0_ffn_in['sd']}

def reference(x, ctx_1024, L0_attn_W_DKV_w, L0_attn_W_DKV_b, L0_attn_W_UK_w, L0_attn_W_UK_b, L0_attn_W_UV_w, L0_attn_W_UV_b, L0_attn_W_KR_w, L0_attn_W_KR_b, L0_attn_W_DQ_w, L0_attn_W_DQ_b, L0_attn_W_UQ_w, L0_attn_W_UQ_b, L0_attn_W_QR_w, L0_attn_W_QR_b, L0_attn_W_O_w, L0_attn_W_O_b, L0_xattn_Wq, L0_xattn_bq, L0_xattn_Wk, L0_xattn_bk, L0_ffn_router_w, L0_ffn_wg, L0_ffn_wu, L0_ffn_wd, L0_ffn_sg, L0_ffn_su, L0_ffn_sd):
    import jax
    import jax.numpy as jnp

    def _L0_attn_ref(hidden_states, W_DKV_w, W_DKV_b, W_UK_w, W_UK_b, W_UV_w, W_UV_b, W_KR_w, W_KR_b, W_DQ_w, W_DQ_b, W_UQ_w, W_UQ_b, W_QR_w, W_QR_b, W_O_w, W_O_b):
        import math
        import jax, jax.numpy as jnp
        import numpy as np
        B, S, HID = (2, 256, 512)
        H, D, R = (16, 128, 64)
        KVC, QC = (128, 384)
        MAX_POS = 1024

        def _lin(x, w, b):
            return x @ w.T + b

        def _rotate_half(x):
            x1, x2 = (x[..., :x.shape[-1] // 2], x[..., x.shape[-1] // 2:])
            return jnp.concatenate([-x2, x1], axis=-1)

        def _rope_tables(dim, end, theta=10000.0):
            freqs = 1.0 / theta ** (jnp.arange(0, dim, 2)[:dim // 2].astype(jnp.float32) / dim)
            f = jnp.outer(jnp.arange(end, dtype=jnp.float32), freqs)
            cos, sin = (jnp.cos(f), jnp.sin(f))
            return (jnp.concatenate([cos, cos], -1), jnp.concatenate([sin, sin], -1))

        def _reference_tuple_inner(hidden_states, W_DKV_w, W_DKV_b, W_UK_w, W_UK_b, W_UV_w, W_UV_b, W_KR_w, W_KR_b, W_DQ_w, W_DQ_b, W_UQ_w, W_UQ_b, W_QR_w, W_QR_b, W_O_w, W_O_b):
            b, s = hidden_states.shape[:2]
            c_kv = _lin(hidden_states, W_DKV_w, W_DKV_b)
            k = _lin(c_kv, W_UK_w, W_UK_b).reshape(b, s, H, D)
            v = _lin(c_kv, W_UV_w, W_UV_b).reshape(b, s, H, D)
            c_q = _lin(hidden_states, W_DQ_w, W_DQ_b)
            q = _lin(c_q, W_UQ_w, W_UQ_b).reshape(b, s, H, D)
            k_r = _lin(k, W_KR_w, W_KR_b)
            q_r = _lin(q, W_QR_w, W_QR_b)
            cos, sin = _rope_tables(R, MAX_POS)
            cos_p = cos[:s][:, None, :]
            sin_p = sin[:s][:, None, :]
            q_r = q_r * cos_p + _rotate_half(q_r) * sin_p
            k_r = k_r * cos_p + _rotate_half(k_r) * sin_p
            scale = 1.0 / math.sqrt(D)
            scores = jnp.einsum('bqhd,bkhd->bhqk', q, k) * scale
            probs = jax.nn.softmax(scores, axis=-1)
            attn = jnp.einsum('bhqk,bkhd->bqhd', probs, v).reshape(b, s, H * D)
            output = _lin(attn, W_O_w, W_O_b)
            return (output, c_kv, k_r)
        return _reference_tuple_inner(hidden_states, W_DKV_w, W_DKV_b, W_UK_w, W_UK_b, W_UV_w, W_UV_b, W_KR_w, W_KR_b, W_DQ_w, W_DQ_b, W_UQ_w, W_UQ_b, W_QR_w, W_QR_b, W_O_w, W_O_b)[0]

    def _L0_xattn_ref(teacher_logits, teacher_features, Wq, bq, Wk, bk):
        import jax, jax.numpy as jnp
        import numpy as np
        query = jnp.einsum('bnc,dc->bnd', teacher_features, Wq) + bq
        key = jnp.einsum('bnc,dc->bnd', teacher_features, Wk) + bk
        energy = jnp.einsum('bnd,bmd->bnm', query, key)
        attention = jax.nn.softmax(energy, axis=-1)
        x_m = jnp.einsum('bln,bmn->blm', teacher_logits, attention)
        return x_m

    def _L0_ffn_ref(x, router_w, wg, wu, wd, sg, su, sd):
        import jax, jax.numpy as jnp
        import numpy as np
        from jax import lax
        E = 8
        K = 2
        D = 512
        H = 352
        NS = 2
        B, T = (2, 512)
        EPS = 1e-20
        HS = H * NS

        def _silu(v):
            return v * jax.nn.sigmoid(v)
        b, t, d = x.shape
        xf = x.reshape(b * t, d)
        n = xf.shape[0]
        gates = jax.nn.softmax(xf @ router_w.T, axis=-1)
        topv, topi = lax.top_k(gates, K)
        masked = jnp.zeros_like(gates).at[jnp.arange(n)[:, None], topi].set(topv)
        masked = masked / (masked.sum(axis=-1, keepdims=True) + EPS)

        def step(acc, p):
            wg_e, wu_e, wd_e, g_e = p
            y = _silu(xf @ wg_e) * (xf @ wu_e) @ wd_e
            return (acc + y * g_e[:, None], None)
        routed, _ = lax.scan(step, jnp.zeros_like(xf), (wg, wu, wd, masked.T))
        shared = _silu(xf @ sg) * (xf @ su) @ sd
        return (routed + shared).reshape(b, t, d)
    x = x + _L0_attn_ref(_layernorm(x, axis=-1), L0_attn_W_DKV_w, L0_attn_W_DKV_b, L0_attn_W_UK_w, L0_attn_W_UK_b, L0_attn_W_UV_w, L0_attn_W_UV_b, L0_attn_W_KR_w, L0_attn_W_KR_b, L0_attn_W_DQ_w, L0_attn_W_DQ_b, L0_attn_W_UQ_w, L0_attn_W_UQ_b, L0_attn_W_QR_w, L0_attn_W_QR_b, L0_attn_W_O_w, L0_attn_W_O_b)
    x = x + _L0_xattn_ref(_layernorm(x, axis=-1), ctx_1024, L0_xattn_Wq, L0_xattn_bq, L0_xattn_Wk, L0_xattn_bk)
    x = x + _L0_ffn_ref(_layernorm(x, axis=-1), L0_ffn_router_w, L0_ffn_wg, L0_ffn_wu, L0_ffn_wd, L0_ffn_sg, L0_ffn_su, L0_ffn_sd)
    return x

_drawn_inputs = setup_inputs


def setup_inputs(seed=0):
    import zlib

    import numpy as np

    out = dict(_drawn_inputs(seed))
    spreads = {'L0_xattn_bq': (0.0, 0.706), 'L0_xattn_bk': (0.0, 2.0)}
    factors = {'L0_attn_W_DKV_w': 8.0,
     'L0_attn_W_DKV_b': 8.0,
     'L0_attn_W_UK_w': 8.0,
     'L0_attn_W_UK_b': 64.0,
     'L0_attn_W_UV_w': 8.0,
     'L0_attn_W_UV_b': 23.896,
     'L0_attn_W_DQ_w': 8.0,
     'L0_attn_W_DQ_b': 8.0,
     'L0_attn_W_UQ_w': 8.0,
     'L0_attn_W_UQ_b': 8.0,
     'L0_attn_W_O_w': 2.902,
     'L0_attn_W_O_b': 22.952,
     'L0_ffn_router_w': 23.352,
     'L0_ffn_wg': 8.0,
     'L0_ffn_wu': 8.0,
     'L0_ffn_wd': 8.0,
     'L0_ffn_sg': 8.0,
     'L0_ffn_su': 8.0,
     'L0_ffn_sd': 8.0}
    for name, (base, spread) in spreads.items():
        noise = np.random.default_rng([zlib.crc32(name.encode()), seed]).standard_normal(out[name].shape)
        drawn = base * np.exp(spread * noise) if base else spread * noise
        out[name] = jnp.asarray(drawn.astype(out[name].dtype))
    for name, factor in factors.items():
        out[name] = (out[name] * factor).astype(out[name].dtype)
    return out
```

```python
from contextlib import ExitStack

import concourse.bass as bass
from concourse import mybir
from concourse.alu_op_type import AluOpType as ALU

ACT = mybir.ActivationFunctionType
AX = mybir.AxisListType
F32 = mybir.dt.float32
F32R = mybir.dt.float32r
U32 = mybir.dt.uint32

P = 128
B, S, D = 4, 512, 512
QT = S // P
TT = B * QT
KD = D // P
H, DH = 16, 128
KVC, QC = 128, 384
KQ = QC // P
C = 256
KC = C // P
E, EH, NSH = 8, 352, 2
NE = E + NSH
KH = 3
HW = [128, 128, EH - 256]
LN_EPS = 1e-5
GATE_EPS = 1e-20
SCALE = float(DH) ** -0.5

PACK = QC + KVC + KVC + D
O_UQ, O_UK, O_UV, O_WO = 0, QC, QC + KVC, QC + 2 * KVC
MN = QC + D

UNITS = H * B
LAP = 2 * B


def decoder_kernel(nc, x, proj_w, proj_b, heads_w, uq_b, uv_b, o_b, ctx_t, qk_w, qk_b,
                   router_w, gate_up_w, down_w, out):
    xv = x.rearrange("(t p) d -> p t d", p=P)
    ov = out.rearrange("(t p) d -> p t d", p=P)
    mn_dram = nc.dram_tensor("mn_scratch", [H, P, 2, MN], F32, kind="Internal").ap()

    with ExitStack() as life:
        def sb(name, shape, dt=F32, stack=life):
            return stack.enter_context(nc.sbuf_tensor(name, shape, dt))

        def sem(name):
            return life.enter_context(nc.semaphore(name))

        resid = sb("resid", [P, TT, D])
        ident = sb("ident", [P, P])
        stats = sb("stats", [P, QT, 6])
        moments = sb("moments", [P, QT, 2])
        rstd = sb("rstd", [P, QT])
        vareps = sb("vareps", [P, QT])
        neg_half = sb("neg_half", [P, QT])
        negmax = sb("negmax", [P, 8])
        rowsum = sb("rowsum", [P, 8])
        rowinv = sb("rowinv", [P, 8])

        latents = ExitStack()
        ckvT = sb("ckvT", [P, 2, B * S], F32R, latents)
        ckv = sb("ckv", [P, B, 2, QT, KVC], F32R, latents)
        cqT = sb("cqT", [P, 2, KQ, B * S], F32R, latents)
        qbias = sb("qbias", [P, H], F32, latents)
        obias = sb("obias", [P, D], F32, latents)

        early = ExitStack()
        pack_raw = sb("pack_raw", [P, 2, PACK], F32, early)
        pack = sb("pack", [P, 2, 2, PACK], F32R, early)
        uvb_wide = sb("uvb_wide", [P, 2, P], F32, early)
        mn = sb("mn", [P, 2, 2, MN], F32R, early)
        uqb = sb("uqb", [P, H], F32, early)
        uvb = sb("uvb", [P, H], F32, early)
        ones = sb("ones", [P, P], F32, early)
        projw_raw = sb("projw_raw", [P, KD, D], F32, early)
        projw = sb("projw", [P, 2, KD, D], F32R, early)
        projb = sb("projb", [P, 1 + KQ], F32, early)
        xnT1 = sb("xnT1", [P, 2, KD, S], F32R, early)
        xn1 = sb("xn1", [P, QT, D], F32, early)
        early.close()

        mid = ExitStack()
        m_sb = sb("m_sb", [P, 2, 2, QC], F32R, mid)
        n_sb = sb("n_sb", [P, 2, 2, 2, D], F32R, mid)
        qT = sb("qT", [P, 2, 2, S], F32R, mid)
        probs = sb("probs", [P, QT, S], F32, mid)
        pT = sb("pT", [P, 2, 2, QT, S], F32R, mid)
        mixT = sb("mixT", [P, 2, 2, 2, S], F32R, mid)
        qb_now = sb("qb_now", [P, 2], F32, mid)
        mid.close()
        latents.close()

        late = ExitStack()
        ctx_raw = sb("ctx_raw", [P, 2, KC, S], F32, late)
        ctxT = sb("ctxT", [P, 2, KC, S], F32R, late)
        qkw_raw = sb("qkw_raw", [P, KC, 2 * P], F32, late)
        qkw = sb("qkw", [P, 2, KC, 2 * P], F32R, late)
        qkb = sb("qkb", [P, 2], F32, late)
        qk3 = sb("qk3", [P, 2, 2, S], F32R, late)
        probs3 = sb("probs3", [P, QT, S], F32, late)
        pT3 = sb("pT3", [P, 2, 2, QT, S], F32R, late)
        xnT3 = sb("xnT3", [P, 2, 2, KD, S], F32R, late)
        xn3 = sb("xn3", [P, QT, D], F32, late)
        late.close()

        last = ExitStack()
        xnT4 = sb("xnT4", [P, 2, KD, B * S], F32R, last)
        ew_raw = sb("ew_raw", [P, KD * 2 * EH + KH * D], F32, last)
        ew = sb("ew", [P, 2, 2, KD * 2 * EH + KH * D], F32R, last)
        routw_raw = sb("routw_raw", [P, KD, E], F32, last)
        routw = sb("routw", [P, 2, KD, E], F32R, last)
        silu_g = sb("silu_g", [P, 2, EH], F32, last)
        hid = sb("hid", [P, 2, EH], F32, last)
        hidT = sb("hidT", [P, 2, 2, KH, P], F32R, last)
        logit = sb("logit", [P, TT, E], F32, last)
        gate = sb("gate", [P, TT, E], F32, last)
        top = sb("top", [P, TT, 8], F32, last)
        topi = sb("topi", [P, TT, 8], U32, last)
        topf = sb("topf", [P, TT, 8], F32, last)
        pick = sb("pick", [P, TT, E], F32, last)
        pick1 = sb("pick1", [P, TT, E], F32, last)
        iota8 = sb("iota8", [P, E], F32, last)
        col16 = sb("col16", [P, TT], F32, last)
        col16b = sb("col16b", [P, TT], F32, last)
        gates = sb("gates", [P, NE, TT], F32, last)
        xn4 = sb("xn4", [P, QT, D], F32, last)
        last.close()

        bank = [life.enter_context(nc.psum_tensor(f"bank{i}", [P, D], F32)) for i in range(8)]

        def trio(stage):
            return sem(f"{stage}_product"), sem(f"{stage}_high"), sem(f"{stage}_split")

        const_loaded = sem("const_loaded")
        x_loaded = sem("x_loaded")
        ident_zero = sem("ident_zero")
        ident_ready = sem("ident_ready")
        var_ready = sem("var_ready")
        rstd_ready = sem("rstd_ready")
        vec_step = sem("vec_step")

        pack_loaded = [sem("pack_loaded0"), sem("pack_loaded1")]
        pack_high = sem("pack_high")
        pack_split = sem("pack_split")
        head_bias = sem("head_bias")
        head_bias_taken = sem("head_bias_taken")
        fold_product, fold_high, fold_split = trio("fold")
        mn_stored = [sem("mn_stored0"), sem("mn_stored1")]

        projw_high = sem("projw_high")
        projw_split = sem("projw_split")
        norm1_ready = sem("norm1_ready")
        proj_product, proj_high, proj_split = trio("proj")
        obias_added = sem("obias_added")
        turned = sem("turned")
        turned_high = sem("turned_high")
        turned_low = sem("turned_low")

        m_loaded = sem("m_loaded")
        n_loaded = sem("n_loaded")
        att_product, att_high, att_split = trio("att")
        qb_ready = sem("qb_ready")
        scores_ready = sem("scores_ready")
        negmax_ready = sem("negmax_ready")
        exp_done = sem("exp_done")
        rowinv_ready = sem("rowinv_ready")
        probs_begun = sem("probs_begun")
        probs_ready = sem("probs_ready")
        out_ready = sem("out_ready")
        out_added = sem("out_added")

        mixw_loaded = sem("mixw_loaded")
        ctx_loaded = [sem("ctx_loaded0"), sem("ctx_loaded1")]
        mixw_high = sem("mixw_high")
        ctx_high = sem("ctx_high")
        ctx_split = sem("ctx_split")
        norm3_ready = sem("norm3_ready")
        mix_product, mix_high, mix_split = trio("mix")
        scores3_ready = sem("scores3_ready")
        negmax3_ready = sem("negmax3_ready")
        exp3_done = sem("exp3_done")
        rowinv3_ready = sem("rowinv3_ready")
        probs3_ready = sem("probs3_ready")
        mixed_ready = sem("mixed_ready")
        mixed_added = sem("mixed_added")

        rout_loaded = sem("rout_loaded")
        rout_high = sem("rout_high")
        rout_split = sem("rout_split")
        norm4_ready = sem("norm4_ready")
        ln4_product, ln4_high, ln4_split = trio("ln4")
        logits_ready = sem("logits_ready")
        gate_shift = sem("gate_shift")
        gate_exp = sem("gate_exp")
        iota_ready = sem("iota_ready")
        ew_loaded = sem("ew_loaded")
        ew_high = sem("ew_high")
        ew_split = sem("ew_split")
        gu_ready = sem("gu_ready")
        silu_done = sem("silu_done")
        hid_ready = sem("hid_ready")
        hidT_product, hidT_high, hidT_split = trio("hidT")
        y_ready = sem("y_ready")
        y_added = sem("y_added")
        stored = sem("stored")

        def mm3(pe, acc, lhs, rhs, first, final):
            pe.matmul(acc, lhs[1], rhs[0], start=first, stop=False)
            pe.matmul(acc, lhs[0], rhs[1], start=False, stop=False)
            return pe.matmul(acc, lhs[0], rhs[0], start=False, stop=final)

        def both(t, *index):
            return t[(slice(None), 0) + index], t[(slice(None), 1) + index]

        def f32(ap):
            return ap.bitcast(F32)

        ALL = slice(None)

        splits, count = {}, 0
        for u in range(-2, UNITS + 3):
            for s in range(QT):
                for kind, unit, here in (("T", u, True), ("Q", u + 2, s == 2), ("V", u - 1, s == 3)):
                    if here and 0 <= unit < UNITS:
                        count += 1
                        splits[kind, unit, s if kind == "T" else 0] = count
        PER_LAP = LAP * (QT + 2)
        assert splits["T", 2 * LAP, 0] - splits["T", LAP, 0] == PER_LAP

        def split_no(kind, unit, s, lap):
            return splits[kind, unit, s] + PER_LAP * lap

        def has(unit):
            return 0 <= unit < UNITS

        def outs_of(u, s):
            if s % 2 == 0 or u < 3:
                return None
            bb, i = ((u - 3) // 2, s // 2) if u % 2 else ((u - 4) // 2, 2 + s // 2)
            return (bb, i) if 0 <= bb < UNITS // 2 else None

        def laps(eng, iteration):
            for u in range(-2, LAP):
                iteration(u, 0)
            with eng.Fori(0, UNITS // LAP - 2) as lap:
                for u in range(LAP, 2 * LAP):
                    iteration(u, lap)
            for u in range(UNITS - LAP, UNITS + 3):
                iteration(u, 0)

        def hold(eng, s, value):
            if not isinstance(value, int) or value > 0:
                eng.wait_ge(s, value)

        block = life.enter_context(nc.Block())

        @block.sync
        def _(sp):
            def load_head(h, j):
                hold(sp, fold_product, 2 * h - 2)
                sp.dma_start(pack_raw[:, j, :], heads_w[h]).then_inc(pack_loaded[j], 16)

            def store_fold(h, j):
                sp.wait_ge(fold_split, 2 * h + 2)
                sp.dma_start(mn_dram[h], f32(mn[:, j, :, :])).then_inc(mn_stored[j], 16)

            for dst, src in ((uqb, uq_b), (uvb, uv_b), (projb, proj_b)):
                sp.dma_start(dst[:], src).then_inc(const_loaded, 16)
            sp.dma_start(obias[:], o_b.partition_broadcast(P)).then_inc(const_loaded, 16)
            load_head(0, 0)
            load_head(1, 1)
            sp.dma_start(projw_raw[:], proj_w).then_inc(const_loaded, 16)
            for b in range(B):
                sp.dma_start(resid[:, QT * b:QT * (b + 1), :], xv[:, QT * b:QT * (b + 1), :]).then_inc(x_loaded, 16)
            with sp.Fori(0, H // 2 - 1) as i:
                for j in range(2):
                    store_fold(2 * i + j, j)
                    load_head(2 * i + j + 2, j)
            for j in range(2):
                store_fold(H - 2 + j, j)

            def load_m(pair):
                for j in range(2):
                    sp.dma_start(f32(m_sb[:, :, j, :]), mn_dram[2 * pair + j][:, :, 0:QC]).then_inc(m_loaded, 16)

            def load_n(pair, slot):
                for j in range(2):
                    sp.dma_start(f32(n_sb[:, slot, :, j, :]), mn_dram[2 * pair + j][:, :, QC:MN]).then_inc(n_loaded, 16)

            for j in range(2):
                sp.wait_ge(mn_stored[j], 16 * (H // 2))
            sp.wait_ge(proj_split, B * (QT + 1 + KQ))
            load_m(0)
            load_n(0, 0)
            sp.wait_ge(att_product, splits["Q", LAP - 1, 0])
            load_m(1)
            load_n(1, 1)
            with sp.Fori(2, UNITS // LAP) as pair:
                sp.wait_ge(att_product, splits["Q", LAP - 1, 0] + PER_LAP * (pair - 1))
                load_m(pair)
                sp.wait_ge(out_ready, QT * B * (pair - 1))
                load_n(pair, pair % 2)

            sp.wait_ge(out_ready, QT * UNITS // 2)
            sp.wait_ge(out_added, QT * UNITS // 2)
            sp.dma_start(qkw_raw[:], qk_w).then_inc(mixw_loaded, 16)
            sp.dma_start(qkb[:], qk_b).then_inc(mixw_loaded, 16)
            for b in range(B):
                if b >= 2:
                    sp.wait_ge(ctx_split, b - 1)
                sp.dma_start(ctx_raw[:, b % 2, :, :], ctx_t[:, :, b * S:(b + 1) * S]).then_inc(ctx_loaded[b % 2], 16)

            sp.wait_ge(mixed_added, TT)
            sp.dma_start(routw_raw[:], router_w).then_inc(rout_loaded, 16)

            def load_expert(e):
                hold(sp, ew_split, e)
                sp.dma_start(ew_raw[:, 0:KD * 2 * EH], gate_up_w[e]).then_inc(ew_loaded, 16)
                for k in range(KH):
                    o = KD * 2 * EH + k * D
                    sp.dma_start(ew_raw[0:HW[k], o:o + D], down_w[e, k * P:k * P + HW[k], :]).then_inc(ew_loaded, 16)

            load_expert(0)
            with sp.Fori(1, NE) as e:
                load_expert(e)
            for t in range(TT):
                sp.wait_ge(y_added, TT * (NE - 1) + t + 1)
                sp.dma_start(ov[:, t, :], resid[:, t, :]).then_inc(stored, 16)
            sp.wait_ge(stored, 16 * TT)

        @block.gpsimd
        def _(pool):
            norms = [0]

            def inverse_std():
                norms[0] += 1
                pool.wait_ge(var_ready, norms[0])
                pool.tensor_tensor(rstd[:], vareps[:], neg_half[:], ALU.pow).then_inc(rstd_ready, 1)

            pool.memset(neg_half[:], -0.5)
            pool.memset(ident[:], 0.0).then_inc(ident_zero, 1)
            pool.memset(ones[:], 1.0).then_inc(ident_ready, 1)
            pool.wait_ge(ident_zero, 1)
            pool.affine_select(out=ident[:], in_=ident[:], compare_op=ALU.not_equal, fill=1.0, base=0,
                               pattern=[[-1, P]], channel_multiplier=1).then_inc(ident_ready, 1)
            for t in range(TT):
                if t % QT == 0:
                    inverse_std()
                pool.wait_ge(norm1_ready, t + 1)
                pool.wait_ge(head_bias_taken, H)
                pool.tensor_tensor(resid[:, t, :], resid[:, t, :], obias[:], ALU.add).then_inc(obias_added, 1)

            def iteration(u, lap):
                for s in range(QT):
                    if has(u + 1):
                        n = QT * (u + 1) + s
                        pool.wait_ge(rowinv_ready, n + 1 + lap * (QT * LAP))
                        pool.sem_inc(probs_begun, 1)
                        pool.tensor_scalar(probs[:, s, :], probs[:, s, :], rowinv[:, n % 8:n % 8 + 1], None,
                                           ALU.mult).then_inc(probs_ready, 1)
            laps(pool, iteration)

            def ctx_low(b):
                pool.wait_ge(ctx_high, b + 1)
                pool.tensor_tensor(ctxT[:, 1, :, :], ctx_raw[:, b % 2, :, :], f32(ctxT[:, 0, :, :]),
                                   ALU.subtract).then_inc(ctx_split, 1)

            def probs_tile(n):
                pool.wait_ge(rowinv3_ready, n + 1)
                pool.tensor_scalar(probs3[:, n % QT, :], probs3[:, n % QT, :], rowinv[:, n % 8:n % 8 + 1], None,
                                   ALU.mult).then_inc(probs3_ready, 1)

            ctx_low(0)
            for b in range(B):
                inverse_std()
                for s in range(QT):
                    probs_tile(QT * b + s)
                if b + 1 < B:
                    ctx_low(b + 1)

            pool.wait_ge(mixed_added, TT)
            pool.iota(topi[:, 0, :], pattern=[[1, E]], base=0, channel_multiplier=0).then_inc(iota_ready, 1)

            for b in range(B):
                inverse_std()

            def expert_low(e):
                pool.wait_ge(ew_high, 2 * e + 2)
                for r, c0, c1 in ((P, 0, KD * 2 * EH + 2 * D), (HW[2], KD * 2 * EH + 2 * D, KD * 2 * EH + 3 * D)):
                    op = pool.tensor_tensor(ew[0:r, e % 2, 1, c0:c1], ew_raw[0:r, c0:c1], f32(ew[0:r, e % 2, 0, c0:c1]),
                                            ALU.subtract)
                op.then_inc(ew_split, 1)

            with pool.Fori(0, NE) as e:
                expert_low(e)

        @block.scalar
        def _(act):
            def copy(dst, src, scale=1.0):
                return act.activation(dst, src, ACT.Copy, scale=scale)

            def head_weights(i, h, j):
                act.wait_ge(pack_loaded[j], 16 * i + 16)
                hold(act, fold_product, 2 * h - 2)
                copy(pack[:, j, 0, :], pack_raw[:, j, :]).then_inc(pack_high, 1)

            def head_fold(i, h, j):
                hold(act, mn_stored[j], 16 * i)
                act.wait_ge(fold_product, 2 * h + 1)
                copy(mn[:, j, 0, 0:QC], bank[2 * j][:, 0:QC], SCALE).then_inc(fold_high, 1)
                act.wait_ge(fold_product, 2 * h + 2)
                copy(mn[:, j, 0, QC:MN], bank[2 * j + 1][:]).then_inc(fold_high, 1)

            head_weights(0, 0, 0)
            head_weights(0, 1, 1)
            head_fold(0, 0, 0)
            head_weights(1, 2, 0)
            head_fold(0, 1, 1)
            with act.Fori(1, H // 2 - 1) as i:
                head_weights(i, 2 * i + 1, 1)
                head_fold(i, 2 * i, 0)
                head_weights(i + 1, 2 * i + 2, 0)
                head_fold(i, 2 * i + 1, 1)
            head_weights(H // 2 - 1, H - 1, 1)
            head_fold(H // 2 - 1, H - 2, 0)
            head_fold(H // 2 - 1, H - 1, 1)

            act.wait_ge(const_loaded, 16 * 5)
            copy(projw[:, 0, :, :], projw_raw[:]).then_inc(projw_high, 1)
            n = 0
            for b in range(B):
                cols = slice(b * S, (b + 1) * S)
                for t in range(QT):
                    n += 1
                    act.wait_ge(proj_product, n)
                    copy(xnT1[:, 0, :, t * P:(t + 1) * P], bank[t % 2][:].rearrange("p (k c) -> p k c", k=KD)).then_inc(proj_high, 1)
                for m in range(1 + KQ):
                    n += 1
                    act.wait_ge(proj_product, n)
                    dst = ckvT[:, 0, cols] if m == 0 else cqT[:, 0, m - 1, cols]
                    act.activation(dst, bank[2 + m][:], ACT.Identity, bias=projb[:, m:m + 1]).then_inc(proj_high, 1)
                act.wait_ge(turned, 2 * b + 1)
                copy(ckv[:, b, 0, :, :], bank[6][:].rearrange("p (k c) -> p k c", k=QT)).then_inc(turned_high, 1)

            def iteration(u, lap):
                tiles = lap * (QT * LAP)
                for s in range(QT):
                    if has(u):
                        act.wait_ge(att_product, split_no("T", u, s, lap))
                        copy(pT[:, u % 2, 0, :, s * P:(s + 1) * P],
                             bank[2 + s % 2][:].rearrange("p (k c) -> p k c", k=QT)).then_inc(att_high, 1)
                    if has(u + 1):
                        n = QT * (u + 1) + s
                        act.wait_ge(negmax_ready, n + 1 + tiles)
                        act.activation(probs[:, s, :], bank[s % 2][:], ACT.Exp, bias=negmax[:, n % 8:n % 8 + 1],
                                       accum_out=rowsum[:, n % 8:n % 8 + 1]).then_inc(exp_done, 1)
                    if s == 2 and has(u + 2):
                        q = u + 2
                        act.wait_ge(qb_ready, q // LAP + 1 + lap)
                        act.wait_ge(att_product, split_no("Q", q, 0, lap))
                        act.activation(qT[:, q % 2, 0, :], bank[4][:], ACT.Identity,
                                       bias=qb_now[:, q % 2:q % 2 + 1]).then_inc(att_high, 1)
                    if s == 3 and has(u - 1):
                        v = u - 1
                        act.wait_ge(att_product, split_no("V", v, 0, lap))
                        copy(mixT[:, v // 2 % 2, v % 2, 0, :], bank[5][:]).then_inc(att_high, 1)
            act.wait_ge(proj_split, B * (QT + 1 + KQ))
            for j in range(2):
                act.wait_ge(mn_stored[j], 16 * (H // 2))
            laps(act, iteration)

            act.wait_ge(out_added, QT * UNITS // 2)
            act.wait_ge(mixw_loaded, 32)
            copy(qkw[:, 0, :, :], qkw_raw[:]).then_inc(mixw_high, 1)
            prod = [0]

            def high(dst, src, bias=None):
                prod[0] += 1
                act.wait_ge(mix_product, prod[0])
                if bias is None:
                    copy(dst, src).then_inc(mix_high, 1)
                else:
                    act.activation(dst, src, ACT.Identity, bias=bias).then_inc(mix_high, 1)

            def ctx_part(b):
                act.wait_ge(ctx_loaded[b % 2], 16 * (b // 2 + 1))
                copy(ctxT[:, 0, :, :], ctx_raw[:, b % 2, :, :]).then_inc(ctx_high, 1)
                for i in range(2):
                    high(qk3[:, i, 0, :], bank[4 + i][:], qkb[:, i:i + 1])

            def exp_tile(b, s):
                n = QT * b + s
                act.wait_ge(negmax3_ready, n + 1)
                act.activation(probs3[:, s, :], bank[s % 2][:], ACT.Exp, bias=negmax[:, n % 8:n % 8 + 1],
                               accum_out=rowsum[:, n % 8:n % 8 + 1]).then_inc(exp3_done, 1)

            def norm_part(b, s):
                high(xnT3[:, b % 2, 0, :, s * P:(s + 1) * P], bank[4 + s % 2][:].rearrange("p (k c) -> p k c", k=KD))

            def turn_part(b, s):
                high(pT3[:, b % 2, 0, :, s * P:(s + 1) * P], bank[2 + s % 2][:].rearrange("p (k c) -> p k c", k=QT))

            for b in range(B):
                ctx_part(b)
                for s in range(QT):
                    exp_tile(b, s)
                    norm_part(b, s)
                for s in range(QT):
                    turn_part(b, s)

            act.wait_ge(rout_loaded, 16)
            copy(routw[:, 0, :, :], routw_raw[:]).then_inc(rout_high, 1)
            for t in range(TT):
                act.wait_ge(ln4_product, t + 1)
                copy(xnT4[:, 0, :, t * P:(t + 1) * P], bank[t % 2][:].rearrange("p (k c) -> p k c", k=KD)).then_inc(ln4_high, 1)
            act.wait_ge(gate_shift, 1)
            act.activation(gate[:], gate[:], ACT.Exp).then_inc(gate_exp, 1)

            def expert_high(e):
                act.wait_ge(ew_loaded, 64 * e + 64)
                c = KD * 2 * EH + 2 * D
                copy(ew[:, e % 2, 0, 0:c], ew_raw[:, 0:c]).then_inc(ew_high, 1)
                copy(ew[0:HW[2], e % 2, 0, c:c + D], ew_raw[0:HW[2], c:c + D]).then_inc(ew_high, 1)

            expert_high(0)

            def expert(e, more):
                for t in range(TT):
                    act.wait_ge(gu_ready, TT * e + t + 1)
                    act.activation(silu_g[:, t % 2, :], bank[0][:, 0:EH], ACT.Silu).then_inc(silu_done, 1)
                    act.wait_ge(hidT_product, TT * e + t + 1)
                    for k, r in ((slice(0, 2), P), (slice(2, 3), HW[2])):
                        copy(hidT[0:r, t % 2, 0, k, :],
                             bank[2][0:r, k.start * P:k.stop * P].rearrange("p (k c) -> p k c", c=P)).then_inc(hidT_high, 1)
                    if t == 2 and more:
                        expert_high(e + 1)

            with act.Fori(0, NE - 1) as e:
                expert(e, True)
            expert(NE - 1, False)

        @block.vector
        def _(dve):
            step, norms = [0], [0]

            def own(op):
                step[0] += 1
                op.then_inc(vec_step, 1)
                return step[0]

            def normalize(xn, b, ready, tiles_free, tiles_free_value):
                for t in range(QT):
                    n = own(dve.bn_stats(stats[:, t, :], resid[:, QT * b + t, :]))
                dve.wait_ge(vec_step, n)
                for t in range(QT):
                    n = own(dve.bn_aggr(moments[:, t, :], stats[:, t, :]))
                dve.wait_ge(vec_step, n)
                dve.tensor_scalar(vareps[:], moments[:, :, 1], LN_EPS, None, ALU.add).then_inc(var_ready, 1)
                norms[0] += 1
                dve.wait_ge(rstd_ready, norms[0])
                hold(dve, tiles_free, tiles_free_value)
                for t in range(QT):
                    dve.tensor_scalar(xn[:, t, :], resid[:, QT * b + t, :], moments[:, t, 0:1], rstd[:, t:t + 1],
                                      ALU.subtract, ALU.mult).then_inc(ready, 1)

            def low(dst, src, hi, scale=1.0):
                return dve.scalar_tensor_tensor(dst, src, scale, f32(hi), ALU.mult, ALU.subtract)

            def low_bias(dst, src, bias, hi):
                return dve.scalar_tensor_tensor(dst, src, bias, f32(hi), ALU.add, ALU.subtract)

            def head_weights(h, j):
                dve.wait_ge(ident_ready, 2)
                dve.wait_ge(pack_high, h + 1)
                low(pack[:, j, 1, :], pack_raw[:, j, :], pack[:, j, 0, :]).then_inc(pack_split, 1)
                dve.tensor_scalar(uvb_wide[:, j, :], ones[:], uvb[:, bass.ds(h, 1)], None, ALU.mult).then_inc(pack_split, 1)

            def head_fold(h, j):
                dve.wait_ge(head_bias, h + 1)
                hold(dve, head_bias_taken, h)
                dve.tensor_scalar(qbias[:, bass.ds(h, 1)], bank[4 + 3 * j][:, 0:1], SCALE, None, ALU.mult)
                dve.tensor_tensor(obias[:], obias[:], bank[5 + j][:], ALU.add).then_inc(head_bias_taken, 1)
                dve.wait_ge(fold_high, 2 * h + 1)
                low(mn[:, j, 1, 0:QC], bank[2 * j][:, 0:QC], mn[:, j, 0, 0:QC], SCALE).then_inc(fold_split, 1)
                dve.wait_ge(fold_high, 2 * h + 2)
                low(mn[:, j, 1, QC:MN], bank[2 * j + 1][:], mn[:, j, 0, QC:MN]).then_inc(fold_split, 1)

            dve.wait_ge(const_loaded, 16 * 5)
            head_weights(0, 0)
            head_weights(1, 1)
            head_fold(0, 0)
            head_weights(2, 0)
            head_fold(1, 1)
            with dve.Fori(1, H // 2 - 1) as i:
                head_weights(2 * i + 1, 1)
                head_fold(2 * i, 0)
                head_weights(2 * i + 2, 0)
                head_fold(2 * i + 1, 1)
            head_weights(H - 1, 1)
            head_fold(H - 2, 0)
            head_fold(H - 1, 1)

            dve.wait_ge(projw_high, 1)
            low(projw[:, 1, :, :], projw_raw[:], projw[:, 0, :, :]).then_inc(projw_split, 1)
            n = 0
            per = QT + 1 + KQ
            for b in range(B):
                cols = slice(b * S, (b + 1) * S)
                dve.wait_ge(x_loaded, 16 * B)
                normalize(xn1, b, norm1_ready, proj_product, per * (b - 1) + QT)
                for t in range(QT):
                    n += 1
                    dve.wait_ge(proj_high, n)
                    low(xnT1[:, 1, :, t * P:(t + 1) * P], bank[t % 2][:].rearrange("p (k c) -> p k c", k=KD),
                        xnT1[:, 0, :, t * P:(t + 1) * P]).then_inc(proj_split, 1)
                for m in range(1 + KQ):
                    n += 1
                    dve.wait_ge(proj_high, n)
                    part = (ckvT[:, i, cols] if m == 0 else cqT[:, i, m - 1, cols] for i in range(2))
                    hi, lo = part
                    low_bias(lo, bank[2 + m][:], projb[:, m:m + 1], hi).then_inc(proj_split, 1)
                dve.wait_ge(turned, 2 * b + 2)
                dve.tensor_copy(ckv[:, b, 1, :, :], bank[7][:].rearrange("p (k c) -> p k c", k=QT)).then_inc(turned_low, 1)

            def invert(n, lap):
                dve.wait_ge(exp_done, n + 1 + lap * (QT * LAP))
                dve.reciprocal(rowinv[:, n % 8:n % 8 + 1], rowsum[:, n % 8:n % 8 + 1]).then_inc(rowinv_ready, 1)

            def iteration(u, lap):
                tiles = lap * (QT * LAP)
                q, v = u + 2, u - 1
                if has(q) and q % LAP == 0:
                    dve.tensor_copy(qb_now[:], qbias[:, bass.ds((q // LAP + lap) * 2, 2)]).then_inc(qb_ready, 1)
                for s in range(QT):
                    n = QT * (u + 1) + s
                    if has((n - 1) // QT):
                        invert(n - 1, lap)
                    if has(u + 1):
                        dve.wait_ge(scores_ready, n + 1 + tiles)
                        dve.tensor_reduce(negmax[:, n % 8:n % 8 + 1], bank[s % 2][:], AX.X, ALU.max,
                                          negate=True).then_inc(negmax_ready, 1)
                    if has(u):
                        dve.wait_ge(att_high, split_no("T", u, s, lap))
                        low(pT[:, u % 2, 1, :, s * P:(s + 1) * P], bank[2 + s % 2][:].rearrange("p (k c) -> p k c", k=QT),
                            pT[:, u % 2, 0, :, s * P:(s + 1) * P]).then_inc(att_split, 1)
                    if s == 2 and has(q):
                        dve.wait_ge(att_high, split_no("Q", q, 0, lap))
                        low_bias(qT[:, q % 2, 1, :], bank[4][:], qb_now[:, q % 2:q % 2 + 1], qT[:, q % 2, 0, :]).then_inc(att_split, 1)
                    if outs_of(u, s):
                        bb, i = outs_of(u, s)
                        m = QT * bb + i
                        t = QT * (bb % B) + i
                        dve.wait_ge(out_ready, m + 1 + lap * (QT * LAP // 2))
                        dve.tensor_tensor(resid[:, t, :], resid[:, t, :], bank[6 + m % 2][:], ALU.add).then_inc(out_added, 1)
                    if s == 3 and has(v):
                        dve.wait_ge(att_high, split_no("V", v, 0, lap))
                        low(mixT[:, v // 2 % 2, v % 2, 1, :], bank[5][:], mixT[:, v // 2 % 2, v % 2, 0, :]).then_inc(att_split, 1)
            dve.wait_ge(obias_added, TT)
            dve.wait_ge(head_bias_taken, H)
            for j in range(2):
                dve.wait_ge(mn_stored[j], 16 * (H // 2))
            laps(dve, iteration)

            dve.wait_ge(out_added, QT * UNITS // 2)
            dve.wait_ge(mixw_high, 1)
            low(qkw[:, 1, :, :], qkw_raw[:], qkw[:, 0, :, :]).then_inc(mixw_high, 1)
            prod = [0]

            def split(dst, src, hi, bias=None):
                prod[0] += 1
                dve.wait_ge(mix_high, prod[0])
                (low(dst, src, hi) if bias is None else low_bias(dst, src, bias, hi)).then_inc(mix_split, 1)

            def invert3(n):
                dve.wait_ge(exp3_done, n + 1)
                dve.reciprocal(rowinv[:, n % 8:n % 8 + 1], rowsum[:, n % 8:n % 8 + 1]).then_inc(rowinv3_ready, 1)

            for b in range(B + 1):
                if b < B:
                    for i in range(2):
                        split(qk3[:, i, 1, :], bank[4 + i][:], qk3[:, i, 0, :], qkb[:, i:i + 1])
                    normalize(xn3, b, norm3_ready, mix_product, (2 + QT + QT) * (b - 1) + 2 + QT)
                for s in range(QT):
                    n = QT * b + s
                    if b < B:
                        dve.wait_ge(scores3_ready, n + 1)
                        dve.tensor_reduce(negmax[:, n % 8:n % 8 + 1], bank[s % 2][:], AX.X, ALU.max,
                                          negate=True).then_inc(negmax3_ready, 1)
                        part = (slice(None), slice(s * P, (s + 1) * P))
                        split(xnT3[(ALL, b % 2, 1) + part], bank[4 + s % 2][:].rearrange("p (k c) -> p k c", k=KD),
                              xnT3[(ALL, b % 2, 0) + part])
                        invert3(n)
                    if b:
                        t = QT * (b - 1) + s
                        dve.wait_ge(mixed_ready, t + 1)
                        dve.tensor_tensor(resid[:, t, :], resid[:, t, :], bank[6 + t % 2][:], ALU.add).then_inc(mixed_added, 1)
                if b < B:
                    for s in range(QT):
                        part = (slice(None), slice(s * P, (s + 1) * P))
                        split(pT3[(ALL, b % 2, 1) + part], bank[2 + s % 2][:].rearrange("p (k c) -> p k c", k=QT),
                              pT3[(ALL, b % 2, 0) + part])

            dve.wait_ge(mixed_added, TT)
            for b in range(B):
                normalize(xn4, b, norm4_ready, ln4_product, QT * b)
                if b == 0:
                    dve.wait_ge(rout_high, 1)
                    low(routw[:, 1, :, :], routw_raw[:], routw[:, 0, :, :]).then_inc(rout_split, 1)
                for t in range(QT * b, QT * (b + 1)):
                    dve.wait_ge(ln4_high, t + 1)
                    low(xnT4[:, 1, :, t * P:(t + 1) * P], bank[t % 2][:].rearrange("p (k c) -> p k c", k=KD),
                        xnT4[:, 0, :, t * P:(t + 1) * P]).then_inc(ln4_split, 1)

            def wide(col):
                return col.rearrange("p (t o) -> p t o", o=1).to_broadcast([P, TT, E])

            def then(op):
                dve.wait_ge(vec_step, own(op))

            dve.wait_ge(iota_ready, 1)
            then(dve.tensor_copy(iota8[:], topi[:, 0, :]))
            then(dve.memset(gates[:], 1.0))
            dve.wait_ge(logits_ready, TT)
            then(dve.tensor_copy(logit[:], bank[2][:, 0:TT * E].rearrange("p (t e) -> p t e", e=E)))
            then(dve.tensor_reduce(col16[:], logit[:], AX.X, ALU.max))
            dve.tensor_tensor(gate[:], logit[:], wide(col16[:]), ALU.subtract).then_inc(gate_shift, 1)
            dve.wait_ge(gate_exp, 1)
            then(dve.tensor_reduce(col16[:], gate[:], AX.X, ALU.add))
            then(dve.reciprocal(col16b[:], col16[:]))
            then(dve.tensor_tensor(gate[:], gate[:], wide(col16b[:]), ALU.mult))
            for t in range(TT):
                n = own(dve.max(top[:, t, :], gate[:, t, :]))
            dve.wait_ge(vec_step, n)
            for t in range(TT):
                n = own(dve.max_index(topi[:, t, :], top[:, t, :], gate[:, t, :]))
            dve.wait_ge(vec_step, n)
            then(dve.tensor_copy(topf[:], topi[:]))
            for t in range(TT):
                n = own(dve.tensor_scalar(pick1[:, t, :], iota8[:], topf[:, t, 0:1], None, ALU.is_equal))
            dve.wait_ge(vec_step, n)
            for t in range(TT):
                n = own(dve.scalar_tensor_tensor(pick[:, t, :], iota8[:], topf[:, t, 1:2], pick1[:, t, :],
                                                 ALU.is_equal, ALU.add))
            dve.wait_ge(vec_step, n)
            then(dve.tensor_tensor(gate[:], gate[:], pick[:], ALU.mult))
            then(dve.tensor_reduce(col16[:], gate[:], AX.X, ALU.add))
            then(dve.tensor_scalar(col16[:], col16[:], GATE_EPS, None, ALU.add))
            then(dve.reciprocal(col16b[:], col16[:]))
            then(dve.tensor_tensor(gates[:, 0:E, :].rearrange("p e t -> p t e"), gate[:], wide(col16b[:]), ALU.mult))

            def expert(e):
                def take(t):
                    dve.wait_ge(y_ready, TT * e + t + 1)
                    dve.tensor_tensor(resid[:, t, :], resid[:, t, :], bank[3 + t % 2][:], ALU.add).then_inc(y_added, 1)
                for t in range(TT):
                    dve.wait_ge(silu_done, TT * e + t + 1)
                    dve.scalar_tensor_tensor(hid[:, t % 2, :], silu_g[:, t % 2, :], gates[:, bass.ds(e, 1), t], bank[1][:, 0:EH],
                                             ALU.mult, ALU.mult).then_inc(hid_ready, 1)
                    dve.wait_ge(hidT_high, (TT * e + t) * 2 + 2)
                    for k, r in ((slice(0, 2), P), (slice(2, 3), HW[2])):
                        low(hidT[0:r, t % 2, 1, k, :], bank[2][0:r, k.start * P:k.stop * P].rearrange("p (k c) -> p k c", c=P),
                            hidT[0:r, t % 2, 0, k, :]).then_inc(hidT_split, 1)
                    take(t)

            with dve.Fori(0, NE) as e:
                expert(e)

        @block.tensor
        def _(pe):
            def head(h, j):
                pe.wait_ge(pack_split, 2 * h + 2)
                hold(pe, head_bias_taken, h - 1)
                raw, parts = pack_raw[:, j, :], pack[:, j]
                pe.matmul(bank[4 + 3 * j][:, 0:1], raw[:, O_UK:O_UK + KVC], uqb[:, bass.ds(h, 1)], start=True, stop=True)
                pe.matmul(bank[5 + j][:], uvb_wide[:, j, :], raw[:, O_WO:O_WO + D], start=True, stop=True).then_inc(head_bias, 1)
                hold(pe, fold_split, 2 * h - 2)
                for r in range(KQ):
                    op = mm3(pe, bank[2 * j][:, r * P:(r + 1) * P],
                             (parts[:, 0, r * P:(r + 1) * P], parts[:, 1, r * P:(r + 1) * P]),
                             (parts[:, 0, O_UK:O_UK + KVC], parts[:, 1, O_UK:O_UK + KVC]), True, True)
                op.then_inc(fold_product, 1)
                mm3(pe, bank[2 * j + 1][:], (parts[:, 0, O_UV:O_UV + KVC], parts[:, 1, O_UV:O_UV + KVC]),
                    (parts[:, 0, O_WO:O_WO + D], parts[:, 1, O_WO:O_WO + D]), True, True).then_inc(fold_product, 1)

            pe.wait_ge(ident_ready, 2)
            pe.wait_ge(const_loaded, 16 * 5)
            head(0, 0)
            head(1, 1)
            with pe.Fori(1, H // 2) as i:
                for j in range(2):
                    head(2 * i + j, j)

            pe.wait_ge(projw_split, 1)
            pe.wait_ge(fold_split, 2 * H)
            pe.wait_ge(head_bias_taken, H)
            n = 0
            for b in range(B):
                for t in range(QT):
                    n += 1
                    pe.wait_ge(norm1_ready, QT * b + t + 1)
                    if t >= 2:
                        pe.wait_ge(proj_split, n - 2)
                    for k in range(KD):
                        op = pe.transpose(bank[t % 2][:, k * P:(k + 1) * P], xn1[:, t, k * P:(k + 1) * P], ident[:])
                    op.then_inc(proj_product, 1)
                pe.wait_ge(proj_split, n)
                for m in range(1 + KQ):
                    n += 1
                    for k in range(KD):
                        op = mm3(pe, bank[2 + m][:], both(projw, k, slice(m * P, (m + 1) * P)), both(xnT1, k, ALL),
                                 k == 0, k == KD - 1)
                    op.then_inc(proj_product, 1)
                pe.wait_ge(proj_split, n - KQ)
                hold(pe, turned_high, b)
                hold(pe, turned_low, b)
                for part in range(2):
                    for t in range(QT):
                        c = b * S + t * P
                        op = pe.transpose(bank[6 + part][:, t * P:(t + 1) * P], f32(ckvT[:, part, c:c + P]), ident[:])
                    op.then_inc(turned, 1)

            pe.wait_ge(turned_high, B)
            pe.wait_ge(turned_low, B)

            def iteration(u, lap):
                tiles = lap * (QT * LAP)
                q, v = u + 2, u - 1
                b_s, b_v, b_q = (u + 1) // 2 % B, v // 2 % B, q // 2 % B
                if has(u + 1):
                    pe.wait_ge(att_split, split_no("Q", u + 1, 0, lap))
                for s in range(QT):
                    if has(u + 1):
                        n = QT * (u + 1) + s
                        hold(pe, exp_done, n - 1 + tiles)
                        mm3(pe, bank[s % 2][:], both(qT[:, (u + 1) % 2], slice(s * P, (s + 1) * P)),
                            both(ckvT, slice(b_s * S, (b_s + 1) * S)), True, True).then_inc(scores_ready, 1)
                    if has(u):
                        n = QT * u + s
                        pe.wait_ge(probs_ready, n + 1 + tiles)
                        if n >= 2:
                            pe.wait_ge(att_split, split_no("T", (n - 2) // QT, (n - 2) % QT, lap))
                        for k in range(QT):
                            op = pe.transpose(bank[2 + s % 2][:, k * P:(k + 1) * P], probs[:, s, k * P:(k + 1) * P], ident[:])
                        op.then_inc(att_product, 1)
                    if has(q) and s in (0, 2):
                        if s == 0:
                            if q:
                                pe.wait_ge(att_split, split_no("Q", q - 1, 0, lap))
                            pe.wait_ge(m_loaded, 32 * (q // LAP + 1 + lap))
                        for k in ((0, 1) if s == 0 else (2,)):
                            op = mm3(pe, bank[4][:], both(m_sb, q % 2, slice(k * P, (k + 1) * P)),
                                     both(cqT, k, slice(b_q * S, (b_q + 1) * S)), k == 0, k == KQ - 1)
                        if s == 2:
                            op.then_inc(att_product, 1)
                    if has(v):
                        if s == 0:
                            pe.wait_ge(att_split, split_no("T", v, QT - 1, lap))
                            if v:
                                pe.wait_ge(att_split, split_no("V", v - 1, 0, lap))
                        op = mm3(pe, bank[5][:], both(ckv[:, b_v], s, ALL), both(pT[:, v % 2], s, ALL), s == 0, s == QT - 1)
                        if s == QT - 1:
                            op.then_inc(att_product, 1)
                    if outs_of(u, s):
                        bb, i = outs_of(u, s)
                        m = QT * bb + i
                        pe.wait_ge(att_split, split_no("V", 2 * bb + 1, 0, lap))
                        pe.wait_ge(n_loaded, 32 * (bb // B + 1 + lap))
                        hold(pe, out_added, m - 1 + lap * (QT * LAP // 2))
                        slot = (bb // B + lap) % 2
                        for j in range(2):
                            op = mm3(pe, bank[6 + m % 2][:], both(mixT[:, bb % 2, j], slice(i * P, (i + 1) * P)),
                                     (n_sb[:, slot, 0, j, :], n_sb[:, slot, 1, j, :]), j == 0, j == 1)
                        op.then_inc(out_ready, 1)
            laps(pe, iteration)

            pe.wait_ge(out_added, QT * UNITS // 2)
            pe.wait_ge(mixw_high, 2)
            made = [0]

            def product(op):
                made[0] += 1
                op.then_inc(mix_product, 1)

            ends = {}

            def project3(b):
                pe.wait_ge(ctx_split, b + 1)
                if b:
                    pe.wait_ge(mix_split, ends["norm", b - 1, QT - 1])
                for i in range(2):
                    for k in range(KC):
                        op = mm3(pe, bank[4 + i][:], both(qkw, k, slice(i * P, (i + 1) * P)), both(ctxT, k, ALL),
                                 k == 0, k == KC - 1)
                    product(op)
                ends["project", b] = made[0]

            def scores3(b, s):
                n = QT * b + s
                if s == 0:
                    pe.wait_ge(mix_split, ends["project", b])
                hold(pe, exp3_done, n - 1)
                mm3(pe, bank[s % 2][:], both(qk3[:, 0], slice(s * P, (s + 1) * P)), both(qk3[:, 1], ALL), True, True).then_inc(scores3_ready, 1)

            def norm3(b, s):
                pe.wait_ge(norm3_ready, QT * b + s + 1)
                if s >= 2:
                    pe.wait_ge(mix_split, ends["norm", b, s - 2])
                for k in range(KD):
                    op = pe.transpose(bank[4 + s % 2][:, k * P:(k + 1) * P], xn3[:, s, k * P:(k + 1) * P], ident[:])
                product(op)
                ends["norm", b, s] = made[0]

            def turn3(b, s):
                pe.wait_ge(probs3_ready, QT * b + s + 1)
                if s >= 2:
                    pe.wait_ge(mix_split, ends["turn", b, s - 2])
                for k in range(QT):
                    op = pe.transpose(bank[2 + s % 2][:, k * P:(k + 1) * P], probs3[:, s, k * P:(k + 1) * P], ident[:])
                product(op)
                ends["turn", b, s] = made[0]

            def mix3(b, s):
                t = QT * b + s
                if s == 0:
                    pe.wait_ge(mix_split, ends["turn", b, QT - 1])
                hold(pe, mixed_added, t - 1)
                for k in range(QT):
                    op = mm3(pe, bank[6 + t % 2][:], both(xnT3[:, b % 2], k, slice(s * P, (s + 1) * P)),
                             both(pT3[:, b % 2], k, ALL), k == 0, k == QT - 1)
                op.then_inc(mixed_ready, 1)

            for b in range(B + 1):
                if b < B:
                    project3(b)
                for s in range(QT):
                    if b < B:
                        scores3(b, s)
                        norm3(b, s)
                    if b:
                        mix3(b - 1, s)
                if b < B:
                    for s in range(QT):
                        turn3(b, s)

            def logits(t):
                pe.wait_ge(ln4_split, t + 1)
                for k in range(KD):
                    op = mm3(pe, bank[2][:, t * E:(t + 1) * E], both(xnT4, k, slice(t * P, (t + 1) * P)), both(routw, k, ALL),
                             k == 0, k == KD - 1)
                op.then_inc(logits_ready, 1)

            pe.wait_ge(mixed_added, TT)
            for t in range(TT):
                pe.wait_ge(norm4_ready, t + 1)
                hold(pe, ln4_split, t - 1)
                for k in range(KD):
                    op = pe.transpose(bank[t % 2][:, k * P:(k + 1) * P], xn4[:, t % QT, k * P:(k + 1) * P], ident[:])
                op.then_inc(ln4_product, 1)
                if t == 0:
                    pe.wait_ge(rout_split, 1)
                if t:
                    logits(t - 1)
            logits(TT - 1)
            pe.wait_ge(gate_shift, 1)

            def weights(slot, k, width, at):
                return ew[:, slot, 0, at:at + width], ew[:, slot, 1, at:at + width]

            def gate_up(e, t):
                hold(pe, hid_ready, TT * e + t)
                for half in range(2):
                    for k in range(KD):
                        o = k * 2 * EH + half * EH
                        op = mm3(pe, bank[half][:, 0:EH], both(xnT4, k, slice(t * P, (t + 1) * P)),
                                 (ew[:, e % 2, 0, o:o + EH], ew[:, e % 2, 1, o:o + EH]), k == 0, k == KD - 1)
                op.then_inc(gu_ready, 1)

            def turn(e, t):
                pe.wait_ge(hid_ready, TT * e + t + 1)
                hold(pe, hidT_split, 2 * (TT * e + t))
                for k in range(KH):
                    op = pe.transpose(bank[2][0:HW[k], k * P:(k + 1) * P], hid[:, t % 2, k * P:k * P + HW[k]], ident[:])
                op.then_inc(hidT_product, 1)

            def down(e, t):
                pe.wait_ge(hidT_split, 2 * (TT * e + t) + 2)
                hold(pe, y_added, TT * e + t - 1)
                for k in range(KH):
                    o = KD * 2 * EH + k * D
                    r = HW[k]
                    op = mm3(pe, bank[3 + t % 2][:], (hidT[0:r, t % 2, 0, k, :], hidT[0:r, t % 2, 1, k, :]),
                             (ew[0:r, e % 2, 0, o:o + D], ew[0:r, e % 2, 1, o:o + D]), k == 0, k == KH - 1)
                op.then_inc(y_ready, 1)

            def expert(e):
                pe.wait_ge(ew_split, e + 1)
                gate_up(e, 0)
                for t in range(1, TT):
                    turn(e, t - 1)
                    gate_up(e, t)
                    down(e, t - 1)
                turn(e, TT - 1)
                down(e, TT - 1)

            expert(0)
            with pe.Fori(1, NE) as e:
                expert(e)


def kernel(**inputs):
    import numpy as np
    import concourse.bacc as bacc
    from concourse.bass_utils import run_bass_kernel_spmd

    a = {k: np.asarray(v) for k, v in inputs.items()}
    g = {k[8:]: v for k, v in a.items() if k.startswith("L0_attn_")}
    f = {k[7:]: v for k, v in a.items() if k.startswith("L0_ffn_")}

    def tiles(w):
        return w.reshape(-1, P, w.shape[1]).transpose(1, 0, 2)

    def columns(v):
        return v.reshape(-1, P).T

    uq, uk, uv = (g[k].reshape(H, DH, -1) for k in ("W_UQ_w", "W_UK_w", "W_UV_w"))
    wo = g["W_O_w"].T.reshape(H, DH, D)
    gu = [np.concatenate([f["wg"], f["wu"]], 2)]
    for i in range(NSH):
        gu.append(np.concatenate([f["sg"][:, i * EH:(i + 1) * EH], f["su"][:, i * EH:(i + 1) * EH]], 1)[None])
    gu = np.concatenate(gu, 0)
    data = {
        "x": a["x"].reshape(B * S, D),
        "proj_w": tiles(np.concatenate([g["W_DKV_w"], g["W_DQ_w"]], 0).T),
        "proj_b": columns(np.concatenate([g["W_DKV_b"], g["W_DQ_b"]])),
        "heads_w": np.concatenate([uq, uk, uv, wo], 2),
        "uq_b": columns(g["W_UQ_b"]),
        "uv_b": columns(g["W_UV_b"]),
        "o_b": g["W_O_b"],
        "ctx_t": tiles(a["ctx_1024"].reshape(B * S, C).T),
        "qk_w": tiles(np.concatenate([a["L0_xattn_Wq"], a["L0_xattn_Wk"]], 0).T),
        "qk_b": np.stack([a["L0_xattn_bq"], a["L0_xattn_bk"]], 1),
        "router_w": tiles(f["router_w"].T),
        "gate_up_w": gu.reshape(NE, KD, P, 2 * EH).transpose(0, 2, 1, 3).reshape(NE, P, KD * 2 * EH),
        "down_w": np.concatenate([f["wd"], f["sd"].reshape(NSH, EH, D)], 0),
    }
    data = {k: np.ascontiguousarray(v) for k, v in data.items()}
    nc = bacc.Bacc("TRN2", target_bir_lowering=False, num_devices=1)
    args = [nc.dram_tensor(k, v.shape, mybir.dt.from_np(v.dtype), kind="ExternalInput").ap() for k, v in data.items()]
    out = nc.dram_tensor("out", [B * S, D], F32, kind="ExternalOutput").ap()
    decoder_kernel(nc, *args, out)
    r = run_bass_kernel_spmd(nc, [data], core_ids=[0])
    return r.results[0]["out"].reshape(B, S, D)
```

```python
from contextlib import ExitStack

import concourse.bass as bass
from concourse import mybir
from concourse.alu_op_type import AluOpType as ALU

ACT = mybir.ActivationFunctionType
AX = mybir.AxisListType
F32 = mybir.dt.float32
F32R = mybir.dt.float32r
U32 = mybir.dt.uint32
I32 = mybir.dt.int32

P = 128
B, S, D = 4, 512, 512
QT = S // P
TT = B * QT
KD = D // P
H, DH = 16, 128
KVC, QC = 128, 384
KQ = QC // P
C = 256
KC = C // P
E, EH, NSH = 8, 352, 2
NE = E + NSH
KH = 3
HW = [128, 128, EH - 256]
EW = KD * 2 * EH + KH * D
LEAST = 2
SLOT_TILES = 2 * TT + E * LEAST
LN_EPS = 1e-5
GATE_EPS = 1e-20
SCALE = float(DH) ** -0.5

PACK = QC + KVC + KVC + D
O_UQ, O_UK, O_UV, O_WO = 0, QC, QC + KVC, QC + 2 * KVC
MN = QC + D

UNITS = H * B
LAP = 2 * B


def decoder_kernel(nc, x, proj_w, proj_b, heads_w, uq_b, uv_b, o_b, ctx_t, qk_w, qk_b,
                   router_w, gate_up_w, down_w, out):
    xv = x.rearrange("(t p) d -> p t d", p=P)
    ov = out.rearrange("(t p) d -> p t d", p=P)
    sorted_dram = nc.dram_tensor("sorted_rows", [SLOT_TILES * P, D], F32, kind="Internal").ap()
    routed_dram = sorted_dram
    mn_dram = nc.dram_tensor("mn_scratch", [H, P, 2, MN], F32, kind="Internal").ap()

    with ExitStack() as life:
        def sb(name, shape, dt=F32, stack=life):
            return stack.enter_context(nc.sbuf_tensor(name, shape, dt))

        def sem(name):
            return life.enter_context(nc.semaphore(name))

        resid = sb("resid", [P, TT, D])
        ident = sb("ident", [P, P])
        zero_rows = sb("zero_rows", [P, D])
        stats = sb("stats", [P, QT, 6])
        moments = sb("moments", [P, QT, 2])
        rstd = sb("rstd", [P, QT])
        vareps = sb("vareps", [P, QT])
        neg_half = sb("neg_half", [P, QT])
        negmax = sb("negmax", [P, 8])
        rowsum = sb("rowsum", [P, 8])
        rowinv = sb("rowinv", [P, 8])

        latents = ExitStack()
        ckvT = sb("ckvT", [P, 2, B * S], F32R, latents)
        ckv = sb("ckv", [P, B, 2, QT, KVC], F32R, latents)
        cqT = sb("cqT", [P, 2, KQ, B * S], F32R, latents)
        qbias = sb("qbias", [P, H], F32, latents)
        obias = sb("obias", [P, D], F32, latents)

        early = ExitStack()
        pack_raw = sb("pack_raw", [P, 2, PACK], F32, early)
        pack = sb("pack", [P, 2, 2, PACK], F32R, early)
        uvb_wide = sb("uvb_wide", [P, 2, P], F32, early)
        mn = sb("mn", [P, 2, 2, MN], F32R, early)
        uqb = sb("uqb", [P, H], F32, early)
        uvb = sb("uvb", [P, H], F32, early)
        ones = sb("ones", [P, P], F32, early)
        projw_raw = sb("projw_raw", [P, KD, D], F32, early)
        projw = sb("projw", [P, 2, KD, D], F32R, early)
        projb = sb("projb", [P, 1 + KQ], F32, early)
        xnT1 = sb("xnT1", [P, 2, KD, S], F32R, early)
        xn1 = sb("xn1", [P, QT, D], F32, early)
        early.close()

        mid = ExitStack()
        m_sb = sb("m_sb", [P, 2, 2, QC], F32R, mid)
        n_sb = sb("n_sb", [P, 2, 2, 2, D], F32R, mid)
        qT = sb("qT", [P, 2, 2, S], F32R, mid)
        probs = sb("probs", [P, QT, S], F32, mid)
        pT = sb("pT", [P, 2, 2, QT, S], F32R, mid)
        mixT = sb("mixT", [P, 2, 2, 2, S], F32R, mid)
        qb_now = sb("qb_now", [P, 2], F32, mid)
        mid.close()
        latents.close()

        late = ExitStack()
        ctx_raw = sb("ctx_raw", [P, 2, KC, S], F32, late)
        ctxT = sb("ctxT", [P, 2, KC, S], F32R, late)
        qkw_raw = sb("qkw_raw", [P, KC, 2 * P], F32, late)
        qkw = sb("qkw", [P, 2, KC, 2 * P], F32R, late)
        qkb = sb("qkb", [P, 2], F32, late)
        qk3 = sb("qk3", [P, 2, 2, S], F32R, late)
        probs3 = sb("probs3", [P, QT, S], F32, late)
        pT3 = sb("pT3", [P, 2, 2, QT, S], F32R, late)
        xnT3 = sb("xnT3", [P, 2, 2, KD, S], F32R, late)
        xn3 = sb("xn3", [P, QT, D], F32, late)
        late.close()

        last = ExitStack()
        xn4 = sb("xn4", [P, TT, D], F32, last)
        xT4 = sb("xT4", [P, 2, 2, KD, P], F32R, last)
        xT = xT4[:, 0]
        ew_raw = sb("ew_raw", [P, EW], F32, last)
        ew = sb("ew", [P, 2, 2, EW], F32R, last)
        routw_raw = sb("routw_raw", [P, KD, E], F32, last)
        routw = sb("routw", [P, 2, KD, E], F32R, last)
        rows = sb("rows", [P, D], F32, last)
        silu_g = sb("silu_g", [P, EH], F32, last)
        hid = sb("hid", [P, EH], F32, last)
        hidT = sb("hidT", [P, 2, KH, P], F32R, last)
        y_out = sb("y_out", [P, D], F32, last)
        picked = sb("picked", [P, 2, 2, D], F32, last)
        tri = sb("tri", [P, P], F32, last)
        ones4 = sb("ones4", [P, P], F32, last)
        grid_i = sb("grid_i", [P, 2, TT, E], I32, last)
        (logit, gate, pick, pick0, pick1, expert_no, tile_floor, rank, sum_a,
         sum_b) = (sb(f"grid{i}", [P, TT, E], F32, last) for i in range(10))
        top = sb("top", [P, TT, 8], F32, last)
        topi = sb("topi", [P, TT, 8], U32, last)
        topf = sb("topf", [P, TT, 8], F32, last)
        col16 = sb("col16", [P, TT], F32, last)
        col16b = sb("col16b", [P, TT], F32, last)
        tiles_of = sb("tiles_of", [P, E], F32, last)
        ends_a = sb("ends_a", [P, E], F32, last)
        ends_b = sb("ends_b", [P, E], F32, last)
        first_f = sb("first_f", [P, E + 1], F32, last)
        first_i = sb("first_i", [P, E + 1], I32, last)
        base = sb("base", [P, E], F32, last)
        choice_gate = sb("choice_gate", [P, 2, TT], F32, last)
        choice_slot = sb("choice_slot", [P, 2, TT], F32, last)
        choice_row = sb("choice_row", [P, 2, TT], U32, last)
        last.close()

        bank = [life.enter_context(nc.psum_tensor(f"bank{i}", [P, D], F32)) for i in range(8)]

        def trio(stage):
            return sem(f"{stage}_product"), sem(f"{stage}_high"), sem(f"{stage}_split")

        const_loaded = sem("const_loaded")
        x_loaded = sem("x_loaded")
        ident_zero = sem("ident_zero")
        ident_ready = sem("ident_ready")
        var_ready = sem("var_ready")
        rstd_ready = sem("rstd_ready")
        vec_step = sem("vec_step")

        pack_loaded = [sem("pack_loaded0"), sem("pack_loaded1")]
        pack_high = sem("pack_high")
        pack_split = sem("pack_split")
        head_bias = sem("head_bias")
        head_bias_taken = sem("head_bias_taken")
        fold_product, fold_high, fold_split = trio("fold")
        mn_stored = [sem("mn_stored0"), sem("mn_stored1")]

        projw_high = sem("projw_high")
        projw_split = sem("projw_split")
        norm1_ready = sem("norm1_ready")
        proj_product, proj_high, proj_split = trio("proj")
        obias_added = sem("obias_added")
        turned = sem("turned")
        turned_high = sem("turned_high")
        turned_low = sem("turned_low")

        m_loaded = sem("m_loaded")
        n_loaded = sem("n_loaded")
        att_product, att_high, att_split = trio("att")
        qb_ready = sem("qb_ready")
        scores_ready = sem("scores_ready")
        negmax_ready = sem("negmax_ready")
        exp_done = sem("exp_done")
        rowinv_ready = sem("rowinv_ready")
        probs_begun = sem("probs_begun")
        probs_ready = sem("probs_ready")
        out_ready = sem("out_ready")
        out_added = sem("out_added")

        mixw_loaded = sem("mixw_loaded")
        ctx_loaded = [sem("ctx_loaded0"), sem("ctx_loaded1")]
        mixw_high = sem("mixw_high")
        ctx_high = sem("ctx_high")
        ctx_split = sem("ctx_split")
        norm3_ready = sem("norm3_ready")
        mix_product, mix_high, mix_split = trio("mix")
        scores3_ready = sem("scores3_ready")
        negmax3_ready = sem("negmax3_ready")
        exp3_done = sem("exp3_done")
        rowinv3_ready = sem("rowinv3_ready")
        probs3_ready = sem("probs3_ready")
        mixed_ready = sem("mixed_ready")
        mixed_added = sem("mixed_added")

        rout_loaded = sem("rout_loaded")
        rout_high = sem("rout_high")
        rout_split = sem("rout_split")
        norm4_ready = sem("norm4_ready")
        ln4_product, ln4_high, ln4_split = trio("ln4")
        logits_ready = sem("logits_ready")
        gate_shift = sem("gate_shift")
        gate_exp = sem("gate_exp")
        grids_ready = sem("grids_ready")
        picks_ready = sem("picks_ready")
        ranks_ready = sem("ranks_ready")
        slots_ready = sem("slots_ready")
        zero_ready = sem("zero_ready")
        zeroed = sem("zeroed")
        scattered = sem("scattered")
        ew_loaded = sem("ew_loaded")
        ew_high = sem("ew_high")
        ew_split = sem("ew_split")
        rows_loaded = sem("rows_loaded")
        x_product, x_high, x_split = trio("x")
        gu_ready = sem("gu_ready")
        silu_done = sem("silu_done")
        hid_ready = sem("hid_ready")
        hidT_product, hidT_high, hidT_split = trio("hidT")
        y_ready = sem("y_ready")
        y_taken = sem("y_taken")
        routed_stored = sem("routed_stored")
        gathered_from = sem("gathered_from")
        gathered = sem("gathered")
        combining = sem("combining")
        combined = sem("combined")
        stored = sem("stored")

        def mm3(pe, acc, lhs, rhs, first, final):
            pe.matmul(acc, lhs[1], rhs[0], start=first, stop=False)
            pe.matmul(acc, lhs[0], rhs[1], start=False, stop=False)
            return pe.matmul(acc, lhs[0], rhs[0], start=False, stop=final)

        def both(t, *index):
            return t[(slice(None), 0) + index], t[(slice(None), 1) + index]

        def f32(ap):
            return ap.bitcast(F32)

        ALL = slice(None)

        splits, count = {}, 0
        for u in range(-2, UNITS + 3):
            for s in range(QT):
                for kind, unit, here in (("T", u, True), ("Q", u + 2, s == 2), ("V", u - 1, s == 3)):
                    if here and 0 <= unit < UNITS:
                        count += 1
                        splits[kind, unit, s if kind == "T" else 0] = count
        PER_LAP = LAP * (QT + 2)
        assert splits["T", 2 * LAP, 0] - splits["T", LAP, 0] == PER_LAP

        def split_no(kind, unit, s, lap):
            return splits[kind, unit, s] + PER_LAP * lap

        def has(unit):
            return 0 <= unit < UNITS

        def outs_of(u, s):
            if s % 2 == 0 or u < 3:
                return None
            bb, i = ((u - 3) // 2, s // 2) if u % 2 else ((u - 4) // 2, 2 + s // 2)
            return (bb, i) if 0 <= bb < UNITS // 2 else None

        def laps(eng, iteration):
            for u in range(-2, LAP):
                iteration(u, 0)
            with eng.Fori(0, UNITS // LAP - 2) as lap:
                for u in range(LAP, 2 * LAP):
                    iteration(u, lap)
            for u in range(UNITS - LAP, UNITS + 3):
                iteration(u, 0)

        def hold(eng, s, value):
            if not isinstance(value, int) or value > 0:
                eng.wait_ge(s, value)

        def first_unit(eng, e):
            least = LEAST * e if isinstance(e, int) else LEAST
            return TT + eng.value_load(first_i[0:1, bass.ds(e, 1)], min_val=least, max_val=SLOT_TILES)

        def units(eng, begin, unit, end):
            begin()
            with eng.Fori(1, TT) as n:
                unit(n, 0, 0, "shared", n, "shared", n - 1)
            eng.wait_ge(slots_ready, 1)

            def expert(e, before):
                start, stop = first_unit(eng, e), first_unit(eng, e + 1)
                unit(start, (e + 1) % 2, e % 2, "routed", None, before, TT - 1, opens=e + 1)
                with eng.Fori(start + 1, stop) as n:
                    unit(n, (e + 1) % 2, (e + 1) % 2, "routed", None, "routed", None)

            expert(0, "shared")
            with eng.Fori(1, E) as e:
                expert(e, "routed")
            start = first_unit(eng, E)
            unit(start, (NE - 1) % 2, NE % 2, "combined", 0, "routed", None, opens=NE - 1)
            with eng.Fori(1, TT - 1) as t:
                unit(start + t, (NE - 1) % 2, (NE - 1) % 2, "combined", t, "combined", t - 1)
            unit(start + (TT - 1), (NE - 1) % 2, (NE - 1) % 2, "combined", TT - 1, "combined", TT - 2, more=False)
            end(start + TT)

        block = life.enter_context(nc.Block())

        @block.sync
        def _(sp):
            def load_head(h, j):
                hold(sp, fold_product, 2 * h - 2)
                sp.dma_start(pack_raw[:, j, :], heads_w[h]).then_inc(pack_loaded[j], 16)

            def store_fold(h, j):
                sp.wait_ge(fold_split, 2 * h + 2)
                sp.dma_start(mn_dram[h], f32(mn[:, j, :, :])).then_inc(mn_stored[j], 16)

            for dst, src in ((uqb, uq_b), (uvb, uv_b), (projb, proj_b)):
                sp.dma_start(dst[:], src).then_inc(const_loaded, 16)
            sp.dma_start(obias[:], o_b.partition_broadcast(P)).then_inc(const_loaded, 16)
            load_head(0, 0)
            load_head(1, 1)
            sp.dma_start(projw_raw[:], proj_w).then_inc(const_loaded, 16)
            for b in range(B):
                sp.dma_start(resid[:, QT * b:QT * (b + 1), :], xv[:, QT * b:QT * (b + 1), :]).then_inc(x_loaded, 16)
            with sp.Fori(0, H // 2 - 1) as i:
                for j in range(2):
                    store_fold(2 * i + j, j)
                    load_head(2 * i + j + 2, j)
            for j in range(2):
                store_fold(H - 2 + j, j)

            sp.wait_ge(zero_ready, 1)
            with sp.Fori(0, SLOT_TILES) as i:
                sp.dma_start(sorted_dram[bass.ds(i * P, P), :], zero_rows[:]).then_inc(zeroed, 16)

            def load_m(pair):
                for j in range(2):
                    sp.dma_start(f32(m_sb[:, :, j, :]), mn_dram[2 * pair + j][:, :, 0:QC]).then_inc(m_loaded, 16)

            def load_n(pair, slot):
                for j in range(2):
                    sp.dma_start(f32(n_sb[:, slot, :, j, :]), mn_dram[2 * pair + j][:, :, QC:MN]).then_inc(n_loaded, 16)

            for j in range(2):
                sp.wait_ge(mn_stored[j], 16 * (H // 2))
            sp.wait_ge(proj_split, B * (QT + 1 + KQ))
            load_m(0)
            load_n(0, 0)
            sp.wait_ge(att_product, splits["Q", LAP - 1, 0])
            load_m(1)
            load_n(1, 1)
            with sp.Fori(2, UNITS // LAP) as pair:
                sp.wait_ge(att_product, splits["Q", LAP - 1, 0] + PER_LAP * (pair - 1))
                load_m(pair)
                sp.wait_ge(out_ready, QT * B * (pair - 1))
                load_n(pair, pair % 2)

            sp.wait_ge(out_ready, QT * UNITS // 2)
            sp.wait_ge(out_added, QT * UNITS // 2)
            sp.dma_start(qkw_raw[:], qk_w).then_inc(mixw_loaded, 16)
            sp.dma_start(qkb[:], qk_b).then_inc(mixw_loaded, 16)
            for b in range(B):
                if b >= 2:
                    sp.wait_ge(ctx_split, b - 1)
                sp.dma_start(ctx_raw[:, b % 2, :, :], ctx_t[:, :, b * S:(b + 1) * S]).then_inc(ctx_loaded[b % 2], 16)

            sp.wait_ge(mixed_added, TT)
            sp.dma_start(routw_raw[:], router_w).then_inc(rout_loaded, 16)

            def load_rows(n, src):
                hold(sp, x_product, n)
                sp.dma_start(rows[:], src).then_inc(rows_loaded, 16)

            def sorted_rows(n):
                return sorted_dram[bass.ds((n - TT) * P, P), :]

            sp.wait_ge(norm4_ready, TT)
            load_rows(0, xn4[:, 0, :])
            with sp.Fori(1, TT) as n:
                load_rows(n, xn4[:, bass.ds(n, 1), :].rearrange("p o d -> p (o d)"))
            sp.wait_ge(slots_ready, 1)
            sp.wait_ge(scattered, 16 * 2 * TT)
            stop = first_unit(sp, E)
            load_rows(TT, sorted_dram[0:P, :])
            with sp.Fori(TT + 1, stop) as n:
                load_rows(n, sorted_rows(n))
            load_rows(stop, xn4[:, 0, :])

            with sp.Fori(1, TT) as t:
                load_rows(stop + t, xn4[:, bass.ds(t, 1), :].rearrange("p o d -> p (o d)"))
            sp.wait_ge(stored, 16 * TT)

        @block.gpsimd
        def _(pool):
            norms = [0]

            def inverse_std():
                norms[0] += 1
                pool.wait_ge(var_ready, norms[0])
                pool.tensor_tensor(rstd[:], vareps[:], neg_half[:], ALU.pow).then_inc(rstd_ready, 1)

            pool.memset(zero_rows[:], 0.0).then_inc(zero_ready, 1)
            pool.memset(neg_half[:], -0.5)
            pool.memset(ident[:], 0.0).then_inc(ident_zero, 1)
            pool.memset(ones[:], 1.0).then_inc(ident_ready, 1)
            pool.wait_ge(ident_zero, 1)
            pool.affine_select(out=ident[:], in_=ident[:], compare_op=ALU.not_equal, fill=1.0, base=0,
                               pattern=[[-1, P]], channel_multiplier=1).then_inc(ident_ready, 1)
            for t in range(TT):
                if t % QT == 0:
                    inverse_std()
                pool.wait_ge(norm1_ready, t + 1)
                pool.wait_ge(head_bias_taken, H)
                pool.tensor_tensor(resid[:, t, :], resid[:, t, :], obias[:], ALU.add).then_inc(obias_added, 1)

            def iteration(u, lap):
                for s in range(QT):
                    if has(u + 1):
                        n = QT * (u + 1) + s
                        pool.wait_ge(rowinv_ready, n + 1 + lap * (QT * LAP))
                        pool.sem_inc(probs_begun, 1)
                        pool.tensor_scalar(probs[:, s, :], probs[:, s, :], rowinv[:, n % 8:n % 8 + 1], None,
                                           ALU.mult).then_inc(probs_ready, 1)
            laps(pool, iteration)

            def ctx_low(b):
                pool.wait_ge(ctx_high, b + 1)
                pool.tensor_tensor(ctxT[:, 1, :, :], ctx_raw[:, b % 2, :, :], f32(ctxT[:, 0, :, :]),
                                   ALU.subtract).then_inc(ctx_split, 1)

            def probs_tile(n):
                pool.wait_ge(rowinv3_ready, n + 1)
                pool.tensor_scalar(probs3[:, n % QT, :], probs3[:, n % QT, :], rowinv[:, n % 8:n % 8 + 1], None,
                                   ALU.mult).then_inc(probs3_ready, 1)

            ctx_low(0)
            for b in range(B):
                inverse_std()
                for s in range(QT):
                    probs_tile(QT * b + s)
                if b + 1 < B:
                    ctx_low(b + 1)

            def load_expert(pos):
                hold(pool, ew_split, pos)
                pool.dma_start(ew_raw[:, 0:KD * 2 * EH], gate_up_w[pos]).then_inc(ew_loaded, 16)
                for k in range(KH):
                    o = KD * 2 * EH + k * D
                    pool.dma_start(ew_raw[0:HW[k], o:o + D], down_w[pos, k * P:k * P + HW[k], :]).then_inc(ew_loaded, 16)

            def expert_low(pos):
                pool.wait_ge(ew_high, 2 * pos + 2)
                for rws, c0, c1 in ((P, 0, EW - D), (HW[2], EW - D, EW)):
                    op = pool.tensor_tensor(ew[0:rws, pos % 2, 1, c0:c1], ew_raw[0:rws, c0:c1],
                                            f32(ew[0:rws, pos % 2, 0, c0:c1]), ALU.subtract)
                op.then_inc(ew_split, 1)

            pool.wait_ge(mixed_added, TT)
            load_expert(0)
            pool.iota(grid_i[:, 0], pattern=[[0, TT], [1, E]], base=0, channel_multiplier=0)
            pool.iota(grid_i[:, 1], pattern=[[P, TT], [0, E]], base=0, channel_multiplier=0)
            pool.memset(ones4[:], 1.0).then_inc(grids_ready, 1)
            pool.wait_ge(grids_ready, 1)
            pool.affine_select(out=tri[:], in_=ones4[:], compare_op=ALU.is_gt, fill=0.0, base=0,
                               pattern=[[1, P]], channel_multiplier=-1).then_inc(grids_ready, 1)
            for b in range(B):
                inverse_std()
            expert_low(0)
            load_expert(1)

            pool.wait_ge(slots_ready, 1)
            pool.wait_ge(zeroed, 16 * SLOT_TILES)
            pool.wait_ge(norm4_ready, TT)
            for t in range(TT):
                for c in range(2):
                    pool.indirect_dma_start(sorted_dram, bass.IndirectOffsetOnAxis(ap=choice_row[:, c, t:t + 1], axis=0),
                                            xn4[:, t, :], None).then_inc(scattered, 16)
            expert_low(1)
            with pool.Fori(2, NE) as pos:
                load_expert(pos)
                expert_low(pos)

            stop = first_unit(pool, E)
            pool.wait_ge(routed_stored, (stop - TT + 1) * 16)
            pool.sem_inc(gathered_from, 1)
            def store_out(t):
                pool.wait_ge(combined, t + 1)
                pool.dma_start(ov[:, t, :], resid[:, t, :]).then_inc(stored, 16)

            for t in range(TT):
                if t >= 2:
                    store_out(t - 2)
                for c in range(2):
                    pool.indirect_dma_start(picked[:, t % 2, c, :], None, routed_dram,
                                            bass.IndirectOffsetOnAxis(ap=choice_row[:, c, t:t + 1], axis=0)).then_inc(gathered, 16)
                pool.wait_ge(gathered, 32 * (t + 1))
            store_out(TT - 2)
            store_out(TT - 1)

        @block.scalar
        def _(act):
            def copy(dst, src, scale=1.0):
                return act.activation(dst, src, ACT.Copy, scale=scale)

            def head_weights(i, h, j):
                act.wait_ge(pack_loaded[j], 16 * i + 16)
                hold(act, fold_product, 2 * h - 2)
                copy(pack[:, j, 0, :], pack_raw[:, j, :]).then_inc(pack_high, 1)

            def head_fold(i, h, j):
                hold(act, mn_stored[j], 16 * i)
                act.wait_ge(fold_product, 2 * h + 1)
                copy(mn[:, j, 0, 0:QC], bank[2 * j][:, 0:QC], SCALE).then_inc(fold_high, 1)
                act.wait_ge(fold_product, 2 * h + 2)
                copy(mn[:, j, 0, QC:MN], bank[2 * j + 1][:]).then_inc(fold_high, 1)

            head_weights(0, 0, 0)
            head_weights(0, 1, 1)
            head_fold(0, 0, 0)
            head_weights(1, 2, 0)
            head_fold(0, 1, 1)
            with act.Fori(1, H // 2 - 1) as i:
                head_weights(i, 2 * i + 1, 1)
                head_fold(i, 2 * i, 0)
                head_weights(i + 1, 2 * i + 2, 0)
                head_fold(i, 2 * i + 1, 1)
            head_weights(H // 2 - 1, H - 1, 1)
            head_fold(H // 2 - 1, H - 2, 0)
            head_fold(H // 2 - 1, H - 1, 1)

            act.wait_ge(const_loaded, 16 * 5)
            copy(projw[:, 0, :, :], projw_raw[:]).then_inc(projw_high, 1)
            n = 0
            for b in range(B):
                cols = slice(b * S, (b + 1) * S)
                for t in range(QT):
                    n += 1
                    act.wait_ge(proj_product, n)
                    copy(xnT1[:, 0, :, t * P:(t + 1) * P], bank[t % 2][:].rearrange("p (k c) -> p k c", k=KD)).then_inc(proj_high, 1)
                for m in range(1 + KQ):
                    n += 1
                    act.wait_ge(proj_product, n)
                    dst = ckvT[:, 0, cols] if m == 0 else cqT[:, 0, m - 1, cols]
                    act.activation(dst, bank[2 + m][:], ACT.Identity, bias=projb[:, m:m + 1]).then_inc(proj_high, 1)
                act.wait_ge(turned, 2 * b + 1)
                copy(ckv[:, b, 0, :, :], bank[6][:].rearrange("p (k c) -> p k c", k=QT)).then_inc(turned_high, 1)

            def iteration(u, lap):
                tiles = lap * (QT * LAP)
                for s in range(QT):
                    if has(u):
                        act.wait_ge(att_product, split_no("T", u, s, lap))
                        copy(pT[:, u % 2, 0, :, s * P:(s + 1) * P],
                             bank[2 + s % 2][:].rearrange("p (k c) -> p k c", k=QT)).then_inc(att_high, 1)
                    if has(u + 1):
                        n = QT * (u + 1) + s
                        act.wait_ge(negmax_ready, n + 1 + tiles)
                        act.activation(probs[:, s, :], bank[s % 2][:], ACT.Exp, bias=negmax[:, n % 8:n % 8 + 1],
                                       accum_out=rowsum[:, n % 8:n % 8 + 1]).then_inc(exp_done, 1)
                    if s == 2 and has(u + 2):
                        q = u + 2
                        act.wait_ge(qb_ready, q // LAP + 1 + lap)
                        act.wait_ge(att_product, split_no("Q", q, 0, lap))
                        act.activation(qT[:, q % 2, 0, :], bank[4][:], ACT.Identity,
                                       bias=qb_now[:, q % 2:q % 2 + 1]).then_inc(att_high, 1)
                    if s == 3 and has(u - 1):
                        v = u - 1
                        act.wait_ge(att_product, split_no("V", v, 0, lap))
                        copy(mixT[:, v // 2 % 2, v % 2, 0, :], bank[5][:]).then_inc(att_high, 1)
            act.wait_ge(proj_split, B * (QT + 1 + KQ))
            for j in range(2):
                act.wait_ge(mn_stored[j], 16 * (H // 2))
            laps(act, iteration)

            act.wait_ge(out_added, QT * UNITS // 2)
            act.wait_ge(mixw_loaded, 32)
            copy(qkw[:, 0, :, :], qkw_raw[:]).then_inc(mixw_high, 1)
            prod = [0]

            def high(dst, src, bias=None):
                prod[0] += 1
                act.wait_ge(mix_product, prod[0])
                if bias is None:
                    copy(dst, src).then_inc(mix_high, 1)
                else:
                    act.activation(dst, src, ACT.Identity, bias=bias).then_inc(mix_high, 1)

            def ctx_part(b):
                act.wait_ge(ctx_loaded[b % 2], 16 * (b // 2 + 1))
                copy(ctxT[:, 0, :, :], ctx_raw[:, b % 2, :, :]).then_inc(ctx_high, 1)
                for i in range(2):
                    high(qk3[:, i, 0, :], bank[4 + i][:], qkb[:, i:i + 1])

            def exp_tile(b, s):
                n = QT * b + s
                act.wait_ge(negmax3_ready, n + 1)
                act.activation(probs3[:, s, :], bank[s % 2][:], ACT.Exp, bias=negmax[:, n % 8:n % 8 + 1],
                               accum_out=rowsum[:, n % 8:n % 8 + 1]).then_inc(exp3_done, 1)

            def norm_part(b, s):
                high(xnT3[:, b % 2, 0, :, s * P:(s + 1) * P], bank[4 + s % 2][:].rearrange("p (k c) -> p k c", k=KD))

            def turn_part(b, s):
                high(pT3[:, b % 2, 0, :, s * P:(s + 1) * P], bank[2 + s % 2][:].rearrange("p (k c) -> p k c", k=QT))

            for b in range(B):
                ctx_part(b)
                for s in range(QT):
                    exp_tile(b, s)
                    norm_part(b, s)
                for s in range(QT):
                    turn_part(b, s)

            act.wait_ge(rout_loaded, 16)
            copy(routw[:, 0, :, :], routw_raw[:]).then_inc(rout_high, 1)
            for t in range(TT):
                act.wait_ge(ln4_product, t + 1)
                copy(xT4[:, t % 2, 0], bank[t % 2][:].rearrange("p (k c) -> p k c", k=KD)).then_inc(ln4_high, 1)
            act.wait_ge(gate_shift, 1)
            act.activation(gate[:], gate[:], ACT.Exp).then_inc(gate_exp, 1)

            def expert_high(pos):
                act.wait_ge(ew_loaded, 64 * pos + 64)
                for rws, c0, c1 in ((P, 0, EW - D), (HW[2], EW - D, EW)):
                    copy(ew[0:rws, pos % 2, 0, c0:c1], ew_raw[0:rws, c0:c1]).then_inc(ew_high, 1)

            def x_part(n):
                act.wait_ge(x_product, n + 1)
                copy(xT[:, 0], bank[4][:].rearrange("p (k c) -> p k c", k=KD)).then_inc(x_high, 1)

            def silu(n):
                act.wait_ge(gu_ready, n + 1)
                act.activation(silu_g[:], bank[0][:, 0:EH], ACT.Silu).then_inc(silu_done, 1)

            def hid_part(n):
                act.wait_ge(hidT_product, n + 1)
                for k, rws in ((slice(0, 2), P), (slice(2, 3), HW[2])):
                    copy(hidT[0:rws, 0, k, :],
                         bank[2][0:rws, k.start * P:k.stop * P].rearrange("p (k c) -> p k c", c=P)).then_inc(hidT_high, 1)

            def take_routed(n):
                act.wait_ge(y_ready, n + 1)
                act.wait_ge(routed_stored, (n - TT + 1) * 16)
                copy(y_out[:], bank[3][:]).then_inc(y_taken, 1)
                act.wait_ge(y_taken, n + 1)
                act.dma_start(routed_dram[bass.ds((n - TT) * P, P), :], y_out[:]).then_inc(routed_stored, 16)

            def begin():
                x_part(0)
                silu(0)
                x_part(1)
                expert_high(1)

            def unit(n, slot, last_slot, stage, tile, last_stage, last_tile, opens=None, more=True):
                hid_part(n - 1)
                silu(n)
                if more:
                    x_part(n + 1)
                if last_stage == "routed":
                    take_routed(n - 1)
                if opens is not None and not (isinstance(opens, int) and opens == NE - 1):
                    if last_stage != "routed":
                        act.wait_ge(y_ready, n)
                    expert_high(opens + 1)

            def end(n):
                hid_part(n - 1)

            act.sem_inc(routed_stored, 16)
            expert_high(0)
            units(act, begin, unit, end)

        @block.vector
        def _(dve):
            step, norms = [0], [0]

            def own(op):
                step[0] += 1
                op.then_inc(vec_step, 1)
                return step[0]

            def normalize(xn, b, ready, tiles_free, tiles_free_value):
                for t in range(QT):
                    n = own(dve.bn_stats(stats[:, t, :], resid[:, QT * b + t, :]))
                dve.wait_ge(vec_step, n)
                for t in range(QT):
                    n = own(dve.bn_aggr(moments[:, t, :], stats[:, t, :]))
                dve.wait_ge(vec_step, n)
                dve.tensor_scalar(vareps[:], moments[:, :, 1], LN_EPS, None, ALU.add).then_inc(var_ready, 1)
                norms[0] += 1
                dve.wait_ge(rstd_ready, norms[0])
                hold(dve, tiles_free, tiles_free_value)
                for t in range(QT):
                    dve.tensor_scalar(xn[:, t, :], resid[:, QT * b + t, :], moments[:, t, 0:1], rstd[:, t:t + 1],
                                      ALU.subtract, ALU.mult).then_inc(ready, 1)

            def low(dst, src, hi, scale=1.0):
                return dve.scalar_tensor_tensor(dst, src, scale, f32(hi), ALU.mult, ALU.subtract)

            def low_bias(dst, src, bias, hi):
                return dve.scalar_tensor_tensor(dst, src, bias, f32(hi), ALU.add, ALU.subtract)

            def head_weights(h, j):
                dve.wait_ge(ident_ready, 2)
                dve.wait_ge(pack_high, h + 1)
                low(pack[:, j, 1, :], pack_raw[:, j, :], pack[:, j, 0, :]).then_inc(pack_split, 1)
                dve.tensor_scalar(uvb_wide[:, j, :], ones[:], uvb[:, bass.ds(h, 1)], None, ALU.mult).then_inc(pack_split, 1)

            def head_fold(h, j):
                dve.wait_ge(head_bias, h + 1)
                hold(dve, head_bias_taken, h)
                dve.tensor_scalar(qbias[:, bass.ds(h, 1)], bank[4 + 3 * j][:, 0:1], SCALE, None, ALU.mult)
                dve.tensor_tensor(obias[:], obias[:], bank[5 + j][:], ALU.add).then_inc(head_bias_taken, 1)
                dve.wait_ge(fold_high, 2 * h + 1)
                low(mn[:, j, 1, 0:QC], bank[2 * j][:, 0:QC], mn[:, j, 0, 0:QC], SCALE).then_inc(fold_split, 1)
                dve.wait_ge(fold_high, 2 * h + 2)
                low(mn[:, j, 1, QC:MN], bank[2 * j + 1][:], mn[:, j, 0, QC:MN]).then_inc(fold_split, 1)

            dve.wait_ge(const_loaded, 16 * 5)
            head_weights(0, 0)
            head_weights(1, 1)
            head_fold(0, 0)
            head_weights(2, 0)
            head_fold(1, 1)
            with dve.Fori(1, H // 2 - 1) as i:
                head_weights(2 * i + 1, 1)
                head_fold(2 * i, 0)
                head_weights(2 * i + 2, 0)
                head_fold(2 * i + 1, 1)
            head_weights(H - 1, 1)
            head_fold(H - 2, 0)
            head_fold(H - 1, 1)

            dve.wait_ge(projw_high, 1)
            low(projw[:, 1, :, :], projw_raw[:], projw[:, 0, :, :]).then_inc(projw_split, 1)
            n = 0
            per = QT + 1 + KQ
            for b in range(B):
                cols = slice(b * S, (b + 1) * S)
                dve.wait_ge(x_loaded, 16 * B)
                normalize(xn1, b, norm1_ready, proj_product, per * (b - 1) + QT)
                for t in range(QT):
                    n += 1
                    dve.wait_ge(proj_high, n)
                    low(xnT1[:, 1, :, t * P:(t + 1) * P], bank[t % 2][:].rearrange("p (k c) -> p k c", k=KD),
                        xnT1[:, 0, :, t * P:(t + 1) * P]).then_inc(proj_split, 1)
                for m in range(1 + KQ):
                    n += 1
                    dve.wait_ge(proj_high, n)
                    part = (ckvT[:, i, cols] if m == 0 else cqT[:, i, m - 1, cols] for i in range(2))
                    hi, lo = part
                    low_bias(lo, bank[2 + m][:], projb[:, m:m + 1], hi).then_inc(proj_split, 1)
                dve.wait_ge(turned, 2 * b + 2)
                dve.tensor_copy(ckv[:, b, 1, :, :], bank[7][:].rearrange("p (k c) -> p k c", k=QT)).then_inc(turned_low, 1)

            def invert(n, lap):
                dve.wait_ge(exp_done, n + 1 + lap * (QT * LAP))
                dve.reciprocal(rowinv[:, n % 8:n % 8 + 1], rowsum[:, n % 8:n % 8 + 1]).then_inc(rowinv_ready, 1)

            def iteration(u, lap):
                tiles = lap * (QT * LAP)
                q, v = u + 2, u - 1
                if has(q) and q % LAP == 0:
                    dve.tensor_copy(qb_now[:], qbias[:, bass.ds((q // LAP + lap) * 2, 2)]).then_inc(qb_ready, 1)
                for s in range(QT):
                    n = QT * (u + 1) + s
                    if has((n - 1) // QT):
                        invert(n - 1, lap)
                    if has(u + 1):
                        dve.wait_ge(scores_ready, n + 1 + tiles)
                        dve.tensor_reduce(negmax[:, n % 8:n % 8 + 1], bank[s % 2][:], AX.X, ALU.max,
                                          negate=True).then_inc(negmax_ready, 1)
                    if has(u):
                        dve.wait_ge(att_high, split_no("T", u, s, lap))
                        low(pT[:, u % 2, 1, :, s * P:(s + 1) * P], bank[2 + s % 2][:].rearrange("p (k c) -> p k c", k=QT),
                            pT[:, u % 2, 0, :, s * P:(s + 1) * P]).then_inc(att_split, 1)
                    if s == 2 and has(q):
                        dve.wait_ge(att_high, split_no("Q", q, 0, lap))
                        low_bias(qT[:, q % 2, 1, :], bank[4][:], qb_now[:, q % 2:q % 2 + 1], qT[:, q % 2, 0, :]).then_inc(att_split, 1)
                    if outs_of(u, s):
                        bb, i = outs_of(u, s)
                        m = QT * bb + i
                        t = QT * (bb % B) + i
                        dve.wait_ge(out_ready, m + 1 + lap * (QT * LAP // 2))
                        dve.tensor_tensor(resid[:, t, :], resid[:, t, :], bank[6 + m % 2][:], ALU.add).then_inc(out_added, 1)
                    if s == 3 and has(v):
                        dve.wait_ge(att_high, split_no("V", v, 0, lap))
                        low(mixT[:, v // 2 % 2, v % 2, 1, :], bank[5][:], mixT[:, v // 2 % 2, v % 2, 0, :]).then_inc(att_split, 1)
            dve.wait_ge(obias_added, TT)
            dve.wait_ge(head_bias_taken, H)
            for j in range(2):
                dve.wait_ge(mn_stored[j], 16 * (H // 2))
            laps(dve, iteration)

            dve.wait_ge(out_added, QT * UNITS // 2)
            dve.wait_ge(mixw_high, 1)
            low(qkw[:, 1, :, :], qkw_raw[:], qkw[:, 0, :, :]).then_inc(mixw_high, 1)
            prod = [0]

            def split(dst, src, hi, bias=None):
                prod[0] += 1
                dve.wait_ge(mix_high, prod[0])
                (low(dst, src, hi) if bias is None else low_bias(dst, src, bias, hi)).then_inc(mix_split, 1)

            def invert3(n):
                dve.wait_ge(exp3_done, n + 1)
                dve.reciprocal(rowinv[:, n % 8:n % 8 + 1], rowsum[:, n % 8:n % 8 + 1]).then_inc(rowinv3_ready, 1)

            for b in range(B + 1):
                if b < B:
                    for i in range(2):
                        split(qk3[:, i, 1, :], bank[4 + i][:], qk3[:, i, 0, :], qkb[:, i:i + 1])
                    normalize(xn3, b, norm3_ready, mix_product, (2 + QT + QT) * (b - 1) + 2 + QT)
                for s in range(QT):
                    n = QT * b + s
                    if b < B:
                        dve.wait_ge(scores3_ready, n + 1)
                        dve.tensor_reduce(negmax[:, n % 8:n % 8 + 1], bank[s % 2][:], AX.X, ALU.max,
                                          negate=True).then_inc(negmax3_ready, 1)
                        part = (slice(None), slice(s * P, (s + 1) * P))
                        split(xnT3[(ALL, b % 2, 1) + part], bank[4 + s % 2][:].rearrange("p (k c) -> p k c", k=KD),
                              xnT3[(ALL, b % 2, 0) + part])
                        invert3(n)
                    if b:
                        t = QT * (b - 1) + s
                        dve.wait_ge(mixed_ready, t + 1)
                        dve.tensor_tensor(resid[:, t, :], resid[:, t, :], bank[6 + t % 2][:], ALU.add).then_inc(mixed_added, 1)
                if b < B:
                    for s in range(QT):
                        part = (slice(None), slice(s * P, (s + 1) * P))
                        split(pT3[(ALL, b % 2, 1) + part], bank[2 + s % 2][:].rearrange("p (k c) -> p k c", k=QT),
                              pT3[(ALL, b % 2, 0) + part])

            dve.wait_ge(mixed_added, TT)
            for b in range(B):
                normalize(xn4[:, QT * b:QT * (b + 1)], b, norm4_ready, ln4_product, 0)
                if b == 0:
                    dve.wait_ge(rout_high, 1)
                    low(routw[:, 1, :, :], routw_raw[:], routw[:, 0, :, :]).then_inc(rout_split, 1)
                for t in range(QT * b, QT * (b + 1)):
                    dve.wait_ge(ln4_high, t + 1)
                    low(xT4[:, t % 2, 1], bank[t % 2][:].rearrange("p (k c) -> p k c", k=KD),
                        xT4[:, t % 2, 0]).then_inc(ln4_split, 1)

            def wide(col):
                return col.unsqueeze(2).to_broadcast([P, TT, E])

            def across(row):
                return row.unsqueeze(1).to_broadcast([P, TT, E])

            def then(op):
                dve.wait_ge(vec_step, own(op))

            dve.wait_ge(grids_ready, 2)
            then(dve.tensor_copy(expert_no[:], grid_i[:, 0]))
            then(dve.tensor_copy(tile_floor[:], grid_i[:, 1]))
            dve.wait_ge(logits_ready, TT)
            then(dve.tensor_copy(logit[:], bank[2][:, 0:TT * E].rearrange("p (t e) -> p t e", e=E)))
            then(dve.tensor_reduce(col16[:], logit[:], AX.X, ALU.max))
            dve.tensor_tensor(gate[:], logit[:], wide(col16[:]), ALU.subtract).then_inc(gate_shift, 1)
            dve.wait_ge(gate_exp, 1)
            then(dve.tensor_reduce(col16[:], gate[:], AX.X, ALU.add))
            then(dve.reciprocal(col16b[:], col16[:]))
            then(dve.tensor_tensor(gate[:], gate[:], wide(col16b[:]), ALU.mult))
            for t in range(TT):
                n = own(dve.max(top[:, t, :], gate[:, t, :]))
            dve.wait_ge(vec_step, n)
            for t in range(TT):
                n = own(dve.max_index(topi[:, t, :], top[:, t, :], gate[:, t, :]))
            dve.wait_ge(vec_step, n)
            then(dve.tensor_copy(topf[:], topi[:]))
            dve.tensor_tensor(pick0[:], expert_no[:], wide(topf[:, :, 0]), ALU.is_equal)
            then(dve.tensor_tensor(pick1[:], expert_no[:], wide(topf[:, :, 1]), ALU.is_equal))
            dve.tensor_tensor(pick[:], pick0[:], pick1[:], ALU.add).then_inc(picks_ready, 1)
            dve.wait_ge(picks_ready, 1)
            then(dve.tensor_tensor(gate[:], gate[:], pick[:], ALU.mult))
            then(dve.tensor_reduce(col16[:], gate[:], AX.X, ALU.add))
            then(dve.tensor_scalar(col16[:], col16[:], GATE_EPS, None, ALU.add))
            then(dve.reciprocal(col16b[:], col16[:]))
            then(dve.tensor_tensor(gate[:], gate[:], wide(col16b[:]), ALU.mult))

            dve.wait_ge(ranks_ready, 1)
            counts = bank[5][:, TT * E:2 * TT * E].rearrange("p (t e) -> p t e", e=E)
            dve.tensor_copy(rank[:], bank[5][:, 0:TT * E].rearrange("p (t e) -> p t e", e=E))
            then(dve.tensor_copy(sum_a[:], counts))

            def running(a, b, shape, size):
                d = 1
                while d < size:
                    dve.tensor_tensor(b[:, d:size], a[:, d:size], a[:, 0:size - d], ALU.add)
                    then(dve.tensor_copy(b[:, 0:d], a[:, 0:d]))
                    a, b = b, a
                    d *= 2
                return a, b

            total, spare = running(sum_a, sum_b, None, TT)
            tokens_of = total[:, TT - 1, :]
            then(dve.tensor_tensor(spare[:], across(tokens_of), tile_floor[:], ALU.is_gt))
            then(dve.tensor_reduce(tiles_of[:], spare[:].rearrange("p t e -> p e t"), AX.X, ALU.add))
            then(dve.tensor_scalar(ends_a[:], tiles_of[:], float(LEAST), None, ALU.max))
            then(dve.tensor_copy(tiles_of[:], ends_a[:]))
            ends, _ = running(ends_a, ends_b, None, E)
            dve.memset(first_f[:, 0:1], 0.0)
            then(dve.tensor_copy(first_f[:, 1:E + 1], ends[:]))
            then(dve.tensor_copy(first_i[:], first_f[:]))
            then(dve.tensor_tensor(base[:], ends[:], tiles_of[:], ALU.subtract))
            then(dve.tensor_scalar(base[:], base[:], float(P), None, ALU.mult))
            then(dve.tensor_tensor(rank[:], rank[:], total[:], ALU.add))
            then(dve.tensor_tensor(rank[:], rank[:], counts, ALU.subtract))
            then(dve.tensor_tensor(rank[:], rank[:], across(base[:]), ALU.add))
            for c, chosen in enumerate((pick0, pick1)):
                then(dve.tensor_tensor(spare[:], chosen[:], gate[:], ALU.mult))
                then(dve.tensor_reduce(choice_gate[:, c, :], spare[:], AX.X, ALU.add))
                then(dve.tensor_tensor(spare[:], chosen[:], rank[:], ALU.mult))
                then(dve.tensor_reduce(choice_slot[:, c, :], spare[:], AX.X, ALU.add))
            dve.tensor_copy(choice_row[:], choice_slot[:]).then_inc(slots_ready, 1)

            def x_low(n):
                dve.wait_ge(x_high, n + 1)
                low(xT[:, 1], bank[4][:].rearrange("p (k c) -> p k c", k=KD), xT[:, 0]).then_inc(x_split, 1)

            def hidden(n):
                dve.wait_ge(silu_done, n + 1)
                dve.tensor_tensor(hid[:], silu_g[:], bank[1][:, 0:EH], ALU.mult).then_inc(hid_ready, 1)

            def hid_low(n):
                dve.wait_ge(hidT_high, 2 * n + 2)
                for k, rws in ((slice(0, 2), P), (slice(2, 3), HW[2])):
                    low(hidT[0:rws, 1, k, :], bank[2][0:rws, k.start * P:k.stop * P].rearrange("p (k c) -> p k c", c=P),
                        hidT[0:rws, 0, k, :]).then_inc(hidT_split, 1)

            def take(n, tile, stage):
                row = resid[:, bass.ds(tile, 1), :].rearrange("p o d -> p (o d)")
                dve.wait_ge(y_ready, n + 1)
                dve.tensor_tensor(row, row, bank[3][:], ALU.add).then_inc(y_taken, 1)
                if stage == "combined":
                    dve.wait_ge(gathered, 32 * (tile + 1))
                    dve.wait_ge(y_taken, n + 1)
                    for c in range(2):
                        if c:
                            dve.wait_ge(combining, tile + 1)
                        dve.scalar_tensor_tensor(row, picked[:, bass.ds(tile % 2, 1), c, :].rearrange("p o d -> p (o d)"),
                                                 choice_gate[:, c, bass.ds(tile, 1)], row,
                                                 ALU.mult, ALU.add).then_inc(combined if c else combining, 1)

            def begin():
                x_low(0)
                hidden(0)
                x_low(1)

            def unit(n, slot, last_slot, stage, tile, last_stage, last_tile, opens=None, more=True):
                hid_low(n - 1)
                hidden(n)
                if more:
                    x_low(n + 1)
                if last_stage != "routed":
                    take(n - 1, last_tile, last_stage)

            def end(n):
                hid_low(n - 1)
                take(n - 1, TT - 1, "combined")

            units(dve, begin, unit, end)

        @block.tensor
        def _(pe):
            def head(h, j):
                pe.wait_ge(pack_split, 2 * h + 2)
                hold(pe, head_bias_taken, h - 1)
                raw, parts = pack_raw[:, j, :], pack[:, j]
                pe.matmul(bank[4 + 3 * j][:, 0:1], raw[:, O_UK:O_UK + KVC], uqb[:, bass.ds(h, 1)], start=True, stop=True)
                pe.matmul(bank[5 + j][:], uvb_wide[:, j, :], raw[:, O_WO:O_WO + D], start=True, stop=True).then_inc(head_bias, 1)
                hold(pe, fold_split, 2 * h - 2)
                for r in range(KQ):
                    op = mm3(pe, bank[2 * j][:, r * P:(r + 1) * P],
                             (parts[:, 0, r * P:(r + 1) * P], parts[:, 1, r * P:(r + 1) * P]),
                             (parts[:, 0, O_UK:O_UK + KVC], parts[:, 1, O_UK:O_UK + KVC]), True, True)
                op.then_inc(fold_product, 1)
                mm3(pe, bank[2 * j + 1][:], (parts[:, 0, O_UV:O_UV + KVC], parts[:, 1, O_UV:O_UV + KVC]),
                    (parts[:, 0, O_WO:O_WO + D], parts[:, 1, O_WO:O_WO + D]), True, True).then_inc(fold_product, 1)

            pe.wait_ge(ident_ready, 2)
            pe.wait_ge(const_loaded, 16 * 5)
            head(0, 0)
            head(1, 1)
            with pe.Fori(1, H // 2) as i:
                for j in range(2):
                    head(2 * i + j, j)

            pe.wait_ge(projw_split, 1)
            pe.wait_ge(fold_split, 2 * H)
            pe.wait_ge(head_bias_taken, H)
            n = 0
            for b in range(B):
                for t in range(QT):
                    n += 1
                    pe.wait_ge(norm1_ready, QT * b + t + 1)
                    if t >= 2:
                        pe.wait_ge(proj_split, n - 2)
                    for k in range(KD):
                        op = pe.transpose(bank[t % 2][:, k * P:(k + 1) * P], xn1[:, t, k * P:(k + 1) * P], ident[:])
                    op.then_inc(proj_product, 1)
                pe.wait_ge(proj_split, n)
                for m in range(1 + KQ):
                    n += 1
                    for k in range(KD):
                        op = mm3(pe, bank[2 + m][:], both(projw, k, slice(m * P, (m + 1) * P)), both(xnT1, k, ALL),
                                 k == 0, k == KD - 1)
                    op.then_inc(proj_product, 1)
                pe.wait_ge(proj_split, n - KQ)
                hold(pe, turned_high, b)
                hold(pe, turned_low, b)
                for part in range(2):
                    for t in range(QT):
                        c = b * S + t * P
                        op = pe.transpose(bank[6 + part][:, t * P:(t + 1) * P], f32(ckvT[:, part, c:c + P]), ident[:])
                    op.then_inc(turned, 1)

            pe.wait_ge(turned_high, B)
            pe.wait_ge(turned_low, B)

            def iteration(u, lap):
                tiles = lap * (QT * LAP)
                q, v = u + 2, u - 1
                b_s, b_v, b_q = (u + 1) // 2 % B, v // 2 % B, q // 2 % B
                if has(u + 1):
                    pe.wait_ge(att_split, split_no("Q", u + 1, 0, lap))
                for s in range(QT):
                    if has(u + 1):
                        n = QT * (u + 1) + s
                        hold(pe, exp_done, n - 1 + tiles)
                        mm3(pe, bank[s % 2][:], both(qT[:, (u + 1) % 2], slice(s * P, (s + 1) * P)),
                            both(ckvT, slice(b_s * S, (b_s + 1) * S)), True, True).then_inc(scores_ready, 1)
                    if has(u):
                        n = QT * u + s
                        pe.wait_ge(probs_ready, n + 1 + tiles)
                        if n >= 2:
                            pe.wait_ge(att_split, split_no("T", (n - 2) // QT, (n - 2) % QT, lap))
                        for k in range(QT):
                            op = pe.transpose(bank[2 + s % 2][:, k * P:(k + 1) * P], probs[:, s, k * P:(k + 1) * P], ident[:])
                        op.then_inc(att_product, 1)
                    if has(q) and s in (0, 2):
                        if s == 0:
                            if q:
                                pe.wait_ge(att_split, split_no("Q", q - 1, 0, lap))
                            pe.wait_ge(m_loaded, 32 * (q // LAP + 1 + lap))
                        for k in ((0, 1) if s == 0 else (2,)):
                            op = mm3(pe, bank[4][:], both(m_sb, q % 2, slice(k * P, (k + 1) * P)),
                                     both(cqT, k, slice(b_q * S, (b_q + 1) * S)), k == 0, k == KQ - 1)
                        if s == 2:
                            op.then_inc(att_product, 1)
                    if has(v):
                        if s == 0:
                            pe.wait_ge(att_split, split_no("T", v, QT - 1, lap))
                            if v:
                                pe.wait_ge(att_split, split_no("V", v - 1, 0, lap))
                        op = mm3(pe, bank[5][:], both(ckv[:, b_v], s, ALL), both(pT[:, v % 2], s, ALL), s == 0, s == QT - 1)
                        if s == QT - 1:
                            op.then_inc(att_product, 1)
                    if outs_of(u, s):
                        bb, i = outs_of(u, s)
                        m = QT * bb + i
                        pe.wait_ge(att_split, split_no("V", 2 * bb + 1, 0, lap))
                        pe.wait_ge(n_loaded, 32 * (bb // B + 1 + lap))
                        hold(pe, out_added, m - 1 + lap * (QT * LAP // 2))
                        slot = (bb // B + lap) % 2
                        for j in range(2):
                            op = mm3(pe, bank[6 + m % 2][:], both(mixT[:, bb % 2, j], slice(i * P, (i + 1) * P)),
                                     (n_sb[:, slot, 0, j, :], n_sb[:, slot, 1, j, :]), j == 0, j == 1)
                        op.then_inc(out_ready, 1)
            laps(pe, iteration)

            pe.wait_ge(out_added, QT * UNITS // 2)
            pe.wait_ge(mixw_high, 2)
            made = [0]

            def product(op):
                made[0] += 1
                op.then_inc(mix_product, 1)

            ends = {}

            def project3(b):
                pe.wait_ge(ctx_split, b + 1)
                if b:
                    pe.wait_ge(mix_split, ends["norm", b - 1, QT - 1])
                for i in range(2):
                    for k in range(KC):
                        op = mm3(pe, bank[4 + i][:], both(qkw, k, slice(i * P, (i + 1) * P)), both(ctxT, k, ALL),
                                 k == 0, k == KC - 1)
                    product(op)
                ends["project", b] = made[0]

            def scores3(b, s):
                n = QT * b + s
                if s == 0:
                    pe.wait_ge(mix_split, ends["project", b])
                hold(pe, exp3_done, n - 1)
                mm3(pe, bank[s % 2][:], both(qk3[:, 0], slice(s * P, (s + 1) * P)), both(qk3[:, 1], ALL), True, True).then_inc(scores3_ready, 1)

            def norm3(b, s):
                pe.wait_ge(norm3_ready, QT * b + s + 1)
                if s >= 2:
                    pe.wait_ge(mix_split, ends["norm", b, s - 2])
                for k in range(KD):
                    op = pe.transpose(bank[4 + s % 2][:, k * P:(k + 1) * P], xn3[:, s, k * P:(k + 1) * P], ident[:])
                product(op)
                ends["norm", b, s] = made[0]

            def turn3(b, s):
                pe.wait_ge(probs3_ready, QT * b + s + 1)
                if s >= 2:
                    pe.wait_ge(mix_split, ends["turn", b, s - 2])
                for k in range(QT):
                    op = pe.transpose(bank[2 + s % 2][:, k * P:(k + 1) * P], probs3[:, s, k * P:(k + 1) * P], ident[:])
                product(op)
                ends["turn", b, s] = made[0]

            def mix3(b, s):
                t = QT * b + s
                if s == 0:
                    pe.wait_ge(mix_split, ends["turn", b, QT - 1])
                hold(pe, mixed_added, t - 1)
                for k in range(QT):
                    op = mm3(pe, bank[6 + t % 2][:], both(xnT3[:, b % 2], k, slice(s * P, (s + 1) * P)),
                             both(pT3[:, b % 2], k, ALL), k == 0, k == QT - 1)
                op.then_inc(mixed_ready, 1)

            for b in range(B + 1):
                if b < B:
                    project3(b)
                for s in range(QT):
                    if b < B:
                        scores3(b, s)
                        norm3(b, s)
                    if b:
                        mix3(b - 1, s)
                if b < B:
                    for s in range(QT):
                        turn3(b, s)

            def logits(t):
                pe.wait_ge(ln4_split, t + 1)
                for k in range(KD):
                    op = mm3(pe, bank[2][:, t * E:(t + 1) * E], both(xT4[:, t % 2], k, ALL), both(routw, k, ALL),
                             k == 0, k == KD - 1)
                op.then_inc(logits_ready, 1)

            pe.wait_ge(mixed_added, TT)
            for t in range(TT):
                pe.wait_ge(norm4_ready, t + 1)
                hold(pe, ln4_split, t - 1)
                for k in range(KD):
                    op = pe.transpose(bank[t % 2][:, k * P:(k + 1) * P], xn4[:, t, k * P:(k + 1) * P], ident[:])
                op.then_inc(ln4_product, 1)
                if t == 0:
                    pe.wait_ge(rout_split, 1)
                if t:
                    logits(t - 1)
            logits(TT - 1)
            pe.wait_ge(gate_shift, 1)

            def turn_rows(n):
                pe.wait_ge(rows_loaded, 16 * n + 16)
                hold(pe, x_split, n)
                for k in range(KD):
                    op = pe.transpose(bank[4][:, k * P:(k + 1) * P], rows[:, k * P:(k + 1) * P], ident[:])
                op.then_inc(x_product, 1)

            def gate_up(n, slot):
                pe.wait_ge(x_split, n + 1)
                for half in range(2):
                    for k in range(KD):
                        o = k * 2 * EH + half * EH
                        op = mm3(pe, bank[half][:, 0:EH], both(xT, k, ALL), (ew[:, slot, 0, o:o + EH], ew[:, slot, 1, o:o + EH]),
                                 k == 0, k == KD - 1)
                op.then_inc(gu_ready, 1)

            def turn_hid(n):
                pe.wait_ge(hid_ready, n + 1)
                hold(pe, hidT_split, 2 * n)
                for k in range(KH):
                    op = pe.transpose(bank[2][0:HW[k], k * P:(k + 1) * P], hid[:, k * P:k * P + HW[k]], ident[:])
                op.then_inc(hidT_product, 1)

            def down(n, slot):
                pe.wait_ge(hidT_split, 2 * n + 2)
                hold(pe, y_taken, n)
                for k in range(KH):
                    o = KD * 2 * EH + k * D
                    rws = HW[k]
                    op = mm3(pe, bank[3][:], (hidT[0:rws, 0, k, :], hidT[0:rws, 1, k, :]),
                             (ew[0:rws, slot, 0, o:o + D], ew[0:rws, slot, 1, o:o + D]), k == 0, k == KH - 1)
                op.then_inc(y_ready, 1)

            def begin():
                turn_rows(0)
                pe.wait_ge(ew_split, 1)
                gate_up(0, 0)
                turn_rows(1)

            def unit(n, slot, last_slot, stage, tile, last_stage, last_tile, opens=None, more=True):
                turn_hid(n - 1)
                if opens is not None:
                    pe.wait_ge(ew_split, opens + 1)
                gate_up(n, slot)
                if more:
                    turn_rows(n + 1)
                down(n - 1, last_slot)

            def end(n):
                turn_hid(n - 1)
                down(n - 1, (NE - 1) % 2)

            pe.wait_ge(picks_ready, 1)
            pe.wait_ge(grids_ready, 2)
            pe.matmul(bank[5][:, 0:TT * E], tri[:], pick[:].rearrange("p t e -> p (t e)"), start=True, stop=True)
            pe.matmul(bank[5][:, TT * E:2 * TT * E], ones4[:], pick[:].rearrange("p t e -> p (t e)"), start=True,
                      stop=True).then_inc(ranks_ready, 1)
            units(pe, begin, unit, end)


def kernel(**inputs):
    import numpy as np
    import concourse.bacc as bacc
    from concourse.bass_utils import run_bass_kernel_spmd

    a = {k: np.asarray(v) for k, v in inputs.items()}
    g = {k[8:]: v for k, v in a.items() if k.startswith("L0_attn_")}
    f = {k[7:]: v for k, v in a.items() if k.startswith("L0_ffn_")}

    def tiles(w):
        return w.reshape(-1, P, w.shape[1]).transpose(1, 0, 2)

    def columns(v):
        return v.reshape(-1, P).T

    uq, uk, uv = (g[k].reshape(H, DH, -1) for k in ("W_UQ_w", "W_UK_w", "W_UV_w"))
    wo = g["W_O_w"].T.reshape(H, DH, D)
    shared = [np.concatenate([f["sg"][:, i * EH:(i + 1) * EH], f["su"][:, i * EH:(i + 1) * EH]], 1)[None] for i in range(NSH)]
    gu = np.concatenate([shared[0], np.concatenate([f["wg"], f["wu"]], 2), shared[1]], 0)
    data = {
        "x": a["x"].reshape(B * S, D),
        "proj_w": tiles(np.concatenate([g["W_DKV_w"], g["W_DQ_w"]], 0).T),
        "proj_b": columns(np.concatenate([g["W_DKV_b"], g["W_DQ_b"]])),
        "heads_w": np.concatenate([uq, uk, uv, wo], 2),
        "uq_b": columns(g["W_UQ_b"]),
        "uv_b": columns(g["W_UV_b"]),
        "o_b": g["W_O_b"],
        "ctx_t": tiles(a["ctx_1024"].reshape(B * S, C).T),
        "qk_w": tiles(np.concatenate([a["L0_xattn_Wq"], a["L0_xattn_Wk"]], 0).T),
        "qk_b": np.stack([a["L0_xattn_bq"], a["L0_xattn_bk"]], 1),
        "router_w": tiles(f["router_w"].T),
        "gate_up_w": gu.reshape(NE, KD, P, 2 * EH).transpose(0, 2, 1, 3).reshape(NE, P, KD * 2 * EH),
        "down_w": np.concatenate([f["sd"][None, :EH], f["wd"], f["sd"][None, EH:]], 0),
    }
    data = {k: np.ascontiguousarray(v) for k, v in data.items()}
    nc = bacc.Bacc("TRN2", target_bir_lowering=False, num_devices=1)
    args = [nc.dram_tensor(k, v.shape, mybir.dt.from_np(v.dtype), kind="ExternalInput").ap() for k, v in data.items()]
    out = nc.dram_tensor("out", [B * S, D], F32, kind="ExternalOutput").ap()
    decoder_kernel(nc, *args, out)
    r = run_bass_kernel_spmd(nc, [data], core_ids=[0])
    return r.results[0]["out"].reshape(B, S, D)
```

```python
from contextlib import ExitStack

import concourse.bass as bass
from concourse import mybir
from concourse.alu_op_type import AluOpType as ALU

ACT = mybir.ActivationFunctionType
AX = mybir.AxisListType
F32 = mybir.dt.float32
F32R = mybir.dt.float32r
U32 = mybir.dt.uint32
I32 = mybir.dt.int32

P = 128
B, S, D = 4, 512, 512
QT = S // P
TT = B * QT
KD = D // P
H, DH = 16, 128
KVC, QC = 128, 384
KQ = QC // P
C = 256
KC = C // P
E, EH, NSH = 8, 352, 2
NE = E + NSH
KH = 3
HW = [128, 128, EH - 256]
EW = KD * 2 * EH + KH * D
LEAST = 3
ROUTER_STEPS = 4
SLOT_TILES = 2 * TT + E * LEAST
LN_EPS = 1e-5
GATE_EPS = 1e-20
SCALE = float(DH) ** -0.5

PACK = QC + KVC + KVC + D
O_UQ, O_UK, O_UV, O_WO = 0, QC, QC + KVC, QC + 2 * KVC

UNITS = H * B
LAP = 2 * B
LAPS = UNITS // LAP
FILL = -(-SLOT_TILES // (LAPS - 1))
FOLDS = {3: ("N", 0), 4: ("M", 0), 5: ("M", 1), 6: ("N", 1)}


def decoder_kernel(nc, x, proj_w, proj_b, heads_w, uq_b, uv_b, o_b, ctx_t, qk_w, qk_b,
                   router_w, gate_up_w, down_w, out):
    xv = x.rearrange("(t p) d -> p t d", p=P)
    ov = out.rearrange("(t p) d -> p t d", p=P)
    sorted_dram = nc.dram_tensor("sorted_rows", [(LAPS - 1) * FILL * P, D], F32, kind="Internal").ap()
    routed_dram = sorted_dram

    with ExitStack() as life:
        def sb(name, shape, dt=F32, stack=life):
            return stack.enter_context(nc.sbuf_tensor(name, shape, dt))

        def sem(name):
            return life.enter_context(nc.semaphore(name))

        resid = sb("resid", [P, TT, D])
        ident = sb("ident", [P, P])
        zero_rows = sb("zero_rows", [P, D])
        stats = sb("stats", [P, 2, QT, 6])
        moments = sb("moments", [P, 2, QT, 2])
        rstd = sb("rstd", [P, 2, QT])
        vareps = sb("vareps", [P, 2, QT])
        neg_half = sb("neg_half", [P, QT])
        routw = sb("routw", [P, KD, E])
        negmax = sb("negmax", [P, 8])
        rowsum = sb("rowsum", [P, 8])
        rowinv = sb("rowinv", [P, 8])

        pack = sb("pack", [P, PACK])

        latents = ExitStack()
        ckvT = sb("ckvT", [P, 2, B * S], F32R, latents)
        ckv = sb("ckv", [P, B, 2, QT, KVC], F32R, latents)
        n_sb = sb("n_sb", [P, 2, 2, 2, D], F32R, latents)
        cqT = sb("cqT", [P, 2, KQ, B * S], F32R, latents)
        m_sb = sb("m_sb", [P, 2, 2, QC], F32R, latents)
        qb_now = sb("qb_now", [P, 2], F32, latents)
        uqb = sb("uqb", [P, H], F32, latents)
        uvb = sb("uvb", [P, H], F32, latents)
        ob_cols = sb("ob_cols", [P, KD], F32, latents)
        ob_wide = pack[:, 0:KD * P]
        ob_row = pack[:, KD * P:KD * P + D]

        early = ExitStack()
        projw_raw = sb("projw_raw", [P, KD, D], F32, early)
        projw = sb("projw", [P, 2, KD, D], F32R, early)
        projb = sb("projb", [P, 1 + KQ], F32, early)
        xnT1 = sb("xnT1", [P, 2, 2, KD, S], F32R, early)
        xn1 = sb("xn1", [P, QT, D], F32, early)
        early.close()

        mid = ExitStack()
        qT = sb("qT", [P, 2, 2, S], F32R, mid)
        probs = sb("probs", [P, QT, S], F32, mid)
        pT = sb("pT", [P, 2, 2, QT, S], F32R, mid)
        mixT = sb("mixT", [P, 2, 2, 2, S], F32R, mid)
        mid.close()
        latents.close()

        late = ExitStack()
        xn4 = sb("xn4", [P, TT, D], F32, late)
        xT4 = sb("xT4", [P, QT, KD, P], F32, late)
        xn3 = sb("xn3", [P, QT, D], F32, late)
        ctx_raw = sb("ctx_raw", [P, 2, KC, S], F32, late)
        ctxT = sb("ctxT", [P, 2, KC, S], F32R, late)
        qkw_raw = sb("qkw_raw", [P, KC, 2 * P], F32, late)
        qkw = sb("qkw", [P, 2, KC, 2 * P], F32R, late)
        qkb = sb("qkb", [P, 2], F32, late)
        qk3 = sb("qk3", [P, 2, 2, S], F32R, late)
        probs3 = sb("probs3", [P, QT, S], F32, late)
        pT3 = sb("pT3", [P, 2, 2, QT, S], F32R, late)
        xnT3 = sb("xnT3", [P, 2, 2, KD, S], F32R, late)
        late.close()

        last = ExitStack()
        last.enter_context(nc.sbuf_tensor("xn4_kept", [P, TT, D], F32))
        silu_g = sb("silu_g", [P, EH], F32, last)
        hid = sb("hid", [P, EH], F32, last)
        y_out = sb("y_out", [P, D], F32, last)
        xT = sb("xT", [P, 2, KD, P], F32R, last)
        rows = sb("rows", [P, D], F32, last)
        (logit, gate, pick, pick0, pick1, expert_no, tile_floor, rank, sum_a,
         sum_b) = (sb(f"grid{i}", [P, TT, E], F32, last) for i in range(10))
        ew_raw = sb("ew_raw", [P, EW], F32, last)
        ew = sb("ew", [P, 2, 2, EW], F32R, last)
        hidT = sb("hidT", [P, 2, KH, P], F32R, last)
        picked = sb("picked", [P, 2, 2, D], F32, last)
        grid_i = sb("grid_i", [P, 2, TT, E], I32, last)
        top = sb("top", [P, TT, 8], F32, last)
        topi = sb("topi", [P, TT, 8], U32, last)
        topf = sb("topf", [P, TT, 8], F32, last)
        col16 = sb("col16", [P, TT], F32, last)
        col16b = sb("col16b", [P, TT], F32, last)
        tiles_of = sb("tiles_of", [P, E], F32, last)
        ends_a = sb("ends_a", [P, E], F32, last)
        ends_b = sb("ends_b", [P, E], F32, last)
        first_f = sb("first_f", [P, E + 1], F32, last)
        first_i = sb("first_i", [P, E + 1], I32, last)
        base = sb("base", [P, E], F32, last)
        choice_gate = sb("choice_gate", [P, 2, TT], F32, last)
        choice_slot = sb("choice_slot", [P, 2, TT], F32, last)
        choice_row = sb("choice_row", [P, 2, TT], U32, last)
        tri = sb("tri", [P, P], F32, last)
        ones = sb("ones", [P, P], F32, last)
        last.close()

        bank = [life.enter_context(nc.psum_tensor(f"bank{i}", [P, D], F32)) for i in range(8)]

        def trio(stage):
            return sem(f"{stage}_product"), sem(f"{stage}_high"), sem(f"{stage}_split")

        projw_loaded = sem("projw_loaded")
        bias_loaded = sem("bias_loaded")
        x_loaded = [sem(f"x_loaded{b}") for b in range(B)]
        ident_zero = sem("ident_zero")
        ident_ready = sem("ident_ready")
        var_ready = sem("var_ready")
        rstd_ready = sem("rstd_ready")
        vec_step = sem("vec_step")

        pack_loaded = sem("pack_loaded")
        fold_product, fold_high, fold_split = trio("fold")
        projw_high = sem("projw_high")
        projw_split = sem("projw_split")
        norm1_ready = sem("norm1_ready")
        proj_product, proj_high, proj_split = trio("proj")
        ob_spread = sem("ob_spread")
        ob_product = sem("ob_product")
        ob_ready = sem("ob_ready")
        obias_added = sem("obias_added")
        turned = sem("turned")
        turned_high = sem("turned_high")
        turned_low = sem("turned_low")

        att_product, att_high, att_split = trio("att")
        scores_ready = sem("scores_ready")
        negmax_ready = sem("negmax_ready")
        exp_done = sem("exp_done")
        rowinv_ready = sem("rowinv_ready")
        probs_begun = sem("probs_begun")
        probs_ready = sem("probs_ready")
        out_ready = sem("out_ready")
        out_added = sem("out_added")

        mixw_loaded = sem("mixw_loaded")
        ctx_loaded = [sem("ctx_loaded0"), sem("ctx_loaded1")]
        mixw_high = sem("mixw_high")
        ctx_high = sem("ctx_high")
        ctx_split = sem("ctx_split")
        norm3_ready = sem("norm3_ready")
        mix_product, mix_high, mix_split = trio("mix")
        scores3_ready = sem("scores3_ready")
        negmax3_ready = sem("negmax3_ready")
        exp3_done = sem("exp3_done")
        rowinv3_ready = sem("rowinv3_ready")
        probs3_ready = sem("probs3_ready")
        mixed_ready = sem("mixed_ready")
        mixed_added = sem("mixed_added")

        rout_loaded = sem("rout_loaded")
        rows4_turned = sem("rows4_turned")
        rows4_taken = sem("rows4_taken")
        norm4_ready = sem("norm4_ready")
        logits_ready = sem("logits_ready")
        gate_shift = sem("gate_shift")
        gate_exp = sem("gate_exp")
        grids_ready = sem("grids_ready")
        picks_ready = sem("picks_ready")
        ranks_ready = sem("ranks_ready")
        slots_ready = sem("slots_ready")
        zero_ready = sem("zero_ready")
        zeroed = sem("zeroed")
        scattered = sem("scattered")
        ew_loaded = sem("ew_loaded")
        ew_high = sem("ew_high")
        ew_split = sem("ew_split")
        rows_loaded = sem("rows_loaded")
        x_product, x_high, x_split = trio("x")
        gu_ready = sem("gu_ready")
        silu_done = sem("silu_done")
        hid_ready = sem("hid_ready")
        hidT_product, hidT_high, hidT_split = trio("hidT")
        y_ready = sem("y_ready")
        y_taken = sem("y_taken")
        routed_stored = sem("routed_stored")
        results_stored = sem("results_stored")
        gathered = sem("gathered")
        combining = sem("combining")
        combined = sem("combined")
        stored = sem("stored")

        def mm3(pe, acc, lhs, rhs, first, final):
            pe.matmul(acc, lhs[1], rhs[0], start=first, stop=False)
            pe.matmul(acc, lhs[0], rhs[1], start=False, stop=False)
            return pe.matmul(acc, lhs[0], rhs[0], start=False, stop=final)

        def both(t, *index):
            return t[(slice(None), 0) + index], t[(slice(None), 1) + index]

        def f32(ap):
            return ap.bitcast(F32)

        ALL = slice(None)

        splits, count = {}, 0
        for u in range(-2, UNITS + 3):
            for s in range(QT):
                for kind, unit, here in (("T", u, True), ("Q", u + 2, s == 2),
                                         ("F", u, s == 3 and u < UNITS - LAP and u % LAP in FOLDS),
                                         ("V", u - 1, s == 3)):
                    if here and 0 <= unit < UNITS:
                        count += 1
                        splits[kind, unit, s if kind == "T" else 0] = count
        PER_LAP = LAP * (QT + 2) + len(FOLDS)
        assert splits["T", 2 * LAP, 0] - splits["T", LAP, 0] == PER_LAP

        def split_no(kind, unit, s, lap):
            return splits[kind, unit, s] + PER_LAP * lap

        def has(unit):
            return 0 <= unit < UNITS

        def fold_of(u):
            return FOLDS.get(u % LAP) if 0 <= u < UNITS - LAP else None

        def outs_of(u, s):
            if s % 2 == 0 or u < 3:
                return None
            bb, i = ((u - 3) // 2, s // 2) if u % 2 else ((u - 4) // 2, 2 + s // 2)
            return (bb, i) if 0 <= bb < UNITS // 2 else None

        def projections(rows_turned, latent, turned_latent, fold_first):
            for t in range(QT):
                rows_turned(0, t)
            for b in range(B):
                if b < 2:
                    fold_first(b)
                for m in range(1 + KQ):
                    latent(b, m)
                    if m >= 2 and b + 1 < B:
                        rows_turned(b + 1, m - 2)
                if b + 1 < B:
                    rows_turned(b + 1, 2)
                turned_latent(b)
                if b + 1 < B:
                    rows_turned(b + 1, 3)

        def none(*_):
            pass

        proj_no = {}
        projections(lambda b, t: proj_no.update({("rows", b, t): len(proj_no) + 1}),
                    lambda b, m: proj_no.update({("latent", b, m): len(proj_no) + 1}), none, none)

        def mixing(context, project, score, invert, turn, stats3, var3, center3, rows3, mix, add, var4, center4, rows4):
            context(1)
            invert(0, 0)
            invert(0, 1)
            for s in range(2, QT):
                score(0, s)
            for s in range(2, QT):
                invert(0, s)
            turn(0, 0)
            turn(0, 1)
            for s in range(QT):
                center3(0, s)
                if s < 2:
                    turn(0, 2 + s)
            for s in range(QT):
                rows3(0, s)
                stats3(1, s)
            var3(1)
            for b in range(B):
                ahead, behind = b + 1 < B, b > 0
                if ahead:
                    project(b + 1)
                    if b + 2 < B:
                        context(b + 2)
                    for s in range(0 if b == 0 else 2, QT):
                        center3(b + 1, s)
                for half in range(4):
                    mix(b, half // 2, half % 2)
                    if half % 2 == 0 and half:
                        add(b, half // 2 - 1)
                    if ahead:
                        rows3(b + 1, half)
                        if half:
                            invert(b + 1, half - 1)
                        score(b + 1, half)
                if ahead:
                    invert(b + 1, QT - 1)
                if behind:
                    for s in range(2):
                        center4(b - 1, s)
                for half in range(4):
                    mix(b, 2 + half // 2, half % 2)
                    if half % 2 == 0:
                        add(b, 1 + half // 2)
                    if behind:
                        rows4(b - 1, half)
                        if half < 2:
                            center4(b - 1, 2 + half)
                    if ahead:
                        turn(b + 1, half)
                    if b + 2 < B:
                        if half < 2:
                            stats3(b + 2, 2 * half)
                            stats3(b + 2, 2 * half + 1)
                        elif half == 2:
                            var3(b + 2)
                        else:
                            center3(b + 2, 0)
                            center3(b + 2, 1)
                add(b, QT - 1)
                var4(b)
            for s in range(QT):
                center4(B - 1, s)
            for s in range(QT):
                rows4(B - 1, s)

        mix_no = {}

        def count_mix(kind):
            return lambda *step: mix_no.update({(kind,) + step: len(mix_no) + 1})

        count_projects = lambda b: [count_mix("project")(b, i) for i in range(2)]
        count_projects(0)
        mixing(none, count_projects, none, none, count_mix("turn"), none, none,
               none, count_mix("rows3"), none, none, none, none, none)

        def rows4_bank(b, s):
            return bank[(4, 0, 1, 2)[s] if b == B - 1 else 4]

        def split_bank(n):
            return bank[2 + n % 2]

        def laps(eng, iteration, before):
            for u in range(-2, LAP):
                iteration(u, 0)
            with eng.Fori(0, UNITS // LAP - 2) as lap:
                for u in range(LAP, 2 * LAP):
                    iteration(u, lap)
            for u in range(UNITS - LAP, UNITS + 3):
                before.get(u, none)()
                iteration(u, 0)

        def hold(eng, s, value):
            if not isinstance(value, int) or value > 0:
                eng.wait_ge(s, value)

        def first_unit(eng, e, others=0):
            least = LEAST * e if isinstance(e, int) else LEAST
            return TT + eng.value_load(first_i[0:1, bass.ds(e, 1)], min_val=least, max_val=SLOT_TILES - LEAST * others)

        def units(eng, begin, unit, end, router):
            begin()
            for n in range(1, ROUTER_STEPS + 1):
                router.get(n, none)()
                unit(n, 0, 0, "shared", n, "shared", n - 1, split=1 if n == ROUTER_STEPS else None)
            with eng.Fori(ROUTER_STEPS + 1, TT) as n:
                unit(n, 0, 0, "shared", n, "shared", n - 1)
            eng.wait_ge(slots_ready, 1)

            def expert(e, before):
                start = first_unit(eng, e, others=1)
                unit(start, (e + 1) % 2, e % 2, "routed", None, before, TT - 1, opens=e + 1)
                stop = first_unit(eng, e + 1)
                unit(start + 1, (e + 1) % 2, (e + 1) % 2, "routed", None, "routed", None, split=e + 2)
                with eng.Fori(start + 2, stop) as n:
                    unit(n, (e + 1) % 2, (e + 1) % 2, "routed", None, "routed", None)

            expert(0, "shared")
            with eng.Fori(1, E) as e:
                expert(e, "routed")
            start = first_unit(eng, E)
            unit(start, (NE - 1) % 2, NE % 2, "combined", 0, "routed", None, opens=NE - 1)
            with eng.Fori(1, TT - 1) as t:
                unit(start + t, (NE - 1) % 2, (NE - 1) % 2, "combined", t, "combined", t - 1)
            unit(start + (TT - 1), (NE - 1) % 2, (NE - 1) % 2, "combined", TT - 1, "combined", TT - 2, more=False)
            end(start + TT)

        PIECES = ((P, 0, KD * EH), (P, KD * EH, 2 * KD * EH), (P, 2 * KD * EH, EW - D), (HW[KH - 1], EW - D, EW))

        def low_pieces(pos, engine):
            mine = 2 if isinstance(pos, int) and pos == 0 else 1
            return PIECES[:mine] if engine == "vector" else PIECES[mine:]

        block = life.enter_context(nc.Block())

        @block.sync
        def _(sp):
            def load_x(b):
                sp.dma_start(resid[:, QT * b:QT * (b + 1), :], xv[:, QT * b:QT * (b + 1), :]).then_inc(x_loaded[b], 16)

            def load_head(h):
                sp.dma_start(pack[:], heads_w[h]).then_inc(pack_loaded, 16)

            load_x(0)
            for dst, src in ((projb, proj_b), (uqb, uq_b), (uvb, uv_b), (ob_cols, o_b)):
                sp.dma_start(dst[:], src).then_inc(bias_loaded, 16)
            load_head(0)
            for b in range(1, B):
                load_x(b)
            sp.wait_ge(fold_product, 2)
            load_head(1)
            sp.wait_ge(fold_product, 4)
            load_head(2)
            sp.wait_ge(zero_ready, 1)

            def lap(pair, another=True):
                sp.wait_ge(att_product, splits["F", 4, 0] + PER_LAP * (pair - 1))
                load_head(2 * pair + 1)
                with sp.Fori((pair - 1) * FILL, (pair - 1) * FILL + FILL) as i:
                    sp.dma_start(sorted_dram[bass.ds(i * P, P), :], zero_rows[:]).then_inc(zeroed, 16)
                if another:
                    sp.wait_ge(att_product, splits["F", 6, 0] + PER_LAP * (pair - 1))
                    load_head(2 * pair + 2)

            with sp.Fori(1, LAPS - 1) as pair:
                lap(pair)
            lap(LAPS - 1, another=False)

            sp.wait_ge(att_product, splits["Q", UNITS - 1, 0])
            sp.dma_start(qkw_raw[:], qk_w).then_inc(mixw_loaded, 16)
            sp.dma_start(qkb[:], qk_b).then_inc(mixw_loaded, 16)
            sp.dma_start(routw[:], router_w).then_inc(rout_loaded, 16)
            for b in range(B):
                if b >= 2:
                    sp.wait_ge(ctx_split, b - 1)
                sp.dma_start(ctx_raw[:, b % 2, :, :], ctx_t[:, :, b * S:(b + 1) * S]).then_inc(ctx_loaded[b % 2], 16)

            def load_rows(n, src):
                hold(sp, x_product, n)
                sp.dma_start(rows[:], src).then_inc(rows_loaded, 16)

            def sorted_rows(n):
                return sorted_dram[bass.ds((n - TT) * P, P), :]

            sp.wait_ge(norm4_ready, TT)
            load_rows(0, xn4[:, 0, :])
            with sp.Fori(1, TT) as n:
                load_rows(n, xn4[:, bass.ds(n, 1), :].rearrange("p o d -> p (o d)"))
            sp.wait_ge(slots_ready, 1)
            sp.wait_ge(scattered, 16 * 2 * TT)
            stop = first_unit(sp, E)
            load_rows(TT, sorted_dram[0:P, :])
            with sp.Fori(TT + 1, stop) as n:
                load_rows(n, sorted_rows(n))
            load_rows(stop, xn4[:, 0, :])

            with sp.Fori(1, TT) as t:
                load_rows(stop + t, xn4[:, bass.ds(t, 1), :].rearrange("p o d -> p (o d)"))
            sp.wait_ge(stored, 16 * TT)

        @block.gpsimd
        def _(pool):
            norms = [0]

            def inverse_std(which=0):
                norms[0] += 1
                pool.wait_ge(var_ready, norms[0])
                pool.tensor_tensor(rstd[:, which], vareps[:, which], neg_half[:], ALU.pow).then_inc(rstd_ready, 1)

            pool.memset(zero_rows[:], 0.0).then_inc(zero_ready, 1)
            pool.memset(neg_half[:], -0.5)
            pool.memset(ident[:], 0.0).then_inc(ident_zero, 1)
            pool.wait_ge(ident_zero, 1)
            pool.affine_select(out=ident[:], in_=ident[:], compare_op=ALU.not_equal, fill=1.0, base=0,
                               pattern=[[-1, P]], channel_multiplier=1).then_inc(ident_ready, 1)
            for b in range(B):
                inverse_std()

            def iteration(u, lap):
                for s in range(QT):
                    if has(u + 1):
                        n = QT * (u + 1) + s
                        pool.wait_ge(rowinv_ready, n + 1 + lap * (QT * LAP))
                        pool.sem_inc(probs_begun, 1)
                        pool.tensor_scalar(probs[:, s, :], probs[:, s, :], rowinv[:, n % 8:n % 8 + 1], None,
                                           ALU.mult).then_inc(probs_ready, 1)
                    if outs_of(u, s) and outs_of(u, s)[0] >= (LAPS - 1) * B and u >= UNITS - LAP:
                        bb, i = outs_of(u, s)
                        t = QT * (bb % B) + i
                        pool.wait_ge(ob_ready, 1)
                        pool.wait_ge(out_added, QT * bb + i + 1)
                        pool.tensor_tensor(resid[:, t, :], resid[:, t, :], ob_row, ALU.add).then_inc(obias_added, 1)
            def load_expert(pos):
                hold(pool, ew_split, 2 * pos)
                pool.dma_start(ew_raw[:, 0:KD * 2 * EH], gate_up_w[pos]).then_inc(ew_loaded, 16)
                for k in range(KH):
                    o = KD * 2 * EH + k * D
                    pool.dma_start(ew_raw[0:HW[k], o:o + D], down_w[pos, k * P:k * P + HW[k], :]).then_inc(ew_loaded, 16)

            def ctx_low(b):
                pool.wait_ge(ctx_high, b + 1)
                pool.tensor_tensor(ctxT[:, 1, :, :], ctx_raw[:, b % 2, :, :], f32(ctxT[:, 0, :, :]),
                                   ALU.subtract).then_inc(ctx_split, 1)

            def var4_pool(b):
                inverse_std(1)
                if b == B - 2:
                    pool.wait_ge(mixed_added, TT - QT)
                    load_expert(0)

            laps(pool, iteration, {UNITS: lambda: ctx_low(0), UNITS + 2: lambda: inverse_std(0)})


            def expert_low(pos):
                pool.wait_ge(ew_high, 4 * pos + 4)
                for rws, c0, c1 in low_pieces(pos, "pool"):
                    op = pool.tensor_tensor(ew[0:rws, pos % 2, 1, c0:c1], ew_raw[0:rws, c0:c1],
                                            f32(ew[0:rws, pos % 2, 0, c0:c1]), ALU.subtract)
                op.then_inc(ew_split, 1)

            mixing(ctx_low, none, none, none, none, none, lambda b: inverse_std(0), none, none, none, none, var4_pool,
                   none, none)
            pool.wait_ge(mixed_added, TT)
            pool.iota(grid_i[:, 0], pattern=[[0, TT], [1, E]], base=0, channel_multiplier=0)
            pool.iota(grid_i[:, 1], pattern=[[P, TT], [0, E]], base=0, channel_multiplier=0)
            pool.memset(ones[:], 1.0).then_inc(grids_ready, 1)
            pool.wait_ge(grids_ready, 1)
            pool.affine_select(out=tri[:], in_=ones[:], compare_op=ALU.is_gt, fill=0.0, base=0,
                               pattern=[[1, P]], channel_multiplier=-1).then_inc(grids_ready, 1)
            expert_low(0)
            load_expert(1)

            pool.wait_ge(slots_ready, 1)
            pool.wait_ge(zeroed, 16 * FILL * (LAPS - 1))
            pool.wait_ge(norm4_ready, TT)
            for t in range(TT):
                for c in range(2):
                    pool.indirect_dma_start(sorted_dram, bass.IndirectOffsetOnAxis(ap=choice_row[:, c, t:t + 1], axis=0),
                                            xn4[:, t, :], None).then_inc(scattered, 16)
            expert_low(1)
            with pool.Fori(2, NE) as pos:
                load_expert(pos)
                expert_low(pos)

            stop = first_unit(pool, E)
            pool.wait_ge(routed_stored, (stop - TT + 1) * 16)
            pool.sem_inc(results_stored, 1)
            def store_out(t):
                pool.wait_ge(combined, t + 1)
                pool.dma_start(ov[:, t, :], resid[:, t, :]).then_inc(stored, 16)

            for t in range(TT):
                if t >= 2:
                    store_out(t - 2)
                for c in range(2):
                    pool.indirect_dma_start(picked[:, t % 2, c, :], None, routed_dram,
                                            bass.IndirectOffsetOnAxis(ap=choice_row[:, c, t:t + 1], axis=0)).then_inc(gathered, 16)
                pool.wait_ge(gathered, 32 * (t + 1))
            store_out(TT - 2)
            store_out(TT - 1)

        @block.scalar
        def _(act):
            def copy(dst, src, scale=1.0):
                return act.activation(dst, src, ACT.Copy, scale=scale)

            def fold_high_part(kind, j, slot, src):
                if kind == "M":
                    return copy(m_sb[:, 0, j, :], src[:, 0:QC], SCALE)
                return copy(n_sb[:, slot, 0, j, :], src[:])

            act.dma_start(projw_raw[:], proj_w).then_inc(projw_loaded, 16)
            act.wait_ge(projw_loaded, 16)
            copy(projw[:, 0, :, :], projw_raw[:]).then_inc(projw_high, 1)

            def rows_high(b, t):
                act.wait_ge(proj_product, proj_no["rows", b, t])
                copy(xnT1[:, b % 2, 0, :, t * P:(t + 1) * P],
                     bank[t % 2][:].rearrange("p (k c) -> p k c", k=KD)).then_inc(proj_high, 1)

            def latent_high(b, m):
                cols = slice(b * S, (b + 1) * S)
                act.wait_ge(proj_product, proj_no["latent", b, m])
                dst = ckvT[:, 0, cols] if m == 0 else cqT[:, 0, m - 1, cols]
                act.activation(dst, bank[2 + m][:], ACT.Identity, bias=projb[:, m:m + 1]).then_inc(proj_high, 1)

            def turned_part(b):
                act.wait_ge(turned, 2 * b + 1)
                copy(ckv[:, b, 0, :, :], bank[6][:].rearrange("p (k c) -> p k c", k=QT)).then_inc(turned_high, 1)

            def fold_first(j):
                for i, kind in enumerate("MN"):
                    act.wait_ge(fold_product, 2 * j + i + 1)
                    fold_high_part(kind, j, 0, bank[6 + i]).then_inc(fold_high, 1)

            act.wait_ge(bias_loaded, 16 * 4)
            projections(rows_high, latent_high, turned_part, fold_first)

            def iteration(u, lap):
                tiles = lap * (QT * LAP)
                for s in range(QT):
                    if has(u):
                        act.wait_ge(att_product, split_no("T", u, s, lap))
                        copy(pT[:, u % 2, 0, :, s * P:(s + 1) * P],
                             bank[2 + s % 2][:].rearrange("p (k c) -> p k c", k=QT)).then_inc(att_high, 1)
                    if has(u + 1):
                        n = QT * (u + 1) + s
                        act.wait_ge(negmax_ready, n + 1 + tiles)
                        act.activation(probs[:, s, :], bank[s % 2][:], ACT.Exp, bias=negmax[:, n % 8:n % 8 + 1],
                                       accum_out=rowsum[:, n % 8:n % 8 + 1]).then_inc(exp_done, 1)
                    if s == 2 and has(u + 2):
                        q = u + 2
                        act.wait_ge(att_product, split_no("Q", q, 0, lap))
                        act.activation(qT[:, q % 2, 0, :], bank[4][:], ACT.Identity,
                                       bias=qb_now[:, q % 2:q % 2 + 1]).then_inc(att_high, 1)
                    if s == 3 and fold_of(u):
                        kind, j = fold_of(u)
                        act.wait_ge(att_product, split_no("F", u, 0, lap))
                        fold_high_part(kind, j, (u // LAP + lap + 1) % 2, bank[4]).then_inc(att_high, 1)
                    if s == 3 and has(u - 1):
                        v = u - 1
                        act.wait_ge(att_product, split_no("V", v, 0, lap))
                        copy(mixT[:, v // 2 % 2, v % 2, 0, :], bank[5][:]).then_inc(att_high, 1)
            act.wait_ge(proj_split, B * (QT + 1 + KQ))
            def expert_high(pos, pieces=PIECES):
                act.wait_ge(ew_loaded, 64 * pos + 64)
                for rws, c0, c1 in pieces:
                    copy(ew[0:rws, pos % 2, 0, c0:c1], ew_raw[0:rws, c0:c1]).then_inc(ew_high, 1)

            def mixing_weights():
                act.wait_ge(mixw_loaded, 32)
                copy(qkw[:, 0, :, :], qkw_raw[:]).then_inc(mixw_high, 1)
                ctx_part(0)

            def high(dst, n, bias=None, k=KD):
                act.wait_ge(mix_product, n)
                src = split_bank(n)[:]
                if bias is None:
                    copy(dst, src.rearrange("p (k c) -> p k c", k=k)).then_inc(mix_high, 1)
                else:
                    act.activation(dst, src, ACT.Identity, bias=bias).then_inc(mix_high, 1)

            def ctx_part(b):
                act.wait_ge(ctx_loaded[b % 2], 16 * (b // 2 + 1))
                if b:
                    act.wait_ge(mix_product, mix_no["project", b - 1, 1])
                copy(ctxT[:, 0, :, :], ctx_raw[:, b % 2, :, :]).then_inc(ctx_high, 1)

            def project_part(b):
                for i in range(2):
                    high(qk3[:, i, 0, :], mix_no["project", b, i], qkb[:, i:i + 1])

            def exp_tile(b, s):
                n = QT * b + s
                act.wait_ge(negmax3_ready, n + 1)
                act.activation(probs3[:, s, :], bank[s % 2][:], ACT.Exp, bias=negmax[:, n % 8:n % 8 + 1],
                               accum_out=rowsum[:, n % 8:n % 8 + 1]).then_inc(exp3_done, 1)

            def turn_part(b, s):
                high(pT3[:, b % 2, 0, :, s * P:(s + 1) * P], mix_no["turn", b, s], k=QT)

            def rows3_part(b, s):
                high(xnT3[:, b % 2, 0, :, s * P:(s + 1) * P], mix_no["rows3", b, s])

            def rows4_part(b, s):
                act.wait_ge(rows4_turned, QT * b + s + 1)
                copy(xT4[:, s], rows4_bank(b, s)[:].rearrange("p (k c) -> p k c", k=KD)).then_inc(rows4_taken, 1)

            def scale_probs(b, s):
                act.wait_ge(rowinv3_ready, QT * b + s + 1)
                n = QT * b + s
                copy(probs3[:, s, :], probs3[:, s, :], rowinv[:, n % 8:n % 8 + 1]).then_inc(probs3_ready, 1)

            def var4_act(b):
                if b == B - 1:
                    expert_high(0)

            def first_scores():
                exp_tile(0, 0)
                exp_tile(0, 1)

            laps(act, iteration, {UNITS: mixing_weights, UNITS + 1: lambda: project_part(0), UNITS + 2: first_scores})


            mixing(ctx_part, project_part, exp_tile, scale_probs, turn_part, none, none, none, rows3_part, none, none, var4_act,
                   none, rows4_part)

            def x_part(n):
                act.wait_ge(x_product, n + 1)
                copy(xT[:, 0], bank[4][:].rearrange("p (k c) -> p k c", k=KD)).then_inc(x_high, 1)

            def silu(n):
                act.wait_ge(gu_ready, n + 1)
                act.activation(silu_g[:], bank[0][:, 0:EH], ACT.Silu).then_inc(silu_done, 1)

            def hid_part(n):
                act.wait_ge(hidT_product, n + 1)
                for k, rws in ((slice(0, 2), P), (slice(2, 3), HW[2])):
                    copy(hidT[0:rws, 0, k, :],
                         bank[2][0:rws, k.start * P:k.stop * P].rearrange("p (k c) -> p k c", c=P)).then_inc(hidT_high, 1)

            def take_routed(n):
                act.wait_ge(y_ready, n + 1)
                act.wait_ge(routed_stored, (n - TT + 1) * 16)
                copy(y_out[:], bank[3][:]).then_inc(y_taken, 1)
                act.wait_ge(y_taken, n + 1)
                act.dma_start(routed_dram[bass.ds((n - TT) * P, P), :], y_out[:]).then_inc(routed_stored, 16)

            def begin():
                x_part(0)
                act.wait_ge(gate_shift, 1)
                act.activation(gate[:], gate[:], ACT.Exp).then_inc(gate_exp, 1)
                silu(0)
                x_part(1)

            def unit(n, slot, last_slot, stage, tile, last_stage, last_tile, opens=None, split=None, more=True):
                hid_part(n - 1)
                if split is not None:
                    act.wait_ge(y_ready, n - 1)
                    expert_high(split, PIECES[:3])
                silu(n)
                if more:
                    x_part(n + 1)
                if last_stage == "routed":
                    take_routed(n - 1)
                if split is not None:
                    expert_high(split, PIECES[3:])

            def end(n):
                hid_part(n - 1)

            act.sem_inc(routed_stored, 16)
            units(act, begin, unit, end, {})

        @block.vector
        def _(dve):
            step, norms = [0], [0]

            def own(op):
                step[0] += 1
                op.then_inc(vec_step, 1)
                return step[0]

            def row_stats(b, s, which=0):
                return dve.bn_stats(stats[:, which, s, :], resid[:, QT * b + s, :])

            def variance(which=0):
                for s in range(QT):
                    n = own(dve.bn_aggr(moments[:, which, s, :], stats[:, which, s, :]))
                dve.wait_ge(vec_step, n)
                dve.tensor_scalar(vareps[:, which], moments[:, which, :, 1], LN_EPS, None, ALU.add).then_inc(var_ready, 1)
                norms[0] += 1
                return norms[0]

            def center(xn, b, s, norm, which=0):
                dve.wait_ge(rstd_ready, norm)
                return dve.tensor_scalar(xn, resid[:, QT * b + s, :], moments[:, which, s, 0:1], rstd[:, which, s:s + 1],
                                         ALU.subtract, ALU.mult)

            def normalize(xn, b, ready, tiles_free, tiles_free_value):
                for s in range(QT):
                    n = own(row_stats(b, s))
                dve.wait_ge(vec_step, n)
                norm = variance()
                hold(dve, tiles_free, tiles_free_value)
                for s in range(QT):
                    center(xn[:, s, :], b, s, norm).then_inc(ready, 1)

            def low(dst, src, hi, scale=1.0):
                return dve.scalar_tensor_tensor(dst, src, scale, f32(hi), ALU.mult, ALU.subtract)

            def low_bias(dst, src, bias, hi):
                return dve.scalar_tensor_tensor(dst, src, bias, f32(hi), ALU.add, ALU.subtract)

            def fold_low_part(kind, h, j, slot, src):
                if kind == "M":
                    dve.tensor_scalar(qb_now[:, j:j + 1], src[:, QC:QC + 1], SCALE, None, ALU.mult)
                    dve.tensor_tensor(ob_cols[:], ob_cols[:], src[:, QC + 1:QC + 1 + KD], ALU.add)
                    return low(m_sb[:, 1, j, :], src[:, 0:QC], m_sb[:, 0, j, :], SCALE)
                return low(n_sb[:, slot, 1, j, :], src[:], n_sb[:, slot, 0, j, :])

            def rows_low(b, t):
                dve.wait_ge(proj_high, proj_no["rows", b, t])
                low(xnT1[:, b % 2, 1, :, t * P:(t + 1) * P], bank[t % 2][:].rearrange("p (k c) -> p k c", k=KD),
                    xnT1[:, b % 2, 0, :, t * P:(t + 1) * P]).then_inc(proj_split, 1)
                if t == QT - 1 and b + 1 < B:
                    dve.wait_ge(x_loaded[b + 1], 16)
                    normalize(xn1, b + 1, norm1_ready, proj_product, proj_no["rows", b, QT - 1])

            def latent_low(b, m):
                cols = slice(b * S, (b + 1) * S)
                dve.wait_ge(proj_high, proj_no["latent", b, m])
                hi, lo = (ckvT[:, i, cols] if m == 0 else cqT[:, i, m - 1, cols] for i in range(2))
                low_bias(lo, bank[2 + m][:], projb[:, m:m + 1], hi).then_inc(proj_split, 1)

            def turned_part(b):
                dve.wait_ge(turned, 2 * b + 2)
                dve.tensor_copy(ckv[:, b, 1, :, :], bank[7][:].rearrange("p (k c) -> p k c", k=QT)).then_inc(turned_low, 1)

            def fold_first(j):
                for i, kind in enumerate("MN"):
                    dve.wait_ge(fold_high, 2 * j + i + 1)
                    fold_low_part(kind, j, j, 0, bank[6 + i]).then_inc(fold_split, 1)

            dve.wait_ge(x_loaded[0], 16)
            normalize(xn1, 0, norm1_ready, proj_product, 0)
            dve.wait_ge(bias_loaded, 16 * 4)
            dve.wait_ge(projw_high, 1)
            low(projw[:, 1, :, :], projw_raw[:], projw[:, 0, :, :]).then_inc(projw_split, 1)
            projections(rows_low, latent_low, turned_part, fold_first)

            def invert(n, lap):
                dve.wait_ge(exp_done, n + 1 + lap * (QT * LAP))
                dve.reciprocal(rowinv[:, n % 8:n % 8 + 1], rowsum[:, n % 8:n % 8 + 1]).then_inc(rowinv_ready, 1)

            def iteration(u, lap):
                tiles = lap * (QT * LAP)
                q, v = u + 2, u - 1
                for s in range(QT):
                    n = QT * (u + 1) + s
                    if has((n - 1) // QT):
                        invert(n - 1, lap)
                    if has(u + 1):
                        dve.wait_ge(scores_ready, n + 1 + tiles)
                        dve.tensor_reduce(negmax[:, n % 8:n % 8 + 1], bank[s % 2][:], AX.X, ALU.max,
                                          negate=True).then_inc(negmax_ready, 1)
                    if has(u):
                        dve.wait_ge(att_high, split_no("T", u, s, lap))
                        low(pT[:, u % 2, 1, :, s * P:(s + 1) * P], bank[2 + s % 2][:].rearrange("p (k c) -> p k c", k=QT),
                            pT[:, u % 2, 0, :, s * P:(s + 1) * P]).then_inc(att_split, 1)
                    if s == 2 and has(q):
                        dve.wait_ge(att_high, split_no("Q", q, 0, lap))
                        low_bias(qT[:, q % 2, 1, :], bank[4][:], qb_now[:, q % 2:q % 2 + 1], qT[:, q % 2, 0, :]).then_inc(att_split, 1)
                    if s == 3 and fold_of(u):
                        kind, j = fold_of(u)
                        dve.wait_ge(att_high, split_no("F", u, 0, lap))
                        fold_low_part(kind, None, j, (u // LAP + lap + 1) % 2, bank[4]).then_inc(att_split, 1)
                    if s == 1 and u == UNITS - LAP:
                        dve.wait_ge(att_split, split_no("F", u - 2, 0, 0))
                        for k in range(KD):
                            op = dve.tensor_copy(ob_wide[:, k * P:(k + 1) * P], ob_cols[:, k:k + 1].to_broadcast([P, P]))
                        op.then_inc(ob_spread, 1)
                    if s == 3 and u == UNITS - LAP:
                        dve.wait_ge(ob_product, 1)
                        dve.tensor_copy(ob_row, bank[4][:]).then_inc(ob_ready, 1)
                    if outs_of(u, s):
                        bb, i = outs_of(u, s)
                        m = QT * bb + i
                        t = QT * (bb % B) + i
                        dve.wait_ge(out_ready, m + 1 + lap * (QT * LAP // 2))
                        dve.tensor_tensor(resid[:, t, :], resid[:, t, :], bank[6 + m % 2][:], ALU.add).then_inc(out_added, 1)
                    if s == 3 and has(v):
                        dve.wait_ge(att_high, split_no("V", v, 0, lap))
                        low(mixT[:, v // 2 % 2, v % 2, 1, :], bank[5][:], mixT[:, v // 2 % 2, v % 2, 0, :]).then_inc(att_split, 1)
            def mixing_weights():
                dve.wait_ge(mixw_high, 1)
                low(qkw[:, 1, :, :], qkw_raw[:], qkw[:, 0, :, :]).then_inc(mixw_high, 1)

            stats_step, norm_of = {}, {}

            def split(dst, hi, n, bias=None, k=KD):
                dve.wait_ge(mix_high, n)
                src = split_bank(n)[:]
                if bias is None:
                    low(dst, src.rearrange("p (k c) -> p k c", k=k), hi).then_inc(mix_split, 1)
                else:
                    low_bias(dst, src, bias, hi).then_inc(mix_split, 1)

            def project_low(b):
                for i in range(2):
                    split(qk3[:, i, 1, :], qk3[:, i, 0, :], mix_no["project", b, i], qkb[:, i:i + 1])

            def score_max(b, s):
                n = QT * b + s
                dve.wait_ge(scores3_ready, n + 1)
                dve.tensor_reduce(negmax[:, n % 8:n % 8 + 1], bank[s % 2][:], AX.X, ALU.max,
                                  negate=True).then_inc(negmax3_ready, 1)

            def invert3(b, s):
                n = QT * b + s
                dve.wait_ge(exp3_done, n + 1)
                dve.reciprocal(rowinv[:, n % 8:n % 8 + 1], rowsum[:, n % 8:n % 8 + 1]).then_inc(rowinv3_ready, 1)

            def part_low(t, b, s, n, k=KD):
                part = (slice(None), slice(s * P, (s + 1) * P))
                split(t[(ALL, b % 2, 1) + part], t[(ALL, b % 2, 0) + part], n, k=k)

            def turn_low(b, s):
                part_low(pT3, b, s, mix_no["turn", b, s], QT)

            def rows3_low(b, s):
                part_low(xnT3, b, s, mix_no["rows3", b, s])

            def stats3(b, s):
                dve.wait_ge(obias_added, QT * b + s + 1)
                stats_step["3", b] = own(row_stats(b, s))

            def var3(b):
                dve.wait_ge(vec_step, stats_step["3", b])
                norm_of["3", b] = variance()

            def center3(b, s):
                if b:
                    dve.wait_ge(mix_product, mix_no["rows3", b - 1, s])
                center(xn3[:, s, :], b, s, norm_of["3", b]).then_inc(norm3_ready, 1)

            def add(b, s):
                t = QT * b + s
                dve.wait_ge(mixed_ready, t + 1)
                dve.tensor_tensor(resid[:, t, :], resid[:, t, :], bank[6 + t % 2][:], ALU.add).then_inc(mixed_added, 1)
                dve.wait_ge(mixed_added, t + 1)
                stats_step["4", b] = own(row_stats(b, s, 1))

            def var4(b):
                dve.wait_ge(vec_step, stats_step["4", b])
                norm_of["4", b] = variance(1)

            def center4(b, s):
                center(xn4[:, QT * b + s, :], b, s, norm_of["4", b], 1).then_inc(norm4_ready, 1)

            def first_scores():
                score_max(0, 0)
                score_max(0, 1)
                for s in range(QT):
                    stats3(0, s)
                var3(0)

            laps(dve, iteration, {UNITS: mixing_weights, UNITS + 1: lambda: project_low(0), UNITS + 2: first_scores})


            mixing(none, project_low, score_max, invert3, turn_low, stats3, var3, center3, rows3_low, none, add, var4,
                   center4, none)

            def expert_low(pos):
                dve.wait_ge(ew_high, 4 * pos + len(low_pieces(pos, "vector")))
                for rws, c0, c1 in low_pieces(pos, "vector"):
                    op = dve.tensor_tensor(ew[0:rws, pos % 2, 1, c0:c1], ew_raw[0:rws, c0:c1],
                                           f32(ew[0:rws, pos % 2, 0, c0:c1]), ALU.subtract)
                op.then_inc(ew_split, 1)

            def wide(col):
                return col.unsqueeze(2).to_broadcast([P, TT, E])

            def across(row):
                return row.unsqueeze(1).to_broadcast([P, TT, E])

            def then(op):
                dve.wait_ge(vec_step, own(op))

            dve.wait_ge(grids_ready, 2)
            then(dve.tensor_copy(expert_no[:], grid_i[:, 0]))
            then(dve.tensor_copy(tile_floor[:], grid_i[:, 1]))
            expert_low(0)

            def gates():
                dve.wait_ge(logits_ready, TT)
                then(dve.tensor_copy(logit[:], bank[5][:, 0:TT * E].rearrange("p (t e) -> p t e", e=E)))
                then(dve.tensor_reduce(col16[:], logit[:], AX.X, ALU.max))
                dve.tensor_tensor(gate[:], logit[:], wide(col16[:]), ALU.subtract).then_inc(gate_shift, 1)
                dve.wait_ge(gate_exp, 1)
                then(dve.tensor_reduce(col16[:], gate[:], AX.X, ALU.add))
                then(dve.reciprocal(col16b[:], col16[:]))
                then(dve.tensor_tensor(gate[:], gate[:], wide(col16b[:]), ALU.mult))

            def pick_experts():
                for t in range(TT):
                    n = own(dve.max(top[:, t, :], gate[:, t, :]))
                dve.wait_ge(vec_step, n)
                for t in range(TT):
                    n = own(dve.max_index(topi[:, t, :], top[:, t, :], gate[:, t, :]))
                dve.wait_ge(vec_step, n)
                then(dve.tensor_copy(topf[:], topi[:]))
                dve.tensor_tensor(pick0[:], expert_no[:], wide(topf[:, :, 0]), ALU.is_equal)
                then(dve.tensor_tensor(pick1[:], expert_no[:], wide(topf[:, :, 1]), ALU.is_equal))
                dve.tensor_tensor(pick[:], pick0[:], pick1[:], ALU.add).then_inc(picks_ready, 1)
                dve.wait_ge(picks_ready, 1)

            def normalize_gates():
                then(dve.tensor_tensor(gate[:], gate[:], pick[:], ALU.mult))
                then(dve.tensor_reduce(col16[:], gate[:], AX.X, ALU.add))
                then(dve.tensor_scalar(col16[:], col16[:], GATE_EPS, None, ALU.add))
                then(dve.reciprocal(col16b[:], col16[:]))
                then(dve.tensor_tensor(gate[:], gate[:], wide(col16b[:]), ALU.mult))

            def running(a, b, size):
                d = 1
                while d < size:
                    dve.tensor_tensor(b[:, d:size], a[:, d:size], a[:, 0:size - d], ALU.add)
                    then(dve.tensor_copy(b[:, 0:d], a[:, 0:d]))
                    a, b = b, a
                    d *= 2
                return a, b

            counts = bank[5][:, TT * E:2 * TT * E].rearrange("p (t e) -> p t e", e=E)
            sums = {}

            def place_experts():
                dve.wait_ge(ranks_ready, 1)
                dve.tensor_copy(rank[:], bank[5][:, 0:TT * E].rearrange("p (t e) -> p t e", e=E))
                then(dve.tensor_copy(sum_a[:], counts))
                total, spare = sums["total"], sums["spare"] = running(sum_a, sum_b, TT)
                tokens_of = total[:, TT - 1, :]
                then(dve.tensor_tensor(spare[:], across(tokens_of), tile_floor[:], ALU.is_gt))
                then(dve.tensor_reduce(tiles_of[:], spare[:].rearrange("p t e -> p e t"), AX.X, ALU.add))
                then(dve.tensor_scalar(ends_a[:], tiles_of[:], float(LEAST), None, ALU.max))
                then(dve.tensor_copy(tiles_of[:], ends_a[:]))
                ends, _ = running(ends_a, ends_b, E)
                dve.memset(first_f[:, 0:1], 0.0)
                then(dve.tensor_copy(first_f[:, 1:E + 1], ends[:]))
                then(dve.tensor_copy(first_i[:], first_f[:]))
                then(dve.tensor_tensor(base[:], ends[:], tiles_of[:], ALU.subtract))
                then(dve.tensor_scalar(base[:], base[:], float(P), None, ALU.mult))

            def place_tokens():
                total, spare = sums["total"], sums["spare"]
                then(dve.tensor_tensor(rank[:], rank[:], total[:], ALU.add))
                then(dve.tensor_tensor(rank[:], rank[:], counts, ALU.subtract))
                then(dve.tensor_tensor(rank[:], rank[:], across(base[:]), ALU.add))
                for c, chosen in enumerate((pick0, pick1)):
                    then(dve.tensor_tensor(spare[:], chosen[:], gate[:], ALU.mult))
                    then(dve.tensor_reduce(choice_gate[:, c, :], spare[:], AX.X, ALU.add))
                    then(dve.tensor_tensor(spare[:], chosen[:], rank[:], ALU.mult))
                    then(dve.tensor_reduce(choice_slot[:, c, :], spare[:], AX.X, ALU.add))
                dve.tensor_copy(choice_row[:], choice_slot[:]).then_inc(slots_ready, 1)

            def x_low(n):
                dve.wait_ge(x_high, n + 1)
                low(xT[:, 1], bank[4][:].rearrange("p (k c) -> p k c", k=KD), xT[:, 0]).then_inc(x_split, 1)

            def hidden(n):
                dve.wait_ge(silu_done, n + 1)
                dve.tensor_tensor(hid[:], silu_g[:], bank[1][:, 0:EH], ALU.mult).then_inc(hid_ready, 1)

            def hid_low(n):
                dve.wait_ge(hidT_high, 2 * n + 2)
                for k, rws in ((slice(0, 2), P), (slice(2, 3), HW[2])):
                    low(hidT[0:rws, 1, k, :], bank[2][0:rws, k.start * P:k.stop * P].rearrange("p (k c) -> p k c", c=P),
                        hidT[0:rws, 0, k, :]).then_inc(hidT_split, 1)

            def take(n, tile, stage):
                row = resid[:, bass.ds(tile, 1), :].rearrange("p o d -> p (o d)")
                dve.wait_ge(y_ready, n + 1)
                dve.tensor_tensor(row, row, bank[3][:], ALU.add).then_inc(y_taken, 1)
                if stage == "combined":
                    dve.wait_ge(gathered, 32 * (tile + 1))
                    dve.wait_ge(y_taken, n + 1)
                    for c in range(2):
                        if c:
                            dve.wait_ge(combining, tile + 1)
                        dve.scalar_tensor_tensor(row, picked[:, bass.ds(tile % 2, 1), c, :].rearrange("p o d -> p (o d)"),
                                                 choice_gate[:, c, bass.ds(tile, 1)], row,
                                                 ALU.mult, ALU.add).then_inc(combined if c else combining, 1)

            def begin():
                x_low(0)
                gates()
                hidden(0)
                x_low(1)

            def unit(n, slot, last_slot, stage, tile, last_stage, last_tile, opens=None, split=None, more=True):
                hid_low(n - 1)
                hidden(n)
                if more:
                    x_low(n + 1)
                if last_stage != "routed":
                    take(n - 1, last_tile, last_stage)
                if split is not None:
                    expert_low(split)

            def end(n):
                hid_low(n - 1)
                take(n - 1, TT - 1, "combined")

            units(dve, begin, unit, end, {1: pick_experts, 2: normalize_gates, 3: place_experts, 4: place_tokens})

        @block.tensor
        def _(pe):
            def fold(kind, h, acc):
                if kind == "M":
                    for r in range(KQ):
                        pe.matmul(acc[:, r * P:(r + 1) * P], pack[:, O_UQ + r * P:O_UQ + (r + 1) * P],
                                  pack[:, O_UK:O_UK + KVC], start=True, stop=True)
                    pe.matmul(acc[:, QC:QC + 1], pack[:, O_UK:O_UK + KVC], uqb[:, bass.ds(h, 1)], start=True, stop=True)
                    for k in range(KD):
                        op = pe.matmul(acc[:, QC + 1 + k:QC + 2 + k], pack[:, O_WO + k * P:O_WO + (k + 1) * P],
                                       uvb[:, bass.ds(h, 1)], start=True, stop=True)
                    return op
                return pe.matmul(acc[:], pack[:, O_UV:O_UV + KVC], pack[:, O_WO:O_WO + D], start=True, stop=True)

            def rows_turn(b, t):
                pe.wait_ge(norm1_ready, QT * b + t + 1)
                if (b, t) > (0, 1):
                    pe.wait_ge(proj_split, proj_no["rows", b - (t < 2), (t - 2) % QT])
                for k in range(KD):
                    op = pe.transpose(bank[t % 2][:, k * P:(k + 1) * P], xn1[:, t, k * P:(k + 1) * P], ident[:])
                op.then_inc(proj_product, 1)

            def latent(b, m):
                if m == 0:
                    pe.wait_ge(proj_split, proj_no["rows", b, QT - 1])
                    if b == 0:
                        pe.wait_ge(projw_split, 1)
                if b:
                    pe.wait_ge(proj_split, proj_no["latent", b - 1, m])
                for k in range(KD):
                    op = mm3(pe, bank[2 + m][:], both(projw, k, slice(m * P, (m + 1) * P)), both(xnT1[:, b % 2], k, ALL),
                             k == 0, k == KD - 1)
                op.then_inc(proj_product, 1)

            def turn(b):
                pe.wait_ge(proj_split, proj_no["latent", b, 0])
                if b < 2:
                    pe.wait_ge(fold_split, 2 * b + 2)
                if b:
                    pe.wait_ge(turned_high, b)
                    pe.wait_ge(turned_low, b)
                for part in range(2):
                    for t in range(QT):
                        c = b * S + t * P
                        op = pe.transpose(bank[6 + part][:, t * P:(t + 1) * P], f32(ckvT[:, part, c:c + P]), ident[:])
                    op.then_inc(turned, 1)

            def fold_first(j):
                pe.wait_ge(pack_loaded, 16 * j + 16)
                if j:
                    pe.wait_ge(turned_high, 1)
                    pe.wait_ge(turned_low, 1)
                for i, kind in enumerate("MN"):
                    op = fold(kind, j, bank[6 + i])
                    op.then_inc(fold_product, 1)

            pe.wait_ge(ident_ready, 1)
            pe.wait_ge(bias_loaded, 16 * 4)
            projections(rows_turn, latent, turn, fold_first)

            pe.wait_ge(turned_high, B)
            pe.wait_ge(turned_low, B)
            pe.wait_ge(fold_split, 4)

            def iteration(u, lap):
                tiles = lap * (QT * LAP)
                q, v = u + 2, u - 1
                b_s, b_v, b_q = (u + 1) // 2 % B, v // 2 % B, q // 2 % B
                if has(u + 1):
                    pe.wait_ge(att_split, split_no("Q", u + 1, 0, lap))
                for s in range(QT):
                    if has(u + 1):
                        n = QT * (u + 1) + s
                        hold(pe, exp_done, n - 1 + tiles)
                        mm3(pe, bank[s % 2][:], both(qT[:, (u + 1) % 2], slice(s * P, (s + 1) * P)),
                            both(ckvT, slice(b_s * S, (b_s + 1) * S)), True, True).then_inc(scores_ready, 1)
                    if has(u):
                        n = QT * u + s
                        pe.wait_ge(probs_ready, n + 1 + tiles)
                        if n >= 2:
                            pe.wait_ge(att_split, split_no("T", (n - 2) // QT, (n - 2) % QT, lap))
                        for k in range(QT):
                            op = pe.transpose(bank[2 + s % 2][:, k * P:(k + 1) * P], probs[:, s, k * P:(k + 1) * P], ident[:])
                        op.then_inc(att_product, 1)
                    if has(q) and s in (0, 2):
                        if s == 0:
                            if fold_of(u - 1):
                                pe.wait_ge(att_split, split_no("F", u - 1, 0, lap))
                            elif u == UNITS - LAP + 1:
                                pe.wait_ge(ob_ready, 1)
                            elif q:
                                pe.wait_ge(att_split, split_no("Q", q - 1, 0, lap))
                        for k in ((0, 1) if s == 0 else (2,)):
                            op = mm3(pe, bank[4][:], both(m_sb, q % 2, slice(k * P, (k + 1) * P)),
                                     both(cqT, k, slice(b_q * S, (b_q + 1) * S)), k == 0, k == KQ - 1)
                        if s == 2:
                            op.then_inc(att_product, 1)
                    if s == 3 and fold_of(u):
                        kind, j = fold_of(u)
                        h = 2 * (u // LAP + lap + 1) + j
                        pe.wait_ge(att_split, split_no("Q", q, 0, lap))
                        pe.wait_ge(pack_loaded, 16 * h + 16)
                        fold(kind, h, bank[4]).then_inc(att_product, 1)
                    if s == 3 and u == UNITS - LAP:
                        pe.wait_ge(att_split, split_no("Q", q, 0, lap))
                        pe.wait_ge(ob_spread, 1)
                        for k in range(KD):
                            op = pe.matmul(bank[4][:, k * P:(k + 1) * P], ob_wide[:, k * P:(k + 1) * P], ident[:],
                                           start=True, stop=True)
                        op.then_inc(ob_product, 1)
                    if has(v):
                        if s == 0:
                            pe.wait_ge(att_split, split_no("T", v, QT - 1, lap))
                            if v:
                                pe.wait_ge(att_split, split_no("V", v - 1, 0, lap))
                        op = mm3(pe, bank[5][:], both(ckv[:, b_v], s, ALL), both(pT[:, v % 2], s, ALL), s == 0, s == QT - 1)
                        if s == QT - 1:
                            op.then_inc(att_product, 1)
                    if outs_of(u, s):
                        bb, i = outs_of(u, s)
                        m = QT * bb + i
                        pe.wait_ge(att_split, split_no("V", 2 * bb + 1, 0, lap))
                        hold(pe, out_added, m - 1 + lap * (QT * LAP // 2))
                        slot = (bb // B + lap) % 2
                        for j in range(2):
                            op = mm3(pe, bank[6 + m % 2][:], both(mixT[:, bb % 2, j], slice(i * P, (i + 1) * P)),
                                     (n_sb[:, slot, 0, j, :], n_sb[:, slot, 1, j, :]), j == 0, j == 1)
                        op.then_inc(out_ready, 1)
            def begin_split(n):
                hold(pe, mix_split, n - 2)
                return split_bank(n)

            def project3(b):
                pe.wait_ge(ctx_split, b + 1)
                if b == 0:
                    pe.wait_ge(mixw_high, 2)
                for i in range(2):
                    acc = begin_split(mix_no["project", b, i])
                    for k in range(KC):
                        op = mm3(pe, acc[:], both(qkw, k, slice(i * P, (i + 1) * P)), both(ctxT, k, ALL),
                                 k == 0, k == KC - 1)
                    op.then_inc(mix_product, 1)

            def scores3(b, s):
                n = QT * b + s
                if s == 0:
                    pe.wait_ge(mix_split, mix_no["project", b, 1])
                hold(pe, exp3_done, n - 1)
                mm3(pe, bank[s % 2][:], both(qk3[:, 0], slice(s * P, (s + 1) * P)), both(qk3[:, 1], ALL), True, True).then_inc(scores3_ready, 1)

            def rows3(b, s):
                pe.wait_ge(norm3_ready, QT * b + s + 1)
                acc = begin_split(mix_no["rows3", b, s])
                for k in range(KD):
                    op = pe.transpose(acc[:, k * P:(k + 1) * P], xn3[:, s, k * P:(k + 1) * P], ident[:])
                op.then_inc(mix_product, 1)

            def turn3(b, s):
                pe.wait_ge(probs3_ready, QT * b + s + 1)
                acc = begin_split(mix_no["turn", b, s])
                for k in range(QT):
                    op = pe.transpose(acc[:, k * P:(k + 1) * P], probs3[:, s, k * P:(k + 1) * P], ident[:])
                op.then_inc(mix_product, 1)

            def mix3(b, s, half):
                t = QT * b + s
                if s == 0 and half == 0:
                    pe.wait_ge(mix_split, max(mix_no["turn", b, QT - 1], mix_no["rows3", b, QT - 1]))
                if half == 0:
                    hold(pe, mixed_added, t - 1)
                for k in (2 * half, 2 * half + 1):
                    op = mm3(pe, bank[6 + t % 2][:], both(xnT3[:, b % 2], k, slice(s * P, (s + 1) * P)),
                             both(pT3[:, b % 2], k, ALL), k == 0, k == QT - 1)
                if half:
                    op.then_inc(mixed_ready, 1)

            def logits(b, s):
                t = QT * b + s
                pe.wait_ge(rows4_taken, t + 1)
                for k in range(KD):
                    op = pe.matmul(bank[5][:, t * E:(t + 1) * E], xT4[:, s, k], routw[:, k],
                                   start=k == 0, stop=k == KD - 1)
                op.then_inc(logits_ready, 1)

            def rows4(b, s):
                t = QT * b + s
                pe.wait_ge(norm4_ready, t + 1)
                if b < B - 1 or s == 0:
                    hold(pe, rows4_taken, t)
                else:
                    pe.wait_ge(exp3_done, TT)
                    pe.wait_ge(mix_split, len(mix_no))
                acc = rows4_bank(b, s)
                for k in range(KD):
                    op = pe.transpose(acc[:, k * P:(k + 1) * P], xn4[:, t, k * P:(k + 1) * P], ident[:])
                op.then_inc(rows4_turned, 1)
                if t and (b < B - 1 or s == 0):
                    logits((t - 1) // QT, (t - 1) % QT)

            def first_scores():
                scores3(0, 0)
                scores3(0, 1)

            laps(pe, iteration, {UNITS + 1: lambda: project3(0), UNITS + 2: first_scores})
            pe.wait_ge(rout_loaded, 16)

            mixing(none, project3, scores3, none, turn3, none, none, none, rows3, mix3, none, none, none, rows4)
            for s in range(QT):
                logits(B - 1, s)
            def turn_rows(n):
                pe.wait_ge(rows_loaded, 16 * n + 16)
                hold(pe, x_split, n)
                for k in range(KD):
                    op = pe.transpose(bank[4][:, k * P:(k + 1) * P], rows[:, k * P:(k + 1) * P], ident[:])
                op.then_inc(x_product, 1)

            def gate_up(n, slot):
                pe.wait_ge(x_split, n + 1)
                for half in range(2):
                    for k in range(KD):
                        o = k * 2 * EH + half * EH
                        op = mm3(pe, bank[half][:, 0:EH], both(xT, k, ALL), (ew[:, slot, 0, o:o + EH], ew[:, slot, 1, o:o + EH]),
                                 k == 0, k == KD - 1)
                op.then_inc(gu_ready, 1)

            def turn_hid(n):
                pe.wait_ge(hid_ready, n + 1)
                hold(pe, hidT_split, 2 * n)
                for k in range(KH):
                    op = pe.transpose(bank[2][0:HW[k], k * P:(k + 1) * P], hid[:, k * P:k * P + HW[k]], ident[:])
                op.then_inc(hidT_product, 1)

            def down(n, slot):
                pe.wait_ge(hidT_split, 2 * n + 2)
                hold(pe, y_taken, n)
                for k in range(KH):
                    o = KD * 2 * EH + k * D
                    rws = HW[k]
                    op = mm3(pe, bank[3][:], (hidT[0:rws, 0, k, :], hidT[0:rws, 1, k, :]),
                             (ew[0:rws, slot, 0, o:o + D], ew[0:rws, slot, 1, o:o + D]), k == 0, k == KH - 1)
                op.then_inc(y_ready, 1)

            def begin():
                turn_rows(0)
                pe.wait_ge(ew_split, 2)
                gate_up(0, 0)
                turn_rows(1)

            def unit(n, slot, last_slot, stage, tile, last_stage, last_tile, opens=None, split=None, more=True):
                turn_hid(n - 1)
                if opens is not None:
                    pe.wait_ge(ew_split, 2 * opens + 2)
                gate_up(n, slot)
                if more:
                    turn_rows(n + 1)
                down(n - 1, last_slot)

            def end(n):
                turn_hid(n - 1)
                down(n - 1, (NE - 1) % 2)

            def ranks():
                pe.wait_ge(gate_shift, 1)
                pe.wait_ge(picks_ready, 1)
                pe.wait_ge(grids_ready, 2)
                pe.matmul(bank[5][:, 0:TT * E], tri[:], pick[:].rearrange("p t e -> p (t e)"), start=True, stop=True)
                pe.matmul(bank[5][:, TT * E:2 * TT * E], ones[:], pick[:].rearrange("p t e -> p (t e)"), start=True,
                          stop=True).then_inc(ranks_ready, 1)

            units(pe, begin, unit, end, {2: ranks})


def kernel(**inputs):
    import numpy as np
    import concourse.bacc as bacc
    from concourse.bass_utils import run_bass_kernel_spmd

    a = {k: np.asarray(v) for k, v in inputs.items()}
    g = {k[8:]: v for k, v in a.items() if k.startswith("L0_attn_")}
    f = {k[7:]: v for k, v in a.items() if k.startswith("L0_ffn_")}

    def tiles(w):
        return w.reshape(-1, P, w.shape[1]).transpose(1, 0, 2)

    def columns(v):
        return v.reshape(-1, P).T

    uq, uk, uv = (g[k].reshape(H, DH, -1) for k in ("W_UQ_w", "W_UK_w", "W_UV_w"))
    wo = g["W_O_w"].T.reshape(H, DH, D)
    shared = [np.concatenate([f["sg"][:, i * EH:(i + 1) * EH], f["su"][:, i * EH:(i + 1) * EH]], 1)[None] for i in range(NSH)]
    gu = np.concatenate([shared[0], np.concatenate([f["wg"], f["wu"]], 2), shared[1]], 0)
    data = {
        "x": a["x"].reshape(B * S, D),
        "proj_w": tiles(np.concatenate([g["W_DKV_w"], g["W_DQ_w"]], 0).T),
        "proj_b": columns(np.concatenate([g["W_DKV_b"], g["W_DQ_b"]])),
        "heads_w": np.concatenate([uq, uk, uv, wo], 2),
        "uq_b": columns(g["W_UQ_b"]),
        "uv_b": columns(g["W_UV_b"]),
        "o_b": columns(g["W_O_b"]),
        "ctx_t": tiles(a["ctx_1024"].reshape(B * S, C).T),
        "qk_w": tiles(np.concatenate([a["L0_xattn_Wq"], a["L0_xattn_Wk"]], 0).T),
        "qk_b": np.stack([a["L0_xattn_bq"], a["L0_xattn_bk"]], 1),
        "router_w": tiles(f["router_w"].T),
        "gate_up_w": gu.reshape(NE, KD, P, 2 * EH).transpose(0, 2, 1, 3).reshape(NE, P, KD * 2 * EH),
        "down_w": np.concatenate([f["sd"][None, :EH], f["wd"], f["sd"][None, EH:]], 0),
    }
    data = {k: np.ascontiguousarray(v) for k, v in data.items()}
    nc = bacc.Bacc("TRN2", target_bir_lowering=False, num_devices=1)
    args = [nc.dram_tensor(k, v.shape, mybir.dt.from_np(v.dtype), kind="ExternalInput").ap() for k, v in data.items()]
    out = nc.dram_tensor("out", [B * S, D], F32, kind="ExternalOutput").ap()
    decoder_kernel(nc, *args, out)
    r = run_bass_kernel_spmd(nc, [data], core_ids=[0])
    return r.results[0]["out"].reshape(B, S, D)
```
